# Optimizing a Trainium2 kernel written in Bass

```python
import numpy as np
import jax
import jax.numpy as jnp

def _softmax(x, axis=-1):
    return jax.nn.softmax(x, axis=axis)

def _gelu(x):
    return jax.nn.gelu(x, approximate=True)

def _silu(x):
    return jax.nn.silu(x)

def _sigmoid(x):
    return jax.nn.sigmoid(x)

def _layernorm(x, axis=-1, eps=1e-05):
    m = jnp.mean(x, axis=axis, keepdims=True)
    v = jnp.var(x, axis=axis, keepdims=True)
    return (x - m) / jnp.sqrt(v + eps)

def _scatter_add(tgt, idx, src, axis=0):
    return tgt.at[idx].add(src)

def _segment_sum(src, seg, n):
    return jax.ops.segment_sum(src, seg, n)
kernel_name = 'mk_adaln_d1_jaxref_r8_953152'

def setup_inputs(seed: int=0):
    np.random.seed(seed)
    _w = jnp.asarray

    def _L0_attn_setup():
        import jax, jax.numpy as jnp
        import numpy as np
        B, T, HID = (2, 256, 256)
        NKH, NVH = (16, 32)
        DK, DV = (128, 128)
        R = NVH // NKH
        KDIM, VDIM = (NKH * DK, NVH * DV)
        CONV_K = 4
        EPS = 1e-06

        def _silu(x):
            return x * jax.nn.sigmoid(x)

        def _l2norm(x, eps=1e-06):
            return x * jax.lax.rsqrt(jnp.sum(x * x, axis=-1, keepdims=True) + eps)
        key = jax.random.key(seed)
        ks = jax.random.split(key, 8)
        w = lambda k, shape, sc=0.02: jax.random.normal(k, shape, jnp.float32) * sc
        return {'hidden_states': jax.random.normal(ks[0], (B, T, HID), jnp.float32), 'W_qkvz': w(ks[1], (HID, 2 * KDIM + 2 * VDIM)), 'W_ba': w(ks[2], (HID, 2 * NVH)), 'conv_w': w(ks[3], (2 * KDIM + VDIM, CONV_K), 0.1), 'dt_bias': jnp.ones((NVH,), jnp.float32), 'A_log': jax.random.normal(ks[4], (NVH,), jnp.float32), 'norm_weight': jnp.ones((DV,), jnp.float32), 'W_out': w(ks[5], (VDIM, HID))}
    _L0_attn_in = _L0_attn_setup()

    def _L0_ffn_setup():
        import jax, jax.numpy as jnp
        import numpy as np
        TOP_K = 4
        key = jax.random.key(seed)
        ks = jax.random.split(key, 8)
        B, S, D, E, H, HS = (2, 256, 256, 16, 128, 512)
        scaled = lambda k, shape, fan: jax.random.normal(k, shape, jnp.float32) * fan ** (-0.5)
        return {'x': jax.random.normal(ks[0], (B, S, D), jnp.float32), 'w_router': scaled(ks[1], (D, E), D), 'we1': scaled(ks[2], (E, D, H), D), 'we3': scaled(ks[3], (E, D, H), D), 'we2': scaled(ks[4], (E, H, D), H), 'ws1': scaled(ks[5], (D, HS), D), 'ws3': scaled(ks[6], (D, HS), D), 'ws2': scaled(ks[7], (HS, D), HS)}
    _L0_ffn_in = _L0_ffn_setup()
    _L0_c = _w((lambda *s: np.random.randn(*s).astype(np.float32) * 0.05)(1, 256))
    _L0_wmod = _w((lambda *s: np.random.randn(*s).astype(np.float32) * 0.05)(256, 6 * 256) * 256 ** (-0.5))
    _d = {'L0_attn_hidden_states': _L0_attn_in['hidden_states'], 'L0_attn_W_qkvz': _L0_attn_in['W_qkvz'], 'L0_attn_W_ba': _L0_attn_in['W_ba'], 'L0_attn_conv_w': _L0_attn_in['conv_w'], 'L0_attn_dt_bias': _L0_attn_in['dt_bias'], 'L0_attn_A_log': _L0_attn_in['A_log'], 'L0_attn_norm_weight': _L0_attn_in['norm_weight'], 'L0_attn_W_out': _L0_attn_in['W_out'], 'L0_ffn_w_router': _L0_ffn_in['w_router'], 'L0_ffn_we1': _L0_ffn_in['we1'], 'L0_ffn_we3': _L0_ffn_in['we3'], 'L0_ffn_we2': _L0_ffn_in['we2'], 'L0_ffn_ws1': _L0_ffn_in['ws1'], 'L0_ffn_ws3': _L0_ffn_in['ws3'], 'L0_ffn_ws2': _L0_ffn_in['ws2'], 'L0_c': _L0_c, 'L0_wmod': _L0_wmod}
    _x0 = _d['L0_attn_hidden_states']
    _d['L0_attn_hidden_states'] = jax.random.normal(jax.random.fold_in(jax.random.key(seed), 1), (1, 1024, 256), dtype=_x0.dtype)
    del _x0
    return _d

def reference(L0_attn_hidden_states, L0_attn_W_qkvz, L0_attn_W_ba, L0_attn_conv_w, L0_attn_dt_bias, L0_attn_A_log, L0_attn_norm_weight, L0_attn_W_out, L0_ffn_w_router, L0_ffn_we1, L0_ffn_we3, L0_ffn_we2, L0_ffn_ws1, L0_ffn_ws3, L0_ffn_ws2, L0_c, L0_wmod):

    def _L0_attn_ref(hidden_states, W_qkvz, W_ba, conv_w, dt_bias, A_log, norm_weight, W_out):
        import jax, jax.numpy as jnp
        import numpy as np
        B, T, HID = (2, 256, 256)
        NKH, NVH = (16, 32)
        DK, DV = (128, 128)
        R = NVH // NKH
        KDIM, VDIM = (NKH * DK, NVH * DV)
        CONV_K = 4
        EPS = 1e-06

        def _silu(x):
            return x * jax.nn.sigmoid(x)

        def _l2norm(x, eps=1e-06):
            return x * jax.lax.rsqrt(jnp.sum(x * x, axis=-1, keepdims=True) + eps)
        Bv, Tv = hidden_states.shape[:2]
        qkvz = hidden_states @ W_qkvz
        ba = hidden_states @ W_ba
        qkvz = qkvz.reshape(Bv, Tv, NKH, 2 * DK + 2 * R * DV)
        q, k, v, z = jnp.split(qkvz, [DK, 2 * DK, 2 * DK + R * DV], axis=3)
        v = v.reshape(Bv, Tv, NVH, DV)
        z = z.reshape(Bv, Tv, NVH, DV)
        ba = ba.reshape(Bv, Tv, NKH, 2 * R)
        b, a = jnp.split(ba, 2, axis=3)
        b = b.reshape(Bv, Tv, NVH)
        a = a.reshape(Bv, Tv, NVH)
        mixed = jnp.concatenate([q.reshape(Bv, Tv, KDIM), k.reshape(Bv, Tv, KDIM), v.reshape(Bv, Tv, VDIM)], axis=-1)
        xp = jnp.pad(mixed, ((0, 0), (CONV_K - 1, 0), (0, 0)))
        conv = sum((xp[:, j:j + Tv, :] * conv_w[:, j] for j in range(CONV_K)))
        conv = _silu(conv)
        q, k, v = jnp.split(conv, [KDIM, 2 * KDIM], axis=-1)
        q = q.reshape(Bv, Tv, NKH, DK)
        k = k.reshape(Bv, Tv, NKH, DK)
        v = v.reshape(Bv, Tv, NVH, DV)
        beta = jax.nn.sigmoid(b)
        g = -jnp.exp(A_log) * jax.nn.softplus(a + dt_bias)
        alpha = jnp.exp(g)
        q = jnp.repeat(q, R, axis=2)
        k = jnp.repeat(k, R, axis=2)
        q = _l2norm(q) * DK ** (-0.5)
        k = _l2norm(k)

        def step(S, inp):
            q_t, k_t, v_t, a_t, b_t = inp
            S = S * a_t[..., None, None]
            err = jnp.einsum('bhkv,bhk->bhv', S, k_t)
            v_new = (v_t - err) * b_t[..., None]
            S = S + k_t[..., None] * v_new[..., None, :]
            o = jnp.einsum('bhkv,bhk->bhv', S, q_t)
            return (S, o)
        tm = lambda x: jnp.swapaxes(x, 0, 1)
        S0 = jnp.zeros((Bv, NVH, DK, DV), hidden_states.dtype)
        _, o = jax.lax.scan(step, S0, (tm(q), tm(k), tm(v), tm(alpha), tm(beta)))
        o = jnp.swapaxes(o, 0, 1)
        og = o * _silu(z)
        og = og * jax.lax.rsqrt(jnp.mean(og * og, axis=-1, keepdims=True) + EPS) * norm_weight
        return og.reshape(Bv, Tv, VDIM) @ W_out

    def _L0_ffn_ref(x, w_router, we1, we3, we2, ws1, ws3, ws2):
        import jax, jax.numpy as jnp
        import numpy as np
        TOP_K = 4
        B, S, D = x.shape
        T = B * S
        E = w_router.shape[1]
        xt = x.reshape(T, D)
        probs = jax.nn.softmax(xt @ w_router, axis=-1)
        top_w, top_i = jax.lax.top_k(probs, TOP_K)
        top_w = top_w / jnp.sum(top_w, axis=-1, keepdims=True)
        cw = jnp.zeros((T, E), xt.dtype).at[jnp.arange(T)[:, None], top_i].add(top_w)
        g = jax.nn.silu(jnp.einsum('td,edh->teh', xt, we1)) * jnp.einsum('td,edh->teh', xt, we3)
        g = g * cw[:, :, None]
        moe_out = jnp.einsum('teh,ehd->td', g, we2)
        shared = jax.nn.silu(xt @ ws1) * (xt @ ws3) @ ws2
        k = TOP_K
        out = shared / (k + 1) + moe_out * (k / (k + 1))
        return out.reshape(B, S, D)
    x = L0_attn_hidden_states
    mod = (_silu(L0_c) @ L0_wmod).reshape(L0_c.shape[0], 6, 1, -1)
    sa, ca, ga, sb, cb, gb = (mod[:, 0], mod[:, 1], mod[:, 2], mod[:, 3], mod[:, 4], mod[:, 5])
    ga = (2 * (ga >= 0) - 1) * jnp.maximum(jnp.abs(ga), 0.25)
    gb = (2 * (gb >= 0) - 1) * jnp.maximum(jnp.abs(gb), 0.25)
    h = _layernorm(x, axis=-1) * (1 + ca) + sa
    x = x + ga * _L0_attn_ref(h, L0_attn_W_qkvz, L0_attn_W_ba, L0_attn_conv_w, L0_attn_dt_bias, L0_attn_A_log, L0_attn_norm_weight, L0_attn_W_out)
    h = _layernorm(x, axis=-1) * (1 + cb) + sb
    x = x + gb * _L0_ffn_ref(h, L0_ffn_w_router, L0_ffn_we1, L0_ffn_we3, L0_ffn_we2, L0_ffn_ws1, L0_ffn_ws3, L0_ffn_ws2)
    return x

_drawn_inputs = setup_inputs


def setup_inputs(seed=0):
    import zlib

    import numpy as np

    out = dict(_drawn_inputs(seed))
    spreads = {'L0_attn_dt_bias': (1.0, 0.6), 'L0_attn_norm_weight': (1.0, 0.6)}
    factors = {'L0_attn_W_qkvz': 6.731,
     'L0_attn_W_ba': 8.0,
     'L0_attn_conv_w': 6.639,
     'L0_attn_A_log': 8.0,
     'L0_attn_W_out': 6.786,
     'L0_ffn_w_router': 13.09,
     'L0_ffn_ws1': 5.772,
     'L0_ffn_ws3': 5.485,
     'L0_ffn_ws2': 5.493,
     'L0_ffn_we1': 4.691,
     'L0_ffn_we3': 4.378,
     'L0_ffn_we2': 4.399}
    for name, (base, spread) in spreads.items():
        noise = np.random.default_rng([zlib.crc32(name.encode()), seed]).standard_normal(out[name].shape)
        drawn = base * np.exp(spread * noise) if base else spread * noise
        out[name] = jnp.asarray(drawn.astype(out[name].dtype))
    for name, factor in factors.items():
        out[name] = (out[name] * factor).astype(out[name].dtype)
    return out
```

```python
import numpy as np
import concourse.bass as bass
from concourse import mybir
from contextlib import ExitStack

F32 = mybir.dt.float32
ALU = mybir.AluOpType
ACT = mybir.ActivationFunctionType
AX = mybir.AxisListType

T, D = 1024, 256
C = 128
NC = T // C
KT = D // 128
NP = 16
NH = 2 * NP
PW = 768
QCOL, KCOL, VCOL, ZCOL = 0, 128, 256, 512
NE, NS, TOPK = 16, 4, 4
HB = 64
LEVELS = 5
UG = 8
NU = 2 * NC
FILLS = 60
RING = 4
NT = NE + NS
MFILLS = 8
F_PROJ, F_Z, F_NORM, F_KK, F_KT, F_VT, F_X1, F_LEVEL, F_LAST = 0, 8, 12, 14, 18, 20, 24, 26, 56
C_ID, C_ID64, C_MASK = 0, 128, 192
C_ONE = C_MASK + HB * (LEVELS + 1)
C_N = C_ONE + 1



class Count:

    def __init__(self, sem, per):
        self.sem, self.per = sem, per

    def at(self, n, k):
        return n * self.per + (k + 1)


def adaln_block(nc, x, w_qkvz, w_ba, conv_w, dt_bias, a_log, norm_w, w_out, w_router, we1, we3, we2,
                ws1, ws3, ws2, c_in, wmod, consts, d_alpha, d_last, out):
    ctx = ExitStack()
    with ctx:
        def sb(name, shape):
            return ctx.enter_context(nc.sbuf_tensor(name, shape, F32))

        def sem(name):
            return ctx.enter_context(nc.semaphore(name))

        rounds = []

        def counted(name, per):
            rounds.append(Count(sem(name), per))
            return rounds[-1]

        cst = sb("cst", [128, C_N])
        hT = sb("hT", [128, KT, T])
        wq = [sb(f"wq{i}", [128, KT, PW]) for i in range(2)]
        cw = [sb(f"cw{i}", [128, 4, 4]) for i in range(2)]
        wo = [sb(f"wo{i}", [128, 2, D]) for i in range(2)]
        xpad = [sb(f"xpad{i}", [128, T + 3]) for i in range(2)]
        cacc = [sb(f"cacc{i}", [128, T]) for i in range(2)]
        kq = [sb(f"kq{i}", [128, NC, 2, C]) for i in range(2)]
        vT = sb("vT", [128, 2, T])
        sz = [sb(f"sz{i}", [128, NC, 2 * C]) for i in range(2)]
        lt = sb("lt", [128, NU, C])
        am = [sb(f"am{i}", [128, NU, 2, C]) for i in range(2)]
        km = [sb(f"km{i}", [128, NU, C]) for i in range(2)]
        vp = [sb(f"vp{i}", [128, NC, 2, C]) for i in range(2)]
        xf = [sb(f"xf{i}", [128, NU, C]) for i in range(2)]
        xt = sb("xt", [128, NU, HB])
        xc = sb("xc", [128, NU, HB])
        yc = sb("yc", [128, NU, HB])
        acc = sb("acc", [128, NC, D])
        st = sb("st", [128, 2, C])
        rr = sb("rr", [128, 2, C])
        uu = sb("uu", [128, 2, C])
        qse = sb("qse", [128, 2, C])
        o1 = [sb(f"o1{i}", [128, 2, C]) for i in range(2)]
        o2 = [sb(f"o2{i}", [128, 2, C]) for i in range(2)]
        ogt = sb("ogt", [128, 2, C])
        junk = sb("junk", [128, 2, C])
        tab = sb("tab", [128, NP, 3, 2, NC])
        sc = [sb(f"sc{i}", [128, 3, 2, NC]) for i in range(2)]
        nk = [sb(f"nk{i}", [128, 5, NC]) for i in range(2)]
        sj = sb("sj", [128, 2, NC])
        wl = sb("wl", [128, 2, NC])
        half = sb("half", [128, 2, NC])
        ss = sb("ss", [128, 2, 4, 2])
        nw = sb("nw", [128, 1])
        sm = sb("sm", [128, 128])
        modc = sb("modc", [128, 8])
        gate = sb("gate", [128, 2, D])
        bank = [ctx.enter_context(nc.psum_tensor(f"bank{i}", [128, 512], F32)) for i in range(8)]
        KSB, XRB, QSB, OGB = bank[4], bank[5], bank[6], bank[7]

        ident = cst[:, C_ID:C_ID + 128]
        ones = cst[:, C_ONE:C_ONE + 1]

        def bc(ap, shape):
            return ap.broadcast_to(shape)

        def mask(lo, hi, lvl, units):
            m = cst[lo:hi, C_MASK + HB * lvl:C_MASK + HB * (lvl + 1)]
            return bc(m.unsqueeze(1), [hi - lo, units, HB])

        flags = {}

        def flag(name):
            if name not in flags:
                flags[name] = sem(name)
            return flags[name]

        steps = {}

        def link(eng, name, ins):
            steps[name] = steps.get(name, 0) + 1
            ins.then_inc(flag(name), 1)
            eng.wait_ge(flag(name), steps[name])

        def hold(eng, name):
            eng.sem_inc(flag(name), 1)

        w_in = [counted(f"w_loaded{i}", 16) for i in range(2)]
        cw_in = [counted(f"taps_loaded{i}", 48) for i in range(2)]
        wo_in = [counted(f"wout_loaded{i}", 16) for i in range(2)]
        al_in = counted("decays_loaded", 16)
        full = counted("bank_filled", FILLS)
        x_copied = counted("projection_copied", 8)
        z_ready = counted("z_ready", 4)
        conv_done = counted("conv_done", 4)
        tap = counted("tap_added", 12)
        silu_done = counted("silu_done", 4)
        sq_ready = counted("squares_ready", 2)
        sc_ready = counted("scalars_ready", 1)
        nk_ready = counted("norms_ready", 2)
        rs_ready = counted("roots_ready", 2)
        s_ready = counted("s_ready", 2)
        lt_ready = counted("decay_products_ready", 1)
        am_ready = counted("attention_matrices_ready", 4)
        wl_ready = counted("key_scales_ready", 1)
        km_done = counted("keys_scaled", 2)
        vp_done = counted("values_scaled", 4)
        inv = counted("inverse_parts", 3 + 6 * LEVELS)
        x1_copied = counted("x1_copied", 2)
        last_copied = counted("last_blocks_copied", 4)
        won_ready = counted("wout_scaled", 1)
        ks_full, qs_full, ku_full = (counted(f"{w}_full", NC - 1) for w in ("ks", "qs", "ku"))
        xr_full, pu_full, og_full, wo_full = (counted(f"{w}_full", NC) for w in ("xr", "pu", "og", "wo"))
        r_ready, st_ready, qse_ready = (counted(f"{w}_ready", NC - 1) for w in ("r", "state", "qse"))
        o1_ready, u_ready, ogt_ready, o2_ready, o3_ready, acc_done = (
            counted(w, NC) for w in ("o1_ready", "u_ready", "ogt_ready", "o2_ready", "o3_ready", "acc_done"))
        ss_ready = counted("ss_ready", 2 * NC)
        f_step = counted("scale_steps", 3 * NC)
        w13_in = [counted(f"w13_loaded{i}", 32) for i in range(2)]
        w2_in = [counted(f"w2_loaded{i}", 16) for i in range(2)]
        mfull = counted("moe_bank_filled", MFILLS)
        sg_ready = counted("silu_gate_ready", 2)
        g_ready = counted("hidden_ready", 2)
        cwe_ready = counted("weights_ready", 1)
        down_done = counted("down_added", NC)

        def drained(f):
            if f < F_Z:
                return x_copied, f - F_PROJ + 1
            if f < F_NORM:
                return z_ready, f - F_Z + 1
            if f < F_KK:
                return nk_ready, f - F_NORM + 1
            if f < F_KT:
                return am_ready, f - F_KK + 1
            if f < F_VT:
                return km_done, f - F_KT + 1
            if f < F_X1:
                return vp_done, f - F_VT + 1
            if f < F_LEVEL:
                return x1_copied, f - F_X1 + 1
            if f < F_LAST:
                return inv, 3 + f - F_LEVEL + 1
            return last_copied, f - F_LAST + 1

        w_v = w_qkvz.rearrange("(k p) m -> p k m", p=128)
        wo_v = w_out.rearrange("(h p) m -> p h m", p=128)
        cw_v = conv_w.rearrange("(t p) j -> p t j", p=128)
        x_v = x.rearrange("b (c p) d -> p (b c) d", p=128)
        out_v = out.rearrange("b (c p) d -> p (b c) d", p=128)
        al_v = d_alpha.rearrange("(g h) c t -> g (h c) t", h=2)

        xs = vT[:, :, :].rearrange("p a (b d) -> p (a b) d", d=D)
        wmod_sb = am[0][:, :, :, :].rearrange("p u a c -> p (u a c)")[:, 0:KT * 6 * D].rearrange(
            "p (k m) -> p k m", k=KT)
        wba_sb = km[0][:, 0, :].rearrange("p (k m) -> p k m", k=KT)
        dtb, alg = km[0][:, 1, 0:NH], km[0][:, 1, NH:2 * NH]
        scb = km[0][:, 2:4, :]
        zero32 = km[0][0:NH, 4, :]
        last32 = km[0][0:NH, 5, 0:NC]
        lastb = km[0][:, 6:8, :].rearrange("p a b -> p (a b)")
        cT, scT = sm[:, 0:2], sm[:, 2:4]
        stat = sm[:, 4:52].rearrange("p (c k) -> p c k", k=6)
        mv = sm[:, 52:68].rearrange("p (c k) -> p c k", k=2)
        rstd, nhalf = sm[:, 68:76], sm[:, 76:84]
        tmp = [vp[0][:, i, :, :].rearrange("p a b -> p (a b)") for i in range(NC)]
        alT = xf[1][0:NH, 0:NC, :]
        eT = xf[1][0:NH, NC:2 * NC, :]
        wr_sb = km[0][:, 0, 0:KT * NE].rearrange("p (k m) -> p k m", k=KT)
        WP = NE + TOPK
        lg = km[0][:, 1, :].rearrange("p (c e) -> p c e", c=NC)
        pv = km[0][:, 2:4, :].rearrange("p a b -> p (a b)")[:, 0:NC * WP].rearrange("p (c e) -> p c e", c=NC)
        rep = km[0][:, 4:6, :].rearrange("p a b -> p (a b)")[:, 0:NC * WP].rearrange("p (c e) -> p c e", c=NC)
        top = km[0][:, 6, 0:NC * 8].rearrange("p (c e) -> p c e", c=NC)
        cwt = km[0][:, 8:10, :].rearrange("p a b -> p (a b)")[:, 0:NT * NC].rearrange("p (e c) -> p e c", c=NC)
        row = km[0][:, 10, 0:NC]
        w13 = [km[1][:, 4 * i:4 * i + 4, :].rearrange("p (w k) h -> p w k h", w=2) for i in range(2)]
        w2 = [km[1][:, 8 + 2 * i:10 + 2 * i, :].rearrange("p a b -> p (a b)") for i in range(2)]
        cwe = [km[0][:, 11 + i, 0:NC] for i in range(2)]
        sg = [cacc[0][:, 512 * i:512 * i + 512] for i in range(2)]
        gT = cacc[1]
        acc2 = kq[0][:, :, :, :].rearrange("p c a b -> p c (a b)")
        fin = kq[1][:, :, :, :].rearrange("p c a b -> p c (a b)")
        BAB, MODB, GATEB = bank[4], bank[5], bank[6]

        block = ctx.enter_context(nc.Block())

        @block.sync
        def _(sp):
            sp.dma_start(xs, x_v).then_inc(flag("x_loaded"), 16)
            sp.dma_start(cst[:, :], consts).then_inc(flag("consts_loaded"), 16)
            sp.dma_start(cT, c_in.rearrange("a (k p) -> p (a k)", p=128), allow_slow_non_contiguous=True).then_inc(flag("c_loaded"), 16)
            sp.dma_start(wmod_sb, wmod.rearrange("(k p) m -> p k m", p=128)).then_inc(flag("wmod_loaded"), 16)
            sp.dma_start(wba_sb, w_ba.rearrange("(k p) m -> p k m", p=128)).then_inc(flag("wba_loaded"), 16)
            sp.dma_start(dtb, bc(dt_bias.unsqueeze(0), [128, NH])).then_inc(flag("gates_loaded"), 16)
            sp.dma_start(alg, bc(a_log.unsqueeze(0), [128, NH])).then_inc(flag("gates_loaded"), 16)
            sp.dma_start(nw[:, :], norm_w.unsqueeze(1)).then_inc(flag("nw_loaded"), 16)

            def weights(n, par):
                m = n if isinstance(n, int) else None
                if m is None:
                    sp.wait_ge(full.sem, full.at(n, F_NORM - 2 * FILLS))
                    hold(sp, "sp_held")
                sp.dma_start(wq[par][:, :, :], w_v[:, :, bass.ds(n * PW, PW)]).then_inc(w_in[par].sem, 16)
                if m is None:
                    sp.wait_ge(conv_done.sem, conv_done.at(n, -4))
                    hold(sp, "sp_held")
                sp.dma_start(cw[par][:, 0:1, :], cw_v[:, bass.ds(n + NP, 1), :]).then_inc(cw_in[par].sem, 16)
                sp.dma_start(cw[par][:, 1:2, :], cw_v[:, bass.ds(n, 1), :]).then_inc(cw_in[par].sem, 16)
                sp.dma_start(cw[par][:, 2:4, :], cw_v[:, bass.ds(n * 2 + 2 * NP, 2), :]).then_inc(
                    cw_in[par].sem, 16)
                if m is None:
                    sp.wait_ge(wo_full.sem, wo_full.at(n, -NC))
                    hold(sp, "sp_held")
                sp.dma_start(wo[par][:, :, :], wo_v[:, bass.ds(n * 2, 2), :]).then_inc(wo_in[par].sem, 16)

            def decays(n):
                sp.wait_ge(am_ready.sem, am_ready.at(n, 0))
                hold(sp, "sp_held")
                sp.wait_ge(wl_ready.sem, wl_ready.at(n, 0))
                hold(sp, "sp_held")
                sp.dma_start(lt[:, :, :], bc(al_v[bass.ds(n, 1)], [128, NU, C])).then_inc(al_in.sem, 16)

            weights(0, 0)
            weights(1, 1)
            sp.wait_ge(flag("decays_ready"), 2)
            sp.dma_start(d_alpha.rearrange("h c t -> h (c t)"),
                         alT.rearrange("h c t -> h (c t)")).then_inc(flag("decays_in_dram"), 16)
            sp.dma_start(d_last, last32).then_inc(flag("last_in_dram"), 16)
            sp.wait_ge(flag("last_in_dram"), 16)
            sp.dma_start(lastb, bc(d_last.rearrange("h c -> (h c)").unsqueeze(0), [128, NH * NC])).then_inc(
                flag("last_spread"), 16)
            sp.wait_ge(flag("decays_in_dram"), 16)
            decays(0)
            decays(1)
            with sp.Fori(1, NP // 2) as i:
                for par in range(2):
                    weights(i * 2 + par, par)
                    decays(i * 2 + par)

            sp.wait_ge(acc_done.sem, acc_done.at(NP, 0))
            sp.dma_start(xs, x_v).then_inc(flag("x_loaded"), 16)
            sp.dma_start(wr_sb, w_router.rearrange("(k p) m -> p k m", p=128)).then_inc(flag("wr_loaded"), 16)

            def expert(e, par, w1, w3, w2s, free):
                if free:
                    sp.wait_ge(mfull.sem, mfull.at(e, 4 - 2 * MFILLS))
                    hold(sp, "sp_held")
                sp.dma_start(w13[par][:, 0:1], w1).then_inc(w13_in[par].sem, 16)
                sp.dma_start(w13[par][:, 1:2], w3).then_inc(w13_in[par].sem, 16)
                if free:
                    sp.wait_ge(mfull.sem, mfull.at(e, -MFILLS))
                    hold(sp, "sp_held")
                sp.dma_start(w2[par].unsqueeze(1), w2s).then_inc(w2_in[par].sem, 16)

            e1, e3 = (w.rearrange("e (k p) h -> p e k h", p=128) for w in (we1, we3))
            e2 = we2.rearrange("e h d -> h e d")
            s1, s3 = (w.rearrange("(k p) (s h) -> p s k h", p=128, h=128) for w in (ws1, ws3))
            s2 = ws2.rearrange("(s h) d -> h s d", h=128)

            def routed(e, par, free):
                one = bass.ds(e, 1)
                expert(e, par, e1[:, one], e3[:, one], e2[:, one], free)

            routed(0, 0, False)
            routed(1, 1, False)
            with sp.Fori(1, NE // 2) as i:
                for par in range(2):
                    routed(i * 2 + par, par, True)
            for s in range(NS):
                expert(NE + s, s % 2, s1[:, s:s + 1], s3[:, s:s + 1], s2[:, s:s + 1], True)
            sp.wait_ge(flag("out_ready"), 1)
            sp.dma_start(out_v, fin).then_inc(flag("out_stored"), 16)
            sp.wait_ge(flag("out_stored"), 16)

        PE = nc.tensor

        @block.tensor
        def _(pe):
            def transposed_rows(part, src):
                for k in range(KT):
                    for q in range(2):
                        b = 2 * k + q
                        for c in range(4):
                            last = PE.transpose(bank[b][:, 128 * c:128 * (c + 1)],
                                                src[:, 4 * q + c, 128 * k:128 * (k + 1)], ident)
                        last.then_inc(flag(f"rows_turned{part}"), 1)

            pe.wait_ge(flag("wmod_loaded"), 16)
            pe.wait_ge(flag("silu_c"), 1)
            for j, slot in enumerate((0, 1, 3, 4)):
                for h in range(2):
                    for k in range(KT):
                        at = slot * D + 128 * h
                        last = PE.matmul(MODB[:, 2 * j + h:2 * j + h + 1], wmod_sb[:, k, at:at + 128],
                                         scT[:, k:k + 1], start=(k == 0), stop=(k == KT - 1))
            last.then_inc(flag("mod_columns"), 1)
            pe.wait_ge(flag("silu_c_spread"), 1)
            for j, slot in enumerate((2, 5)):
                for k in range(KT):
                    last = PE.matmul(GATEB[:, D * j:D * (j + 1)], scb[:, k, :],
                                     wmod_sb[:, k, slot * D:(slot + 1) * D], start=(k == 0), stop=(k == KT - 1))
            last.then_inc(flag("gate_rows"), 1)
            pe.wait_ge(flag("consts_loaded"), 16)
            pe.wait_ge(flag("rows_normed0"), NC)
            transposed_rows(0, xs)
            pe.wait_ge(flag("hT_ready0"), 4)
            pe.wait_ge(flag("wba_loaded"), 16)
            for c in range(NC):
                for k in range(KT):
                    last = PE.matmul(BAB[:, 64 * c:64 * (c + 1)], hT[:, k, C * c:C * (c + 1)], wba_sb[:, k, :],
                                     start=(k == 0), stop=(k == KT - 1))
            last.then_inc(flag("gates_projected"), 1)
            pe.wait_ge(flag("alpha_ready"), 1)
            pe.wait_ge(flag("beta_stored"), 1)
            pe.wait_ge(flag("mods_stored"), 1)
            for c in range(NC):
                last = PE.transpose(bank[4 + c // 4][0:NH, 128 * (c % 4):128 * (c % 4 + 1)],
                                    tmp[3][:, NH * c:NH * (c + 1)], ident)
            last.then_inc(flag("alpha_turned"), 1)
            pe.wait_ge(flag("products_ready"), 1)
            for c in range(NC):
                last = PE.transpose(bank[6][:, NH * c:NH * (c + 1)], eT[:, c, :], ident[0:NH, 0:NH])
            last.then_inc(flag("products_turned"), 1)
            pe.wait_ge(flag("tables_ready"), 1)

            def fill(n, f):
                ev, k = drained(f - RING) if f >= RING else (last_copied, 0)
                if ev is not inv:
                    pe.wait_ge(ev.sem, ev.at(n, k))
                return bank[f % RING]

            def front(n, m, par):
                pe.wait_ge(w_in[par].sem, w_in[par].at(m, 16))
                for t, col in enumerate((KCOL, QCOL, VCOL, VCOL + 128)):
                    for q in range(2):
                        b = fill(n, F_PROJ + 2 * t + q)
                        for k in range(KT):
                            last = PE.matmul(b[:, :], wq[par][:, k, col:col + 128], hT[:, k, 512 * q:512 * (q + 1)],
                                             start=(k == 0), stop=(k == KT - 1))
                        last.then_inc(full.sem, 1)
                for j in range(4):
                    b = fill(n, F_Z + j)
                    for c in (2 * j, 2 * j + 1):
                        for k in range(KT):
                            last = PE.matmul(b[:, D * (c % 2):D * (c % 2 + 1)], hT[:, k, C * c:C * (c + 1)],
                                             wq[par][:, k, ZCOL:ZCOL + D], start=(k == 0), stop=(k == KT - 1))
                    last.then_inc(full.sem, 1)
                for w in range(2):
                    b = fill(n, F_NORM + w)
                    pe.wait_ge(sq_ready.sem, sq_ready.at(n, w + 1))
                    for c in range(NC):
                        last = PE.matmul(b[:, c:c + 1], vT[:, w, C * c:C * (c + 1)], ones, start=True, stop=True)
                    last.then_inc(full.sem, 1)
                for j in range(4):
                    b = fill(n, F_KK + j)
                    for c in (2 * j, 2 * j + 1):
                        last = PE.matmul(b[:, 256 * (c % 2):256 * (c % 2 + 1)], kq[par][:, c, 0, :],
                                         kq[par][:, c, :, :].rearrange("p a b -> p (a b)"), start=True, stop=True)
                    last.then_inc(full.sem, 1)
                for j in range(2):
                    b = fill(n, F_KT + j)
                    for c in range(4):
                        last = PE.transpose(b[:, 128 * c:128 * (c + 1)], kq[par][:, 4 * j + c, 0, :], ident)
                    last.then_inc(full.sem, 1)
                pe.wait_ge(silu_done.sem, silu_done.at(n, 4))
                for j in range(4):
                    b = fill(n, F_VT + j)
                    for i in range(4):
                        c, h = 2 * j + i // 2, i % 2
                        last = PE.transpose(b[:, 128 * i:128 * (i + 1)], vT[:, h, C * c:C * (c + 1)], ident)
                    last.then_inc(full.sem, 1)

            def blocks(b, g, lhs, rhs):
                hold(pe, "pe_held")
                for i in range(UG):
                    u = UG * g + i
                    for lo in (0, HB):
                        last = PE.matmul(b[lo:lo + HB, HB * i:HB * (i + 1)], lhs(u, lo), rhs(u, lo),
                                         start=True, stop=True)
                last.then_inc(full.sem, 1)

            def invert(n, par):
                def a_of(u, lo):
                    return am[par][lo:lo + HB, u, 0, lo:lo + HB]

                def of(t):
                    return lambda u, lo: t[lo:lo + HB, u, :]

                pe.wait_ge(inv.sem, inv.at(n, 3))
                for g in range(2):
                    b = fill(n, F_X1 + g)
                    blocks(b, g, of(xt), lambda u, lo: cst[lo:lo + HB, C_ID64:C_ID64 + HB])
                for lvl in range(LEVELS):
                    f0, done = F_LEVEL + 6 * lvl, 3 + 6 * lvl
                    for g in range(2):
                        b = fill(n, f0 + g)
                        if lvl == 0:
                            pe.wait_ge(x1_copied.sem, x1_copied.at(n, g + 1))
                        else:
                            pe.wait_ge(inv.sem, inv.at(n, done - 6 + (4, 6)[g]))
                        blocks(b, g, a_of, of(xc))
                    for g in range(2):
                        pe.wait_ge(inv.sem, inv.at(n, done + 1 + g))
                        b = fill(n, f0 + 2 + 2 * g)
                        blocks(b, g, of(yc), of(xt))
                        b = fill(n, f0 + 3 + 2 * g)
                        blocks(b, g, of(xt), of(yc))
                for g in range(2):
                    b = fill(n, F_LAST + g)
                    pe.wait_ge(inv.sem, inv.at(n, 3 + 6 * LEVELS - 6 + (4, 6)[g]))
                    hold(pe, "pe_held")
                    for i in range(UG):
                        u = UG * g + i
                        last = PE.matmul(b[HB:C, HB * i:HB * (i + 1)], am[par][0:HB, u, 0, HB:C], xc[0:HB, u, :],
                                         start=True, stop=True)
                    last.then_inc(full.sem, 1)
                for g in range(2):
                    b = fill(n, F_LAST + 2 + g)
                    pe.wait_ge(last_copied.sem, last_copied.at(n, g + 1))
                    hold(pe, "pe_held")
                    for i in range(UG):
                        u = UG * g + i
                        last = PE.matmul(b[0:HB, HB * i:HB * (i + 1)], yc[HB:C, u, :], xf[par][HB:C, u, HB:C],
                                         start=True, stop=True)
                    last.then_inc(full.sem, 1)

            def turn_out(n, c):
                pe.wait_ge(o3_ready.sem, o3_ready.at(n, c + 1))
                pe.wait_ge(acc_done.sem, acc_done.at(n, c))
                for h in range(2):
                    last = PE.transpose(OGB[:, 128 * h:128 * (h + 1)], o2[c % 2][:, h, :], ident)
                last.then_inc(og_full.sem, 1)

            def project_out(n, par, c):
                pe.wait_ge(ogt_ready.sem, ogt_ready.at(n, c + 1))
                pe.wait_ge(won_ready.sem, won_ready.at(n, 1))
                for h in range(2):
                    last = PE.matmul(OGB[:, 256:512], ogt[:, h, :], wo[par][:, h, :], start=(h == 0), stop=(h == 1))
                last.then_inc(wo_full.sem, 1)

            def scan(n, par):
                state = st[:, :, :].rearrange("p a b -> p (a b)")
                pe.wait_ge(km_done.sem, km_done.at(n, 2))
                pe.wait_ge(vp_done.sem, vp_done.at(n, 4))
                pe.wait_ge(last_copied.sem, last_copied.at(n, 4))
                for c in range(NC):
                    if c:
                        pe.wait_ge(st_ready.sem, st_ready.at(n, c))
                        PE.matmul(KSB[:, 0:256], kq[par][:, c, 0, :], state, start=True, stop=True).then_inc(
                            ks_full.sem, 1)
                        pe.wait_ge(o1_ready.sem, o1_ready.at(n, c))
                        PE.matmul(QSB[:, 0:256], kq[par][:, c, 1, :], state, start=True, stop=True).then_inc(
                            qs_full.sem, 1)
                    if c >= 2:
                        project_out(n, par, c - 2)
                    if c:
                        pe.wait_ge(r_ready.sem, r_ready.at(n, c))
                    pe.wait_ge(u_ready.sem, u_ready.at(n, c))
                    for h in range(2):
                        last = PE.matmul(XRB[:, 128 * h:128 * (h + 1)], xf[par][:, NC * h + c, :],
                                         rr[:, h, :] if c else vp[par][:, c, h, :], start=True, stop=True)
                    last.then_inc(xr_full.sem, 1)
                    pe.wait_ge(u_ready.sem, u_ready.at(n, c + 1))
                    if c < NC - 1:
                        if c == 0:
                            pe.wait_ge(st_ready.sem, st_ready.at(n, 0))
                        for h in range(2):
                            last = PE.matmul(KSB[:, 256 + 128 * h:256 + 128 * (h + 1)], km[par][:, NC * h + c, :],
                                             uu[:, h, :], start=True, stop=True)
                        last.then_inc(ku_full.sem, 1)
                    if c:
                        pe.wait_ge(qse_ready.sem, qse_ready.at(n, c))
                    else:
                        pe.wait_ge(o1_ready.sem, o1_ready.at(n, 0))
                    for h in range(2):
                        last = PE.matmul(QSB[:, 256 + 128 * h:256 + 128 * (h + 1)], am[par][:, NC * h + c, 1, :],
                                         uu[:, h, :], start=True, stop=True)
                    last.then_inc(pu_full.sem, 1)
                    if c:
                        turn_out(n, c - 1)
                project_out(n, par, NC - 2)
                turn_out(n, NC - 1)
                project_out(n, par, NC - 1)

            with pe.Fori(0, NP // 2) as i:
                for par in range(2):
                    n = i * 2 + par
                    front(n, i, par)
                    invert(n, par)
                    scan(n, par)

            pe.wait_ge(flag("rows_normed1"), NC)
            transposed_rows(1, xs)
            pe.wait_ge(flag("hT_ready1"), 4)
            pe.wait_ge(flag("wr_loaded"), 16)
            for c in range(NC):
                for k in range(KT):
                    last = PE.matmul(bank[4][:, NE * c:NE * (c + 1)], hT[:, k, C * c:C * (c + 1)], wr_sb[:, k, :],
                                     start=(k == 0), stop=(k == KT - 1))
            last.then_inc(flag("logits_full"), 1)
            pe.wait_ge(flag("router_done"), 1)

            def hidden_tile(e, m, par):
                pe.wait_ge(w13_in[par].sem, w13_in[par].at(m, 32))
                pe.wait_ge(g_ready.sem, g_ready.at(e, 0))
                for q in range(2):
                    for w in range(2):
                        for k in range(KT):
                            last = PE.matmul(bank[2 * q + w][:, :], w13[par][:, w, k, :],
                                             hT[:, k, 512 * q:512 * (q + 1)], start=(k == 0), stop=(k == KT - 1))
                        last.then_inc(mfull.sem, 1)
                pe.wait_ge(w2_in[par].sem, w2_in[par].at(m, 16))
                pe.wait_ge(down_done.sem, down_done.at(e, 0))
                for j in range(4):
                    pe.wait_ge(g_ready.sem, g_ready.at(e, 1 + j // 2))
                    for i in range(2):
                        c = 2 * j + i
                        last = PE.matmul(bank[4 + j][:, D * i:D * (i + 1)], gT[:, C * c:C * (c + 1)], w2[par],
                                         start=True, stop=True)
                    last.then_inc(mfull.sem, 1)

            with pe.Fori(0, NT // 2) as i:
                for par in range(2):
                    hidden_tile(i * 2 + par, i, par)

        @block.scalar
        def _(act):
            act.wait_ge(flag("c_loaded"), 16)
            nc.scalar.activation(scT, cT, ACT.Silu).then_inc(flag("silu_c"), 1)

            def to_hT(part):
                act.wait_ge(flag("mods_stored"), 1)
                for k in range(KT):
                    for q in range(2):
                        act.wait_ge(flag(f"rows_turned{part}"), 2 * k + q + 1)
                        nc.scalar.activation(hT[:, k, 512 * q:512 * (q + 1)], bank[2 * k + q][:, :], ACT.Identity,
                                             bias=modc[:, 4 * part + k:4 * part + k + 1],
                                             scale=modc[:, 4 * part + 2 + k:4 * part + 3 + k]).then_inc(
                                                 flag(f"hT_ready{part}"), 1)

            to_hT(0)
            act.wait_ge(flag("neg_abs_ready"), 1)
            nc.scalar.activation(tmp[2], tmp[1], ACT.Exp).then_inc(flag("exp_ready"), 1)
            act.wait_ge(flag("gates_loaded"), 32)
            nc.scalar.activation(tmp[6][:, 0:NH], alg, ACT.Exp).then_inc(flag("exp_ready"), 1)
            act.wait_ge(flag("b_copied"), 1)
            nc.scalar.activation(tmp[7], tmp[5], ACT.Exp, scale=-1.0).then_inc(flag("exp_ready"), 1)
            act.wait_ge(flag("g_ready"), 1)
            nc.scalar.activation(tmp[3], tmp[4], ACT.Exp, scale=-1.0).then_inc(flag("alpha_ready"), 1)

            def copy_projection(n, t):
                act.wait_ge(conv_done.sem, conv_done.at(n, max(t - 1, 0)))
                for q in range(2):
                    f = F_PROJ + 2 * t + q
                    act.wait_ge(full.sem, full.at(n, f + 1))
                    nc.scalar.activation(xpad[t % 2][:, 3 + 512 * q:3 + 512 * (q + 1)], bank[f % RING][:, :],
                                         ACT.Copy).then_inc(x_copied.sem, 1)

            def silu(n, par, t):
                act.wait_ge(conv_done.sem, conv_done.at(n, t + 1))
                dst = kq[par][:, :, t, :] if t < 2 else vT[:, t - 2, :]
                src = cacc[t % 2][:, :]
                nc.scalar.activation(dst, src.rearrange("p (c t) -> p c t", c=NC) if t < 2 else src,
                                     ACT.Silu).then_inc(silu_done.sem, 1)

            def front(n, par):
                copy_projection(n, 0)
                copy_projection(n, 1)
                silu(n, par, 0)
                copy_projection(n, 2)
                silu(n, par, 1)
                copy_projection(n, 3)
                for j in range(4):
                    act.wait_ge(full.sem, full.at(n, F_Z + j + 1))
                    nc.scalar.activation(sz[par][:, 2 * j:2 * j + 2, :].rearrange("p a b -> p (a b)"),
                                         bank[(F_Z + j) % RING][:, :], ACT.Silu).then_inc(z_ready.sem, 1)
                act.wait_ge(full.sem, full.at(n, F_KK))
                silu(n, par, 2)
                silu(n, par, 3)
                act.wait_ge(rs_ready.sem, rs_ready.at(n, 2))
                for j in range(4):
                    act.wait_ge(full.sem, full.at(n, F_VT + j + 1))
                    for i in range(2):
                        c = 2 * j + i
                        last = nc.scalar.activation(
                            vp[par][:, c, :, :].rearrange("p a b -> p (a b)"),
                            bank[(F_VT + j) % RING][:, 256 * i:256 * (i + 1)], ACT.Copy, scale=nk[par][:, 3, c:c + 1])
                    last.then_inc(vp_done.sem, 1)
                for g in range(2):
                    act.wait_ge(full.sem, full.at(n, F_X1 + g + 1))
                    nc.scalar.activation(xc[:, UG * g:UG * (g + 1), :].rearrange("p a b -> p (a b)"),
                                         bank[(F_X1 + g) % RING][:, :], ACT.Copy).then_inc(x1_copied.sem, 1)
                for g in range(2):
                    act.wait_ge(full.sem, full.at(n, F_LAST + g + 1))
                    nc.scalar.activation(yc[HB:C, UG * g:UG * (g + 1), :].rearrange("p a b -> p (a b)"),
                                         bank[(F_LAST + g) % RING][HB:C, :], ACT.Copy, scale=-1.0).then_inc(
                                             last_copied.sem, 1)
                for g in range(2):
                    act.wait_ge(full.sem, full.at(n, F_LAST + g + 3))
                    nc.scalar.activation(
                        xf[par][0:HB, UG * g:UG * (g + 1), HB:C],
                        bank[(F_LAST + 2 + g) % RING][0:HB, :].rearrange("p (u c) -> p u c", u=UG),
                        ACT.Copy).then_inc(last_copied.sem, 1)

            def copy_out(n, c):
                act.wait_ge(og_full.sem, og_full.at(n, c + 1))
                nc.scalar.activation(ogt[:, :, :].rearrange("p a b -> p (a b)"), OGB[:, 0:256],
                                     ACT.Copy).then_inc(ogt_ready.sem, 1)

            def square_sums(n, par, c):
                act.wait_ge(o2_ready.sem, o2_ready.at(n, c + 1))
                act.wait_ge(ss_ready.sem, ss_ready.at(n, 2 * c))
                for h in range(2):
                    nc.scalar.activation(junk[:, h, :], o2[c % 2][:, h, :], ACT.Square, scale=nk[par][:, 4, c:c + 1],
                                         accum_out=ss[:, c % 2, 0, h:h + 1]).then_inc(ss_ready.sem, 1)

            def scan(n, par):
                for c in range(NC):
                    if c >= 2:
                        copy_out(n, c - 2)
                    if c:
                        act.wait_ge(qs_full.sem, qs_full.at(n, c))
                        for h in range(2):
                            last = nc.scalar.activation(qse[:, h, :], QSB[:, 128 * h:128 * (h + 1)], ACT.Copy,
                                                        scale=sc[par][:, 0, h, c:c + 1])
                        last.then_inc(qse_ready.sem, 1)
                    act.wait_ge(xr_full.sem, xr_full.at(n, c + 1))
                    nc.scalar.activation(uu[:, :, :].rearrange("p a b -> p (a b)"), XRB[:, 0:256],
                                         ACT.Copy).then_inc(u_ready.sem, 1)
                    if c:
                        square_sums(n, par, c - 1)
                copy_out(n, NC - 2)
                square_sums(n, par, NC - 1)
                copy_out(n, NC - 1)

            act.wait_ge(flag("tables_ready"), 1)
            with act.Fori(0, NP // 2) as i:
                for par in range(2):
                    n = i * 2 + par
                    front(n, par)
                    scan(n, par)

            to_hT(1)
            act.wait_ge(flag("logits_shifted"), 1)
            nc.scalar.activation(pv[:, :, 0:NE], lg, ACT.Exp).then_inc(flag("exp_logits"), 1)
            with act.Fori(0, NT // 2) as i:
                for par in range(2):
                    e = i * 2 + par
                    for q in range(2):
                        act.wait_ge(mfull.sem, mfull.at(e, 2 * q + 1))
                        act.wait_ge(g_ready.sem, g_ready.at(e, 0))
                        nc.scalar.activation(sg[q], bank[2 * q][:, :], ACT.Silu).then_inc(sg_ready.sem, 1)

        V = nc.vector

        @block.vector
        def _(dve):
            def then(ins):
                link(dve, "dve_step", ins)

            def norm_rows(part, src):
                for c in range(NC):
                    last = V.bn_stats(stat[:, c, :], src[:, c, :])
                then(last)
                for c in range(NC):
                    last = V.bn_aggr(mv[:, c, :], stat[:, c, :])
                last.then_inc(flag(f"variances{part}"), 1)
                dve.wait_ge(flag(f"variances{part}"), 1)
                dve.wait_ge(flag(f"rstd{part}"), 1)
                for c in range(NC):
                    V.tensor_scalar(xs[:, c, :], src[:, c, :], mv[:, c, 0:1], rstd[:, c:c + 1], ALU.subtract,
                                    ALU.mult).then_inc(flag(f"rows_normed{part}"), 1)

            V.memset(half[:, 0, :], 0.5)
            V.memset(half[:, 1, :], -0.5)
            V.memset(nhalf, -0.5)
            for i in range(2):
                V.memset(xpad[i][:, 0:3], 0.0)
            for i in range(2):
                last = V.memset(xf[i][HB:C, :, 0:HB], 0.0)
            last = V.memset(zero32, 0.0)
            then(last)
            V.tensor_copy(half[:, 0, 0:1], half[:, 0, 1:2]).then_inc(flag("exponents_ready"), 1)
            dve.wait_ge(flag("silu_c"), 1)
            V.tensor_copy(scb, bc(scT.unsqueeze(2), [128, KT, 128])).then_inc(flag("silu_c_spread"), 1)
            dve.wait_ge(flag("x_loaded"), 16)
            norm_rows(0, xs)
            dve.wait_ge(flag("mod_columns"), 1)
            mb = MODB[:, 0:8].rearrange("p (a b) -> p a b", a=4)
            mc = modc[:, :].rearrange("p (a b) -> p a b", a=4)
            V.tensor_copy(mc[:, 0:4:2, :], mb[:, 0:4:2, :])
            V.tensor_scalar(mc[:, 1:4:2, :], mb[:, 1:4:2, :], 1.0, None, ALU.add)
            dve.wait_ge(flag("gate_rows"), 1)
            g_all = gate[:, :, :].rearrange("p a b -> p (a b)")
            sign = lt[:, 0:4, :].rearrange("p a b -> p (a b)")
            mag = lt[:, 4:8, :].rearrange("p a b -> p (a b)")
            V.tensor_scalar(sign, GATEB[:, :], 0.0, 2.0, ALU.is_ge, ALU.mult)
            then(V.tensor_scalar(mag, GATEB[:, :], -1.0, None, ALU.mult))
            then(V.tensor_tensor(mag, GATEB[:, :], mag, ALU.max))
            then(V.tensor_scalar(mag, mag, 0.25, None, ALU.max))
            V.scalar_tensor_tensor(out=g_all, in0=sign, scalar=-1.0, in1=mag, op0=ALU.add,
                                   op1=ALU.mult).then_inc(flag("mods_stored"), 1)
            dve.wait_ge(flag("gates_projected"), 1)
            dve.wait_ge(flag("gates_loaded"), 32)
            ba = BAB[:, :].rearrange("p (c g k r) -> p c g k r", c=NC, g=NP, k=2)

            def by_head(t):
                return t.rearrange("p (c g r) -> p c g r", c=NC, g=NP)

            aa, neg, y, al, gg, bb = tmp[0], tmp[1], tmp[2], tmp[3], tmp[4], tmp[5]
            then(V.tensor_copy(by_head(aa), ba[:, :, :, 1, :]))
            then(V.tensor_tensor(aa.rearrange("p (c h) -> p c h", c=NC), aa.rearrange("p (c h) -> p c h", c=NC),
                                 bc(dtb.unsqueeze(1), [128, NC, NH]), ALU.add))
            then(V.tensor_scalar(neg, aa, -1.0, None, ALU.mult))
            then(V.tensor_tensor(neg, aa, neg, ALU.min))
            then(V.tensor_scalar(neg, neg, 1.0, None, ALU.mult))
            V.tensor_copy(gg, neg).then_inc(flag("neg_abs_ready"), 1)
            V.tensor_copy(by_head(bb), ba[:, :, :, 0, :]).then_inc(flag("b_copied"), 1)
            dve.wait_ge(flag("exp_ready"), 3)
            den, s2 = tmp[1], tmp[4]
            then(V.tensor_scalar(den, y, 2.0, None, ALU.add))
            then(V.reciprocal(den, den))
            then(V.tensor_tensor(y, y, den, ALU.mult))
            then(V.tensor_tensor(s2, y, y, ALU.mult))
            then(V.tensor_scalar(den, s2, 1.0 / 19, None, ALU.mult))
            for k in range(8, 0, -1):
                then(V.scalar_tensor_tensor(out=den, in0=den, scalar=1.0 / (2 * k + 1), in1=s2, op0=ALU.add,
                                            op1=ALU.mult))
            then(V.scalar_tensor_tensor(out=den, in0=den, scalar=1.0, in1=y, op0=ALU.add, op1=ALU.mult))
            then(V.tensor_scalar(aa, aa, 0.0, None, ALU.max))
            then(V.scalar_tensor_tensor(out=aa, in0=den, scalar=2.0, in1=aa, op0=ALU.mult, op1=ALU.add))
            V.tensor_tensor(gg.rearrange("p (c h) -> p c h", c=NC), aa.rearrange("p (c h) -> p c h", c=NC),
                            bc(tmp[6][:, 0:NH].unsqueeze(1), [128, NC, NH]), ALU.mult).then_inc(flag("g_ready"), 1)
            then(V.tensor_scalar(bb, tmp[7], 1.0, None, ALU.add))
            then(V.reciprocal(bb, bb))

            def table(kind):
                return tab[:, :, kind, :, :]

            def heads_first(t):
                return t.rearrange("p (c g r) -> p g r c", c=NC, g=NP)

            for r in range(2):
                last = V.tensor_copy(table(2)[:, :, r, :], heads_first(bb)[:, :, r, :])
            last.then_inc(flag("beta_stored"), 1)
            dve.wait_ge(flag("alpha_turned"), 1)
            for q in range(2):
                last = V.tensor_copy(alT[:, 4 * q:4 * q + 4, :].rearrange("p a b -> p (a b)"), bank[4 + q][0:NH, :])
            last.then_inc(flag("decays_ready"), 1)
            dve.wait_ge(flag("decays_ready"), 1)
            for c in range(NC):
                last = V.tensor_tensor_scan(eT[:, c, :], alT[:, c, :], zero32, 1.0, ALU.mult, ALU.add)
            last.then_inc(flag("products_ready"), 1)
            dve.wait_ge(flag("products_ready"), 1)
            V.tensor_copy(last32, eT[:, :, C - 1]).then_inc(flag("decays_ready"), 1)
            dve.wait_ge(flag("products_turned"), 1)
            eb = heads_first(bank[6][:, 0:NC * NH])
            for r in range(2):
                V.tensor_scalar(table(0)[:, :, r, :], eb[:, :, r, :], -1.0, None, ALU.mult)
            dve.wait_ge(flag("last_spread"), 16)
            V.tensor_copy(table(1), lastb.rearrange("p (g r c) -> p g r c", g=NP, r=2)).then_inc(
                flag("tables_ready"), 1)
            dve.wait_ge(flag("tables_ready"), 1)
            dve.wait_ge(flag("consts_loaded"), 16)

            def conv(n, m, par, t):
                dve.wait_ge(x_copied.sem, x_copied.at(n, 2 * t + 2))
                dve.wait_ge(silu_done.sem, silu_done.at(n, max(t - 1, 0)))
                if t == 0:
                    dve.wait_ge(cw_in[par].sem, cw_in[par].at(m, 48))
                a, src = cacc[t % 2][:, :], xpad[t % 2]
                V.tensor_scalar(a, src[:, 0:T], cw[par][:, t, 0:1], None, ALU.mult).then_inc(tap.sem, 1)
                for j in range(1, 4):
                    dve.wait_ge(tap.sem, tap.at(n, 3 * t + j))
                    V.scalar_tensor_tensor(out=a, in0=src[:, j:j + T], scalar=cw[par][:, t, j:j + 1], in1=a,
                                           op0=ALU.mult, op1=ALU.add).then_inc((tap if j < 3 else conv_done).sem, 1)

            def front(n, m, par):
                V.tensor_copy(sc[par][:, :, :, :].rearrange("p k r c -> p (k r c)"),
                              tab[:, bass.ds(n, 1), :, :, :].rearrange("p g k r c -> p (g k r c)")).then_inc(
                                  sc_ready.sem, 1)
                dve.wait_ge(al_in.sem, al_in.at(n, 16))
                for u in range(NU):
                    last = V.tensor_tensor_scan(lt[:, u, :], lt[:, u, :], ident, 0.0, ALU.mult, ALU.add)
                last.then_inc(lt_ready.sem, 1)
                for t in range(4):
                    conv(n, m, par, t)
                dve.wait_ge(full.sem, full.at(n, F_NORM + 1))
                V.tensor_scalar(nk[par][:, 0, :], bank[F_NORM % RING][:, 0:NC], 1e-6, None, ALU.add).then_inc(
                    nk_ready.sem, 1)
                dve.wait_ge(full.sem, full.at(n, F_NORM + 2))
                V.tensor_scalar(nk[par][:, 1, :], bank[(F_NORM + 1) % RING][:, 0:NC], 1e-6, float(C), ALU.add,
                                ALU.mult).then_inc(nk_ready.sem, 1)
                dve.wait_ge(nk_ready.sem, nk_ready.at(n, 1))
                V.reciprocal(nk[par][:, 2, :], nk[par][:, 0, :]).then_inc(s_ready.sem, 1)
                dve.wait_ge(s_ready.sem, s_ready.at(n, 1))
                dve.wait_ge(sc_ready.sem, sc_ready.at(n, 1))
                V.tensor_tensor(sj[:, :, :], sc[par][:, 2, :, :], bc(nk[par][:, 2:3, :], [128, 2, NC]),
                                ALU.mult).then_inc(s_ready.sem, 1)
                dve.wait_ge(s_ready.sem, s_ready.at(n, 2))
                dve.wait_ge(lt_ready.sem, lt_ready.at(n, 1))
                for j in range(4):
                    dve.wait_ge(full.sem, full.at(n, F_KK + j + 1))
                    for i in range(4):
                        c, h = 2 * j + i // 2, i % 2
                        u = NC * h + c
                        last = V.scalar_tensor_tensor(
                            out=am[par][:, u, :, :],
                            in0=bank[(F_KK + j) % RING][:, 256 * (c % 2):256 * (c % 2 + 1)].rearrange(
                                "p (a b) -> p a b", a=2),
                            scalar=sj[:, h, c:c + 1], in1=bc(lt[:, u:u + 1, :], [128, 2, C]),
                            op0=ALU.mult, op1=ALU.mult)
                    last.then_inc(am_ready.sem, 1)
                V.tensor_tensor(wl[:, :, :], sj[:, :, :],
                                lt[:, :, C - 1].rearrange("p (h c) -> p h c", h=2), ALU.mult).then_inc(wl_ready.sem, 1)
                dve.wait_ge(wl_ready.sem, wl_ready.at(n, 1))
                for j in range(2):
                    dve.wait_ge(full.sem, full.at(n, F_KT + j + 1))
                    for h in range(2):
                        last = V.tensor_tensor(
                            km[par][:, NC * h + 4 * j:NC * h + 4 * j + 4, :],
                            bank[(F_KT + j) % RING][:, :].rearrange("p (c d) -> p c d", c=4),
                            bc(wl[:, h, 4 * j:4 * j + 4].unsqueeze(2), [128, 4, C]), ALU.mult)
                    last.then_inc(km_done.sem, 1)

            def invert(n, par):
                dve.wait_ge(am_ready.sem, am_ready.at(n, 4))
                for lo in (0, HB):
                    V.tensor_tensor(xt[lo:lo + HB, :, :], am[par][lo:lo + HB, :, 0, lo:lo + HB],
                                    mask(lo, lo + HB, 0, NU), ALU.mult).then_inc(inv.sem, 1)
                dve.wait_ge(inv.sem, inv.at(n, 2))
                V.tensor_tensor(xt[:, :, :], xt[:, :, :],
                                bc(cst[:, C_ID64:C_ID64 + HB].unsqueeze(1), [128, NU, HB]), ALU.add).then_inc(inv.sem, 1)
                for lvl in range(LEVELS):
                    f0 = F_LEVEL + 6 * lvl

                    def filled(k):
                        return bank[(f0 + k) % RING][:, :].rearrange("p (u c) -> p u c", u=UG)

                    for g in range(2):
                        dve.wait_ge(full.sem, full.at(n, f0 + g + 1))
                        V.tensor_tensor(yc[:, UG * g:UG * (g + 1), :], filled(g), mask(0, 128, lvl + 1, UG),
                                        ALU.mult).then_inc(inv.sem, 1)
                    for g in range(2):
                        us = slice(UG * g, UG * (g + 1))
                        dve.wait_ge(full.sem, full.at(n, f0 + 4 + 2 * g))
                        if lvl < LEVELS - 1:
                            last = V.tensor_tensor(xt[:, us, :], filled(2 + 2 * g), xt[:, us, :], ALU.add)
                        else:
                            for lo in (0, HB):
                                last = V.tensor_tensor(xf[par][lo:lo + HB, us, lo:lo + HB],
                                                       filled(2 + 2 * g)[lo:lo + HB], xt[lo:lo + HB, us, :], ALU.add)
                        last.then_inc(inv.sem, 1)
                        V.tensor_tensor(xc[:, us, :], filled(3 + 2 * g), xc[:, us, :], ALU.add).then_inc(inv.sem, 1)

            def add_out(n, c):
                dve.wait_ge(wo_full.sem, wo_full.at(n, c + 1))
                V.tensor_tensor(acc[:, c, :], OGB[:, 256:512], acc[:, c, :], ALU.add).then_inc(acc_done.sem, 1)

            def scan(n, par):
                for c in range(NC):
                    if c:
                        dve.wait_ge(ks_full.sem, ks_full.at(n, c))
                        if c == 1:
                            dve.wait_ge(vp_done.sem, vp_done.at(n, 4))
                        for h in range(2):
                            last = V.scalar_tensor_tensor(out=rr[:, h, :], in0=KSB[:, 128 * h:128 * (h + 1)],
                                                          scalar=sc[par][:, 0, h, c:c + 1], in1=vp[par][:, c, h, :],
                                                          op0=ALU.mult, op1=ALU.add)
                        last.then_inc(r_ready.sem, 1)
                    if c >= 2:
                        add_out(n, c - 2)
                    if c < NC - 1:
                        dve.wait_ge(ku_full.sem, ku_full.at(n, c + 1))
                        for h in range(2):
                            ku = KSB[:, 256 + 128 * h:256 + 128 * (h + 1)]
                            if c == 0:
                                last = V.tensor_copy(st[:, h, :], ku)
                            else:
                                last = V.scalar_tensor_tensor(out=st[:, h, :], in0=st[:, h, :],
                                                              scalar=sc[par][:, 1, h, c:c + 1], in1=ku,
                                                              op0=ALU.mult, op1=ALU.add)
                        last.then_inc(st_ready.sem, 1)
                    dve.wait_ge(pu_full.sem, pu_full.at(n, c + 1))
                    dve.wait_ge(o2_ready.sem, o2_ready.at(n, max(c - 1, 0)))
                    pu = QSB[:, 256:512].rearrange("p (a b) -> p a b", a=2)
                    if c == 0:
                        last = V.tensor_copy(o1[0][:, :, :], pu)
                    else:
                        dve.wait_ge(qse_ready.sem, qse_ready.at(n, c))
                        last = V.tensor_tensor(o1[c % 2][:, :, :], pu, qse[:, :, :], ALU.subtract)
                    last.then_inc(o1_ready.sem, 1)
                add_out(n, NC - 2)
                add_out(n, NC - 1)

            dve.wait_ge(flag("acc_cleared"), 1)
            with dve.Fori(0, NP // 2) as i:
                for par in range(2):
                    n = i * 2 + par
                    front(n, i, par)
                    invert(n, par)
                    scan(n, par)

            dve.wait_ge(flag("x_loaded"), 32)
            dve.wait_ge(acc_done.sem, acc_done.at(NP, 0))
            then(V.tensor_tensor(acc[:, :, :], acc[:, :, :], bc(gate[:, 0:1, :], [128, NC, D]), ALU.mult))
            then(V.tensor_tensor(acc[:, :, :], acc[:, :, :], xs, ALU.add))
            norm_rows(1, acc)
            dve.wait_ge(flag("logits_full"), 1)
            lb = bank[4][:, 0:NC * NE].rearrange("p (c e) -> p c e", c=NC)
            then(V.tensor_reduce(row, lb, AX.X, ALU.max))
            V.tensor_tensor(lg, lb, bc(row.unsqueeze(2), [128, NC, NE]), ALU.subtract).then_inc(
                flag("logits_shifted"), 1)
            dve.wait_ge(flag("exp_logits"), 1)
            then(V.tensor_reduce(row, pv[:, :, 0:NE], AX.X, ALU.add))
            then(V.reciprocal(row, row))
            then(V.tensor_tensor(pv[:, :, 0:NE], pv[:, :, 0:NE], bc(row.unsqueeze(2), [128, NC, NE]), ALU.mult))
            for c in range(NC):
                last = V.max(top[:, c, :], pv[:, c, 0:NE])
            then(last)
            V.memset(pv[:, :, NE:WP], -1.0)
            then(V.memset(top[:, :, TOPK:8], -1.0))
            for c in range(NC):
                last = V.match_replace(rep[:, c, :], top[:, c, :], pv[:, c, :], -2.0)
            then(last)
            then(V.scalar_tensor_tensor(out=lg, in0=rep[:, :, 0:NE], scalar=-1.5, in1=pv[:, :, 0:NE], op0=ALU.is_lt,
                                        op1=ALU.mult))
            then(V.tensor_reduce(row, lg, AX.X, ALU.add))
            then(V.reciprocal(row, row))
            then(V.tensor_scalar(row, row, TOPK / (TOPK + 1.0), None, ALU.mult))
            V.tensor_tensor(cwt[:, 0:NE, :].rearrange("p e c -> p c e"), lg, bc(row.unsqueeze(2), [128, NC, NE]),
                            ALU.mult)
            V.memset(cwt[:, NE:NT, :], 1.0 / (TOPK + 1.0)).then_inc(flag("router_done"), 1)
            dve.wait_ge(flag("router_done"), 1)
            dve.wait_ge(flag("acc2_cleared"), 1)

            with dve.Fori(0, NT // 2) as i:
                for par in range(2):
                    e = i * 2 + par
                    V.tensor_copy(cwe[par], cwt[:, bass.ds(e, 1), :].rearrange("p a c -> p (a c)")).then_inc(
                        cwe_ready.sem, 1)
                    for q in range(2):
                        dve.wait_ge(mfull.sem, mfull.at(e, 2 * q + 2))
                        dve.wait_ge(sg_ready.sem, sg_ready.at(e, q + 1))
                        V.tensor_tensor(gT[:, 512 * q:512 * (q + 1)], bank[2 * q + 1][:, :], sg[q],
                                        ALU.mult).then_inc(g_ready.sem, 1)
                    dve.wait_ge(cwe_ready.sem, cwe_ready.at(e, 1))
                    dve.wait_ge(down_done.sem, down_done.at(e, 0))
                    for c in range(NC):
                        dve.wait_ge(mfull.sem, mfull.at(e, 4 + c // 2 + 1))
                        V.scalar_tensor_tensor(out=acc2[:, c, :], in0=bank[4 + c // 2][:, D * (c % 2):D * (c % 2 + 1)],
                                               scalar=cwe[par][:, c:c + 1], in1=acc2[:, c, :], op0=ALU.mult,
                                               op1=ALU.add).then_inc(down_done.sem, 1)
            dve.wait_ge(down_done.sem, down_done.at(NT, 0))
            then(V.tensor_tensor(acc2, acc2, bc(gate[:, 1:2, :], [128, NC, D]), ALU.mult))
            V.tensor_tensor(fin, acc2, acc[:, :, :], ALU.add).then_inc(flag("out_ready"), 1)

        @block.gpsimd
        def _(pool):
            P = nc.gpsimd
            for r in rounds:
                pool.sem_inc(r.sem, 1)
            P.memset(acc[:, :, :], 0.0).then_inc(flag("acc_cleared"), 1)

            def rstds(part):
                pool.wait_ge(flag(f"variances{part}"), 1)
                link(pool, "pool_step", P.tensor_scalar(rstd, mv[:, :, 1], 1e-5, None, ALU.add))
                P.tensor_tensor(rstd, rstd, nhalf, ALU.pow).then_inc(flag(f"rstd{part}"), 1)

            pool.wait_ge(flag("exponents_ready"), 1)
            rstds(0)
            pool.wait_ge(flag("tables_ready"), 1)
            pool.wait_ge(flag("nw_loaded"), 16)

            def front(n, m, par):
                pool.wait_ge(wo_in[par].sem, wo_in[par].at(m, 16))
                hold(pool, "pool_held")
                P.tensor_scalar(wo[par][:, :, :], wo[par][:, :, :], nw[:, :], None, ALU.mult).then_inc(won_ready.sem, 1)
                for w in range(2):
                    pool.wait_ge(silu_done.sem, silu_done.at(n, w + 1))
                    src = kq[par][:, :, w, :]
                    P.tensor_tensor(vT[:, w, :].rearrange("p (c t) -> p c t", c=NC), src, src,
                                    ALU.mult).then_inc(sq_ready.sem, 1)
                pool.wait_ge(nk_ready.sem, nk_ready.at(n, 2))
                for w in range(2):
                    P.tensor_tensor(nk[par][:, 3 + w, :], nk[par][:, w, :], half[:, w, :],
                                    ALU.pow).then_inc(rs_ready.sem, 1)

            def scan(n, par):
                pool.wait_ge(z_ready.sem, z_ready.at(n, 4))
                pool.wait_ge(rs_ready.sem, rs_ready.at(n, 2))
                for c in range(NC):
                    pool.wait_ge(o1_ready.sem, o1_ready.at(n, c + 1))
                    pool.wait_ge(og_full.sem, og_full.at(n, max(c - 1, 0)))
                    P.tensor_tensor(o2[c % 2][:, :, :], o1[c % 2][:, :, :],
                                    sz[par][:, c, :].rearrange("p (a b) -> p a b", a=2), ALU.mult).then_inc(
                                        o2_ready.sem, 1)
                    sq, t1, t2, t3 = (ss[:, c % 2, k, :] for k in range(4))
                    pool.wait_ge(ss_ready.sem, ss_ready.at(n, 2 * c + 2))
                    hold(pool, "pool_held")
                    P.tensor_scalar(t1, sq, 1.0 / C, 1e-6, ALU.mult, ALU.add).then_inc(f_step.sem, 1)
                    pool.wait_ge(f_step.sem, f_step.at(n, 3 * c + 1))
                    P.tensor_tensor(t2, t1, half[:, 1, 0:2], ALU.pow).then_inc(f_step.sem, 1)
                    pool.wait_ge(f_step.sem, f_step.at(n, 3 * c + 2))
                    hold(pool, "pool_held")
                    P.tensor_scalar(t3, t2, nk[par][:, 4, c:c + 1], None, ALU.mult).then_inc(f_step.sem, 1)
                    pool.wait_ge(f_step.sem, f_step.at(n, 3 * c + 3))
                    P.tensor_tensor(o2[c % 2][:, :, :], o2[c % 2][:, :, :], bc(t3.unsqueeze(2), [128, 2, C]),
                                    ALU.mult).then_inc(o3_ready.sem, 1)

            with pool.Fori(0, NP // 2) as i:
                for par in range(2):
                    n = i * 2 + par
                    front(n, i, par)
                    scan(n, par)
            pool.wait_ge(acc_done.sem, acc_done.at(NP, 0))
            P.memset(acc2, 0.0).then_inc(flag("acc2_cleared"), 1)
            rstds(1)


_INS = ["L0_attn_hidden_states", "L0_attn_W_qkvz", "L0_attn_W_ba", "L0_attn_conv_w", "L0_attn_dt_bias",
        "L0_attn_A_log", "L0_attn_norm_weight", "L0_attn_W_out", "L0_ffn_w_router", "L0_ffn_we1", "L0_ffn_we3",
        "L0_ffn_we2", "L0_ffn_ws1", "L0_ffn_ws3", "L0_ffn_ws2", "L0_c", "L0_wmod"]


def constants():
    c = np.zeros((128, C_N), np.float32)
    c[:, C_ID:C_ID + 128] = np.eye(128)
    p, q = np.arange(128)[:, None] % HB, np.arange(HB)[None, :]
    c[:, C_ID64:C_ID64 + HB] = p == q
    c[:, C_MASK:C_MASK + HB] = -1.0 * ((p // 2 == q // 2) & (p < q))
    for lvl in range(1, LEVELS + 1):
        b = 2 ** lvl
        c[:, C_MASK + HB * lvl:C_MASK + HB * (lvl + 1)] = -1.0 * ((p // (2 * b) == q // (2 * b)) & (p // b > q // b))
    c[:, C_ONE] = 1.0
    return c


def kernel(**inputs):
    import concourse.bacc as _bacc
    from concourse.bass_utils import run_bass_kernel_spmd as _run

    nc = _bacc.Bacc("TRN2", target_bir_lowering=False, num_devices=1)
    arrays, args = {}, []
    for name in _INS:
        a = np.ascontiguousarray(inputs[name])
        arrays[f"in_{name}"] = a
        args.append(nc.dram_tensor(f"in_{name}", a.shape, F32, kind="ExternalInput").ap())
    arrays["in_constants"] = constants()
    args.append(nc.dram_tensor("in_constants", (128, C_N), F32, kind="ExternalInput").ap())
    args.append(nc.dram_tensor("decays", (NH, NC, C), F32, kind="Internal").ap())
    args.append(nc.dram_tensor("last_decays", (NH, NC), F32, kind="Internal").ap())
    args.append(nc.dram_tensor("out_0", (1, T, D), F32, kind="ExternalOutput").ap())
    adaln_block(nc, *args)
    r = _run(nc, [arrays], core_ids=[0])
    return r.results[0]["out_0"]
```

```python
import numpy as np
import concourse.bass as bass
from concourse import mybir
from contextlib import ExitStack

F32 = mybir.dt.float32
ALU = mybir.AluOpType
ACT = mybir.ActivationFunctionType
AX = mybir.AxisListType

T, D = 1024, 256
C = 128
NC = T // C
KT = D // 128
NP = 16
NH = 2 * NP
PW = 768
QCOL, KCOL, VCOL, ZCOL = 0, 128, 256, 512
NE, NS, TOPK = 16, 4, 4
HB = 64
BB = 16
LEVELS = 2
UG = 8
NU = 2 * NC
FILLS = 42
RING = 4
NT = NE + NS
MFILLS = 8
F_PROJ, F_NORM, F_KK, F_Z, F_KT, F_X1, F_LEVEL = 0, 8, 10, 14, 18, 20, 22
F_LAST = F_LEVEL + 6 * LEVELS
F_VT = F_LAST + 4
C_ID, C_ID64, C_MASK = 0, 128, 192
C_ONE = C_MASK + HB * LEVELS
C_ID16 = C_ONE + 1
C_BASE = C_ID16 + BB
C_PLACE = C_BASE + 2 * BB
C_N = C_PLACE + HB



class Count:

    def __init__(self, sem, per):
        self.sem, self.per = sem, per

    def at(self, n, k):
        return n * self.per + (k + 1)


def adaln_block(nc, x, w_qkvz, w_ba, conv_w, dt_bias, a_log, norm_w, w_out, w_router, we1, we3, we2,
                ws1, ws3, ws2, c_in, wmod, consts, d_alpha, d_last, out):
    ctx = ExitStack()
    with ctx:
        def sb(name, shape):
            return ctx.enter_context(nc.sbuf_tensor(name, shape, F32))

        def sem(name):
            return ctx.enter_context(nc.semaphore(name))

        rounds = []

        def counted(name, per):
            rounds.append(Count(sem(name), per))
            return rounds[-1]

        cst = sb("cst", [128, C_N])
        hT = sb("hT", [128, KT, T])
        wq = [sb(f"wq{i}", [128, KT, PW]) for i in range(2)]
        cw = [sb(f"cw{i}", [128, 4, 4]) for i in range(2)]
        wo = [sb(f"wo{i}", [128, 2, D]) for i in range(2)]
        xpad = [sb(f"xpad{i}", [128, T + 3]) for i in range(2)]
        cacc = [sb(f"cacc{i}", [128, T]) for i in range(2)]
        kq = [sb(f"kq{i}", [128, NC, 2, C]) for i in range(2)]
        vT = sb("vT", [128, 2, T])
        sz = [sb(f"sz{i}", [128, NC, 2 * C]) for i in range(2)]
        lt = sb("lt", [128, NU, C])
        am = [sb(f"am{i}", [128, NU, 2, C]) for i in range(2)]
        km = [sb(f"km{i}", [128, NU, C]) for i in range(2)]
        vp = [sb(f"vp{i}", [128, NC, 2, C]) for i in range(2)]
        xf = [sb(f"xf{i}", [128, NU, C]) for i in range(2)]
        xt = sb("xt", [128, NU, HB])
        xc = sb("xc", [128, NU, HB])
        yc = sb("yc", [128, NU, HB])
        acc = sb("acc", [128, NC, D])
        st = sb("st", [128, 2, C])
        rr = sb("rr", [128, 2, C])
        uu = sb("uu", [128, 2, C])
        qse = sb("qse", [128, 2, C])
        o1 = [sb(f"o1{i}", [128, 2, C]) for i in range(2)]
        o2 = [sb(f"o2{i}", [128, 2, C]) for i in range(2)]
        ogt = sb("ogt", [128, 2, C])
        junk = sb("junk", [128, 2, C])
        tab = sb("tab", [128, NP, 3, 2, NC])
        sc = [sb(f"sc{i}", [128, 3, 2, NC]) for i in range(2)]
        nk = [sb(f"nk{i}", [128, 5, NC]) for i in range(2)]
        sj = sb("sj", [128, 2, NC])
        wl = sb("wl", [128, 2, NC])
        half = sb("half", [128, 2, NC])
        ss = sb("ss", [128, 2, 4, 2])
        nw = sb("nw", [128, 1])
        sm = sb("sm", [128, 128])
        modc = sb("modc", [128, 8])
        gate = sb("gate", [128, 2, D])
        bank = [ctx.enter_context(nc.psum_tensor(f"bank{i}", [128, 512], F32)) for i in range(8)]
        KSB, XRB, QSB, OGB = bank[4], bank[5], bank[6], bank[7]

        ident = cst[:, C_ID:C_ID + 128]
        ones = cst[:, C_ONE:C_ONE + 1]

        def bc(ap, shape):
            return ap.broadcast_to(shape)

        def mask(lo, hi, lvl, units):
            m = cst[lo:hi, C_MASK + HB * lvl:C_MASK + HB * (lvl + 1)]
            return bc(m.unsqueeze(1), [hi - lo, units, HB])

        flags = {}

        def flag(name):
            if name not in flags:
                flags[name] = sem(name)
            return flags[name]

        steps = {}

        def link(eng, name, ins):
            steps[name] = steps.get(name, 0) + 1
            ins.then_inc(flag(name), 1)
            eng.wait_ge(flag(name), steps[name])

        def hold(eng, name):
            eng.sem_inc(flag(name), 1)

        w_in = [counted(f"w_loaded{i}", 16) for i in range(2)]
        cw_in = [counted(f"taps_loaded{i}", 48) for i in range(2)]
        wo_in = [counted(f"wout_loaded{i}", 16) for i in range(2)]
        al_in = counted("decays_loaded", 16)
        full = counted("bank_filled", FILLS)
        x_copied = counted("projection_copied", 8)
        z_ready = counted("z_ready", 4)
        conv_done = counted("conv_done", 4)
        tap = counted("tap_added", 12)
        silu_done = counted("silu_done", 4)
        sq_ready = counted("squares_ready", 2)
        sc_ready = counted("scalars_ready", 1)
        nk_ready = counted("norms_ready", 2)
        rs_ready = counted("roots_ready", 2)
        s_ready = counted("s_ready", 2)
        lt_ready = counted("decay_products_ready", 1)
        am_ready = counted("attention_matrices_ready", 4)
        wl_ready = counted("key_scales_ready", 1)
        km_done = counted("keys_scaled", 2)
        vp_done = counted("values_scaled", 4)
        base = counted("substitution_steps", 6 + 3 * (BB - 1))
        inv = counted("inverse_parts", 1 + 6 * LEVELS)
        x1_copied = counted("x1_copied", 2)
        last_copied = counted("last_blocks_copied", 4)
        won_ready = counted("wout_scaled", 1)
        ks_full, qs_full, ku_full = (counted(f"{w}_full", NC - 1) for w in ("ks", "qs", "ku"))
        xr_full, pu_full, og_full, wo_full = (counted(f"{w}_full", NC) for w in ("xr", "pu", "og", "wo"))
        r_ready, st_ready, qse_ready = (counted(f"{w}_ready", NC - 1) for w in ("r", "state", "qse"))
        o1_ready, u_ready, ogt_ready, o2_ready, o3_ready, acc_done = (
            counted(w, NC) for w in ("o1_ready", "u_ready", "ogt_ready", "o2_ready", "o3_ready", "acc_done"))
        ss_ready = counted("ss_ready", 2 * NC)
        f_step = counted("scale_steps", 3 * NC)
        w13_in = [counted(f"w13_loaded{i}", 32) for i in range(2)]
        w2_in = [counted(f"w2_loaded{i}", 16) for i in range(2)]
        mfull = counted("moe_bank_filled", MFILLS)
        sg_ready = counted("silu_gate_ready", 2)
        g_ready = counted("hidden_ready", 2)
        cwe_ready = counted("weights_ready", 1)
        down_done = counted("down_added", NC)

        def drained(f):
            if f < F_NORM:
                return x_copied, f - F_PROJ + 1
            if f < F_KK:
                return nk_ready, f - F_NORM + 1
            if f < F_Z:
                return am_ready, f - F_KK + 1
            if f < F_KT:
                return z_ready, f - F_Z + 1
            if f < F_X1:
                return km_done, f - F_KT + 1
            if f < F_LEVEL:
                return x1_copied, f - F_X1 + 1
            if f < F_LAST:
                return inv, 1 + f - F_LEVEL + 1
            if f < F_VT:
                return last_copied, f - F_LAST + 1
            return vp_done, f - F_VT + 1

        def ring(f, par):
            return bank[(f + FILLS * par) % RING]

        def pairs(eng, front, scan):
            def both(n, before, m, par):
                work = front(n, m, par)
                scan(before, 1 - par, lambda: next(work, None))
                assert next(work, "over") == "over"

            for _ in front(0, 0, 0):
                pass
            with eng.Fori(0, NP // 2 - 1) as i:
                both(i * 2 + 1, i * 2, i, 1)
                both(i * 2 + 2, i * 2 + 1, i + 1, 0)
            both(NP - 1, NP - 2, NP // 2 - 1, 1)
            scan(NP - 1, 1, lambda: None)

        w_v = w_qkvz.rearrange("(k p) m -> p k m", p=128)
        wo_v = w_out.rearrange("(h p) m -> p h m", p=128)
        cw_v = conv_w.rearrange("(t p) j -> p t j", p=128)
        x_v = x.rearrange("b (c p) d -> p (b c) d", p=128)
        out_v = out.rearrange("b (c p) d -> p (b c) d", p=128)
        al_v = d_alpha.rearrange("(g h) c t -> g (h c) t", h=2)

        xs = vT[:, :, :].rearrange("p a (b d) -> p (a b) d", d=D)
        wmod_sb = am[0][:, :, :, :].rearrange("p u a c -> p (u a c)")[:, 0:KT * 6 * D].rearrange(
            "p (k m) -> p k m", k=KT)
        wba_sb = km[0][:, 0, :].rearrange("p (k m) -> p k m", k=KT)
        dtb, alg = km[0][:, 1, 0:NH], km[0][:, 1, NH:2 * NH]
        scb = km[0][:, 2:4, :]
        zero32 = km[0][0:NH, 4, :]
        last32 = km[0][0:NH, 5, 0:NC]
        lastb = km[0][:, 6:8, :].rearrange("p a b -> p (a b)")
        cT, scT = sm[:, 0:2], sm[:, 2:4]
        stat = sm[:, 4:52].rearrange("p (c k) -> p c k", k=6)
        mv = sm[:, 52:68].rearrange("p (c k) -> p c k", k=2)
        rstd, nhalf = sm[:, 68:76], sm[:, 76:84]
        tmp = [vp[0][:, i, :, :].rearrange("p a b -> p (a b)") for i in range(NC)]
        alT = xf[1][0:NH, 0:NC, :]
        eT = xf[1][0:NH, NC:2 * NC, :]
        wr_sb = km[0][:, 0, 0:KT * NE].rearrange("p (k m) -> p k m", k=KT)
        WP = NE + TOPK
        lg = km[0][:, 1, :].rearrange("p (c e) -> p c e", c=NC)
        pv = km[0][:, 2:4, :].rearrange("p a b -> p (a b)")[:, 0:NC * WP].rearrange("p (c e) -> p c e", c=NC)
        rep = km[0][:, 4:6, :].rearrange("p a b -> p (a b)")[:, 0:NC * WP].rearrange("p (c e) -> p c e", c=NC)
        top = km[0][:, 6, 0:NC * 8].rearrange("p (c e) -> p c e", c=NC)
        cwt = km[0][:, 8:10, :].rearrange("p a b -> p (a b)")[:, 0:NT * NC].rearrange("p (e c) -> p e c", c=NC)
        row = km[0][:, 10, 0:NC]
        w13 = [km[1][:, 4 * i:4 * i + 4, :].rearrange("p (w k) h -> p w k h", w=2) for i in range(2)]
        w2 = [km[1][:, 8 + 2 * i:10 + 2 * i, :].rearrange("p a b -> p (a b)") for i in range(2)]
        cwe = [km[0][:, 11 + i, 0:NC] for i in range(2)]
        sg = [cacc[0][:, 512 * i:512 * i + 512] for i in range(2)]
        gT = cacc[1]
        acc2 = kq[0][:, :, :, :].rearrange("p c a b -> p c (a b)")
        fin = kq[1][:, :, :, :].rearrange("p c a b -> p c (a b)")
        BAB, MODB, GATEB = bank[4], bank[5], bank[6]

        block = ctx.enter_context(nc.Block())

        @block.sync
        def _(sp):
            sp.dma_start(xs, x_v).then_inc(flag("x_loaded"), 16)
            sp.dma_start(cst[:, :], consts).then_inc(flag("consts_loaded"), 16)
            sp.dma_start(cT, c_in.rearrange("a (k p) -> p (a k)", p=128), allow_slow_non_contiguous=True).then_inc(flag("c_loaded"), 16)
            sp.dma_start(wmod_sb, wmod.rearrange("(k p) m -> p k m", p=128)).then_inc(flag("wmod_loaded"), 16)
            sp.dma_start(wba_sb, w_ba.rearrange("(k p) m -> p k m", p=128)).then_inc(flag("wba_loaded"), 16)
            sp.dma_start(dtb, bc(dt_bias.unsqueeze(0), [128, NH])).then_inc(flag("gates_loaded"), 16)
            sp.dma_start(alg, bc(a_log.unsqueeze(0), [128, NH])).then_inc(flag("gates_loaded"), 16)
            sp.dma_start(nw[:, :], norm_w.unsqueeze(1)).then_inc(flag("nw_loaded"), 16)

            def weights(n, par):
                m = n if isinstance(n, int) else None
                if m is None:
                    sp.wait_ge(full.sem, full.at(n, F_KT - 2 * FILLS))
                    hold(sp, "sp_held")
                sp.dma_start(wq[par][:, :, :], w_v[:, :, bass.ds(n * PW, PW)]).then_inc(w_in[par].sem, 16)
                if m is None:
                    sp.wait_ge(conv_done.sem, conv_done.at(n, -4))
                    hold(sp, "sp_held")
                sp.dma_start(cw[par][:, 0:1, :], cw_v[:, bass.ds(n + NP, 1), :]).then_inc(cw_in[par].sem, 16)
                sp.dma_start(cw[par][:, 1:2, :], cw_v[:, bass.ds(n, 1), :]).then_inc(cw_in[par].sem, 16)
                sp.dma_start(cw[par][:, 2:4, :], cw_v[:, bass.ds(n * 2 + 2 * NP, 2), :]).then_inc(
                    cw_in[par].sem, 16)
                if m is None:
                    sp.wait_ge(wo_full.sem, wo_full.at(n, -NC))
                    hold(sp, "sp_held")
                sp.dma_start(wo[par][:, :, :], wo_v[:, bass.ds(n * 2, 2), :]).then_inc(wo_in[par].sem, 16)

            def decays(n):
                sp.wait_ge(am_ready.sem, am_ready.at(n, 0))
                hold(sp, "sp_held")
                sp.wait_ge(wl_ready.sem, wl_ready.at(n, 0))
                hold(sp, "sp_held")
                sp.dma_start(lt[:, :, :], bc(al_v[bass.ds(n, 1)], [128, NU, C])).then_inc(al_in.sem, 16)

            weights(0, 0)
            weights(1, 1)
            sp.wait_ge(flag("decays_ready"), 2)
            sp.dma_start(d_alpha.rearrange("h c t -> h (c t)"),
                         alT.rearrange("h c t -> h (c t)")).then_inc(flag("decays_in_dram"), 16)
            sp.dma_start(d_last, last32).then_inc(flag("last_in_dram"), 16)
            sp.wait_ge(flag("last_in_dram"), 16)
            sp.dma_start(lastb, bc(d_last.rearrange("h c -> (h c)").unsqueeze(0), [128, NH * NC])).then_inc(
                flag("last_spread"), 16)
            sp.wait_ge(flag("decays_in_dram"), 16)
            decays(0)
            decays(1)
            with sp.Fori(1, NP // 2) as i:
                for par in range(2):
                    weights(i * 2 + par, par)
                    decays(i * 2 + par)

            sp.wait_ge(acc_done.sem, acc_done.at(NP, 0))
            sp.dma_start(xs, x_v).then_inc(flag("x_loaded"), 16)
            sp.dma_start(wr_sb, w_router.rearrange("(k p) m -> p k m", p=128)).then_inc(flag("wr_loaded"), 16)

            def expert(e, par, w1, w3, w2s, free):
                if free:
                    sp.wait_ge(mfull.sem, mfull.at(e, 4 - 2 * MFILLS))
                    hold(sp, "sp_held")
                sp.dma_start(w13[par][:, 0:1], w1).then_inc(w13_in[par].sem, 16)
                sp.dma_start(w13[par][:, 1:2], w3).then_inc(w13_in[par].sem, 16)
                if free:
                    sp.wait_ge(mfull.sem, mfull.at(e, -MFILLS))
                    hold(sp, "sp_held")
                sp.dma_start(w2[par].unsqueeze(1), w2s).then_inc(w2_in[par].sem, 16)

            e1, e3 = (w.rearrange("e (k p) h -> p e k h", p=128) for w in (we1, we3))
            e2 = we2.rearrange("e h d -> h e d")
            s1, s3 = (w.rearrange("(k p) (s h) -> p s k h", p=128, h=128) for w in (ws1, ws3))
            s2 = ws2.rearrange("(s h) d -> h s d", h=128)

            def routed(e, par, free):
                one = bass.ds(e, 1)
                expert(e, par, e1[:, one], e3[:, one], e2[:, one], free)

            routed(0, 0, False)
            routed(1, 1, False)
            with sp.Fori(1, NE // 2) as i:
                for par in range(2):
                    routed(i * 2 + par, par, True)
            for s in range(NS):
                expert(NE + s, s % 2, s1[:, s:s + 1], s3[:, s:s + 1], s2[:, s:s + 1], True)
            sp.wait_ge(flag("out_ready"), 1)
            sp.dma_start(out_v, fin).then_inc(flag("out_stored"), 16)
            sp.wait_ge(flag("out_stored"), 16)

        PE = nc.tensor

        @block.tensor
        def _(pe):
            def transposed_rows(part, src):
                for k in range(KT):
                    for q in range(2):
                        b = 2 * k + q
                        for c in range(4):
                            last = PE.transpose(bank[b][:, 128 * c:128 * (c + 1)],
                                                src[:, 4 * q + c, 128 * k:128 * (k + 1)], ident)
                        last.then_inc(flag(f"rows_turned{part}"), 1)

            pe.wait_ge(flag("wmod_loaded"), 16)
            pe.wait_ge(flag("silu_c"), 1)
            for j, slot in enumerate((0, 1, 3, 4)):
                for h in range(2):
                    for k in range(KT):
                        at = slot * D + 128 * h
                        last = PE.matmul(MODB[:, 2 * j + h:2 * j + h + 1], wmod_sb[:, k, at:at + 128],
                                         scT[:, k:k + 1], start=(k == 0), stop=(k == KT - 1))
            last.then_inc(flag("mod_columns"), 1)
            pe.wait_ge(flag("silu_c_spread"), 1)
            for j, slot in enumerate((2, 5)):
                for k in range(KT):
                    last = PE.matmul(GATEB[:, D * j:D * (j + 1)], scb[:, k, :],
                                     wmod_sb[:, k, slot * D:(slot + 1) * D], start=(k == 0), stop=(k == KT - 1))
            last.then_inc(flag("gate_rows"), 1)
            pe.wait_ge(flag("consts_loaded"), 16)
            pe.wait_ge(flag("rows_normed0"), NC)
            transposed_rows(0, xs)
            pe.wait_ge(flag("hT_ready0"), 4)
            pe.wait_ge(flag("wba_loaded"), 16)
            for c in range(NC):
                for k in range(KT):
                    last = PE.matmul(BAB[:, 64 * c:64 * (c + 1)], hT[:, k, C * c:C * (c + 1)], wba_sb[:, k, :],
                                     start=(k == 0), stop=(k == KT - 1))
            last.then_inc(flag("gates_projected"), 1)
            pe.wait_ge(flag("alpha_ready"), 1)
            pe.wait_ge(flag("beta_stored"), 1)
            pe.wait_ge(flag("mods_stored"), 1)
            for c in range(NC):
                last = PE.transpose(bank[4 + c // 4][0:NH, 128 * (c % 4):128 * (c % 4 + 1)],
                                    tmp[3][:, NH * c:NH * (c + 1)], ident)
            last.then_inc(flag("alpha_turned"), 1)
            pe.wait_ge(flag("products_ready"), 1)
            for c in range(NC):
                last = PE.transpose(bank[6][:, NH * c:NH * (c + 1)], eT[:, c, :], ident[0:NH, 0:NH])
            last.then_inc(flag("products_turned"), 1)
            pe.wait_ge(flag("tables_ready"), 1)

            def fill(n, par, f):
                ev, k = drained(f - RING) if f >= RING else (vp_done, 0)
                if ev is not inv:
                    pe.wait_ge(ev.sem, ev.at(n, k))
                return ring(f, par)

            def project(n, par, f):
                t, q = (f - F_PROJ) // 2, (f - F_PROJ) % 2
                col = (KCOL, QCOL, VCOL, VCOL + 128)[t]
                b = fill(n, par, f)
                for k in range(KT):
                    last = PE.matmul(b[:, :], wq[par][:, k, col:col + 128], hT[:, k, 512 * q:512 * (q + 1)],
                                     start=(k == 0), stop=(k == KT - 1))
                last.then_inc(full.sem, 1)

            def project_z(n, par, j):
                b = fill(n, par, F_Z + j)
                for c in (2 * j, 2 * j + 1):
                    for k in range(KT):
                        last = PE.matmul(b[:, D * (c % 2):D * (c % 2 + 1)], hT[:, k, C * c:C * (c + 1)],
                                         wq[par][:, k, ZCOL:ZCOL + D], start=(k == 0), stop=(k == KT - 1))
                last.then_inc(full.sem, 1)

            def products(n, par, j):
                b = fill(n, par, F_KK + j)
                for c in (2 * j, 2 * j + 1):
                    last = PE.matmul(b[:, 256 * (c % 2):256 * (c % 2 + 1)], kq[par][:, c, 0, :],
                                     kq[par][:, c, :, :].rearrange("p a b -> p (a b)"), start=True, stop=True)
                last.then_inc(full.sem, 1)

            def front(n, m, par):
                pe.wait_ge(w_in[par].sem, w_in[par].at(m, 16))
                for f in range(F_PROJ, F_NORM):
                    project(n, par, f)
                    if f in (1, 3, 6):
                        yield
                for w in range(2):
                    b = fill(n, par, F_NORM + w)
                    pe.wait_ge(sq_ready.sem, sq_ready.at(n, w + 1))
                    for c in range(NC):
                        last = PE.matmul(b[:, c:c + 1], vT[:, w, C * c:C * (c + 1)], ones, start=True, stop=True)
                    last.then_inc(full.sem, 1)
                products(n, par, 0)
                products(n, par, 1)
                yield
                products(n, par, 2)
                products(n, par, 3)
                yield
                for j in range(4):
                    project_z(n, par, j)
                    yield
                for j in range(2):
                    b = fill(n, par, F_KT + j)
                    for c in range(4):
                        last = PE.transpose(b[:, 128 * c:128 * (c + 1)], kq[par][:, 4 * j + c, 0, :], ident)
                    last.then_inc(full.sem, 1)
                yield
                yield
                yield from invert(n, par)
                yield
                pe.wait_ge(silu_done.sem, silu_done.at(n, 4))
                for j in range(4):
                    b = fill(n, par, F_VT + j)
                    for i in range(4):
                        c, h = 2 * j + i // 2, i % 2
                        last = PE.transpose(b[:, 128 * i:128 * (i + 1)], vT[:, h, C * c:C * (c + 1)], ident)
                    last.then_inc(full.sem, 1)

            def blocks(b, g, lhs, rhs):
                hold(pe, "pe_held")
                for i in range(UG):
                    u = UG * g + i
                    for lo in (0, HB):
                        last = PE.matmul(b[lo:lo + HB, HB * i:HB * (i + 1)], lhs(u, lo), rhs(u, lo),
                                         start=True, stop=True)
                last.then_inc(full.sem, 1)

            def invert(n, par):
                def a_of(u, lo):
                    return am[par][lo:lo + HB, u, 0, lo:lo + HB]

                def of(t):
                    return lambda u, lo: t[lo:lo + HB, u, :]

                pe.wait_ge(inv.sem, inv.at(n, 1))
                for g in range(2):
                    b = fill(n, par, F_X1 + g)
                    blocks(b, g, of(xt), lambda u, lo: cst[lo:lo + HB, C_ID64:C_ID64 + HB])
                yield
                for lvl in range(LEVELS):
                    f0, done = F_LEVEL + 6 * lvl, 1 + 6 * lvl
                    for g in range(2):
                        b = fill(n, par, f0 + g)
                        if lvl == 0:
                            pe.wait_ge(x1_copied.sem, x1_copied.at(n, g + 1))
                        else:
                            pe.wait_ge(inv.sem, inv.at(n, done - 6 + (4, 6)[g]))
                        blocks(b, g, a_of, of(xc))
                    yield
                    for g in range(2):
                        pe.wait_ge(inv.sem, inv.at(n, done + 1 + g))
                        b = fill(n, par, f0 + 2 + 2 * g)
                        blocks(b, g, of(yc), of(xt))
                        b = fill(n, par, f0 + 3 + 2 * g)
                        blocks(b, g, of(xt), of(yc))
                        yield
                for g in range(2):
                    b = fill(n, par, F_LAST + g)
                    pe.wait_ge(inv.sem, inv.at(n, 1 + 6 * LEVELS - 6 + (4, 6)[g]))
                    hold(pe, "pe_held")
                    for i in range(UG):
                        u = UG * g + i
                        last = PE.matmul(b[HB:C, HB * i:HB * (i + 1)], am[par][0:HB, u, 0, HB:C], xc[0:HB, u, :],
                                         start=True, stop=True)
                    last.then_inc(full.sem, 1)
                yield
                for g in range(2):
                    b = fill(n, par, F_LAST + 2 + g)
                    pe.wait_ge(last_copied.sem, last_copied.at(n, g + 1))
                    hold(pe, "pe_held")
                    for i in range(UG):
                        u = UG * g + i
                        last = PE.matmul(b[0:HB, HB * i:HB * (i + 1)], yc[HB:C, u, :], xf[par][HB:C, u, HB:C],
                                         start=True, stop=True)
                    last.then_inc(full.sem, 1)

            def turn_out(n, c):
                pe.wait_ge(o3_ready.sem, o3_ready.at(n, c + 1))
                pe.wait_ge(acc_done.sem, acc_done.at(n, c))
                for h in range(2):
                    last = PE.transpose(OGB[:, 128 * h:128 * (h + 1)], o2[c % 2][:, h, :], ident)
                last.then_inc(og_full.sem, 1)

            def project_out(n, par, c):
                pe.wait_ge(ogt_ready.sem, ogt_ready.at(n, c + 1))
                pe.wait_ge(won_ready.sem, won_ready.at(n, 1))
                for h in range(2):
                    last = PE.matmul(OGB[:, 256:512], ogt[:, h, :], wo[par][:, h, :], start=(h == 0), stop=(h == 1))
                last.then_inc(wo_full.sem, 1)

            def scan(n, par, between):
                state = st[:, :, :].rearrange("p a b -> p (a b)")
                pe.wait_ge(km_done.sem, km_done.at(n, 2))
                pe.wait_ge(vp_done.sem, vp_done.at(n, 4))
                pe.wait_ge(last_copied.sem, last_copied.at(n, 4))
                for c in range(NC):
                    if c:
                        pe.wait_ge(st_ready.sem, st_ready.at(n, c))
                        PE.matmul(KSB[:, 0:256], kq[par][:, c, 0, :], state, start=True, stop=True).then_inc(
                            ks_full.sem, 1)
                        pe.wait_ge(o1_ready.sem, o1_ready.at(n, c))
                        PE.matmul(QSB[:, 0:256], kq[par][:, c, 1, :], state, start=True, stop=True).then_inc(
                            qs_full.sem, 1)
                    if c >= 3:
                        project_out(n, par, c - 3)
                    between()
                    if c:
                        pe.wait_ge(r_ready.sem, r_ready.at(n, c))
                    pe.wait_ge(u_ready.sem, u_ready.at(n, c))
                    for h in range(2):
                        last = PE.matmul(XRB[:, 128 * h:128 * (h + 1)], xf[par][:, NC * h + c, :],
                                         rr[:, h, :] if c else vp[par][:, c, h, :], start=True, stop=True)
                    last.then_inc(xr_full.sem, 1)
                    between()
                    pe.wait_ge(u_ready.sem, u_ready.at(n, c + 1))
                    if c < NC - 1:
                        if c == 0:
                            pe.wait_ge(st_ready.sem, st_ready.at(n, 0))
                        for h in range(2):
                            last = PE.matmul(KSB[:, 256 + 128 * h:256 + 128 * (h + 1)], km[par][:, NC * h + c, :],
                                             uu[:, h, :], start=True, stop=True)
                        last.then_inc(ku_full.sem, 1)
                    if c:
                        pe.wait_ge(qse_ready.sem, qse_ready.at(n, c))
                    else:
                        pe.wait_ge(o1_ready.sem, o1_ready.at(n, 0))
                    for h in range(2):
                        last = PE.matmul(QSB[:, 256 + 128 * h:256 + 128 * (h + 1)], am[par][:, NC * h + c, 1, :],
                                         uu[:, h, :], start=True, stop=True)
                    last.then_inc(pu_full.sem, 1)
                    if c >= 2:
                        turn_out(n, c - 2)
                    between()
                for c in range(NC - 3, NC):
                    project_out(n, par, c)
                    if c < NC - 1:
                        turn_out(n, c + 1)
                    if c == NC - 3:
                        between()

            pairs(pe, front, scan)

            pe.wait_ge(flag("rows_normed1"), NC)
            transposed_rows(1, xs)
            pe.wait_ge(flag("hT_ready1"), 4)
            pe.wait_ge(flag("wr_loaded"), 16)
            for c in range(NC):
                for k in range(KT):
                    last = PE.matmul(bank[4][:, NE * c:NE * (c + 1)], hT[:, k, C * c:C * (c + 1)], wr_sb[:, k, :],
                                     start=(k == 0), stop=(k == KT - 1))
            last.then_inc(flag("logits_full"), 1)
            pe.wait_ge(flag("router_done"), 1)

            def hidden_tile(e, m, par):
                pe.wait_ge(w13_in[par].sem, w13_in[par].at(m, 32))
                pe.wait_ge(g_ready.sem, g_ready.at(e, 0))
                for q in range(2):
                    for w in range(2):
                        for k in range(KT):
                            last = PE.matmul(bank[2 * q + w][:, :], w13[par][:, w, k, :],
                                             hT[:, k, 512 * q:512 * (q + 1)], start=(k == 0), stop=(k == KT - 1))
                        last.then_inc(mfull.sem, 1)
                pe.wait_ge(w2_in[par].sem, w2_in[par].at(m, 16))
                pe.wait_ge(down_done.sem, down_done.at(e, 0))
                for j in range(4):
                    pe.wait_ge(g_ready.sem, g_ready.at(e, 1 + j // 2))
                    for i in range(2):
                        c = 2 * j + i
                        last = PE.matmul(bank[4 + j][:, D * i:D * (i + 1)], gT[:, C * c:C * (c + 1)], w2[par],
                                         start=True, stop=True)
                    last.then_inc(mfull.sem, 1)

            with pe.Fori(0, NT // 2) as i:
                for par in range(2):
                    hidden_tile(i * 2 + par, i, par)

        @block.scalar
        def _(act):
            act.wait_ge(flag("c_loaded"), 16)
            nc.scalar.activation(scT, cT, ACT.Silu).then_inc(flag("silu_c"), 1)

            def to_hT(part):
                act.wait_ge(flag("mods_stored"), 1)
                for k in range(KT):
                    for q in range(2):
                        act.wait_ge(flag(f"rows_turned{part}"), 2 * k + q + 1)
                        nc.scalar.activation(hT[:, k, 512 * q:512 * (q + 1)], bank[2 * k + q][:, :], ACT.Identity,
                                             bias=modc[:, 4 * part + k:4 * part + k + 1],
                                             scale=modc[:, 4 * part + 2 + k:4 * part + 3 + k]).then_inc(
                                                 flag(f"hT_ready{part}"), 1)

            to_hT(0)
            act.wait_ge(flag("neg_abs_ready"), 1)
            nc.scalar.activation(tmp[2], tmp[1], ACT.Exp).then_inc(flag("exp_ready"), 1)
            act.wait_ge(flag("gates_loaded"), 32)
            nc.scalar.activation(tmp[6][:, 0:NH], alg, ACT.Exp).then_inc(flag("exp_ready"), 1)
            act.wait_ge(flag("b_copied"), 1)
            nc.scalar.activation(tmp[7], tmp[5], ACT.Exp, scale=-1.0).then_inc(flag("exp_ready"), 1)
            act.wait_ge(flag("g_ready"), 1)
            nc.scalar.activation(tmp[3], tmp[4], ACT.Exp, scale=-1.0).then_inc(flag("alpha_ready"), 1)

            def copy_projection(n, par, f):
                t, q = (f - F_PROJ) // 2, (f - F_PROJ) % 2
                if q == 0:
                    act.wait_ge(conv_done.sem, conv_done.at(n, max(t - 1, 0)))
                act.wait_ge(full.sem, full.at(n, f + 1))
                nc.scalar.activation(xpad[t % 2][:, 3 + 512 * q:3 + 512 * (q + 1)], ring(f, par)[:, :],
                                     ACT.Copy).then_inc(x_copied.sem, 1)

            def silu(n, par, t):
                act.wait_ge(conv_done.sem, conv_done.at(n, t + 1))
                dst = kq[par][:, :, t, :] if t < 2 else vT[:, t - 2, :]
                src = cacc[t % 2][:, :]
                nc.scalar.activation(dst, src.rearrange("p (c t) -> p c t", c=NC) if t < 2 else src,
                                     ACT.Silu).then_inc(silu_done.sem, 1)

            def silu_z(n, par, j):
                act.wait_ge(full.sem, full.at(n, F_Z + j + 1))
                nc.scalar.activation(sz[par][:, 2 * j:2 * j + 2, :].rearrange("p a b -> p (a b)"),
                                     ring(F_Z + j, par)[:, :], ACT.Silu).then_inc(z_ready.sem, 1)

            def front(n, m, par):
                copy_projection(n, par, 0)
                copy_projection(n, par, 1)
                yield
                copy_projection(n, par, 2)
                copy_projection(n, par, 3)
                yield
                silu(n, par, 0)
                copy_projection(n, par, 4)
                copy_projection(n, par, 5)
                silu(n, par, 1)
                copy_projection(n, par, 6)
                yield
                copy_projection(n, par, 7)
                yield
                yield
                for j in range(4):
                    silu_z(n, par, j)
                    yield
                yield
                yield
                for g in range(2):
                    act.wait_ge(full.sem, full.at(n, F_X1 + g + 1))
                    nc.scalar.activation(xc[:, UG * g:UG * (g + 1), :].rearrange("p a b -> p (a b)"),
                                         ring(F_X1 + g, par)[:, :], ACT.Copy).then_inc(x1_copied.sem, 1)
                yield
                act.wait_ge(full.sem, full.at(n, F_KK))
                for k in range(3 * LEVELS):
                    if k == 3 * LEVELS - 2:
                        silu(n, par, 2)
                    yield
                for g in range(2):
                    act.wait_ge(full.sem, full.at(n, F_LAST + g + 1))
                    nc.scalar.activation(yc[HB:C, UG * g:UG * (g + 1), :].rearrange("p a b -> p (a b)"),
                                         ring(F_LAST + g, par)[HB:C, :], ACT.Copy, scale=-1.0).then_inc(
                                             last_copied.sem, 1)
                yield
                for g in range(2):
                    act.wait_ge(full.sem, full.at(n, F_LAST + g + 3))
                    nc.scalar.activation(
                        xf[par][0:HB, UG * g:UG * (g + 1), HB:C],
                        ring(F_LAST + 2 + g, par)[0:HB, :].rearrange("p (u c) -> p u c", u=UG),
                        ACT.Copy).then_inc(last_copied.sem, 1)
                yield
                silu(n, par, 3)
                yield
                act.wait_ge(rs_ready.sem, rs_ready.at(n, 2))
                for j in range(4):
                    act.wait_ge(full.sem, full.at(n, F_VT + j + 1))
                    for i in range(2):
                        c = 2 * j + i
                        last = nc.scalar.activation(
                            vp[par][:, c, :, :].rearrange("p a b -> p (a b)"),
                            ring(F_VT + j, par)[:, 256 * i:256 * (i + 1)], ACT.Copy, scale=nk[par][:, 3, c:c + 1])
                    last.then_inc(vp_done.sem, 1)

            def copy_out(n, c):
                act.wait_ge(og_full.sem, og_full.at(n, c + 1))
                nc.scalar.activation(ogt[:, :, :].rearrange("p a b -> p (a b)"), OGB[:, 0:256],
                                     ACT.Copy).then_inc(ogt_ready.sem, 1)

            def square_sums(n, par, c):
                act.wait_ge(o2_ready.sem, o2_ready.at(n, c + 1))
                act.wait_ge(ss_ready.sem, ss_ready.at(n, 2 * c))
                for h in range(2):
                    nc.scalar.activation(junk[:, h, :], o2[c % 2][:, h, :], ACT.Square, scale=nk[par][:, 4, c:c + 1],
                                         accum_out=ss[:, c % 2, 0, h:h + 1]).then_inc(ss_ready.sem, 1)

            def scan(n, par, between):
                for c in range(NC):
                    if c:
                        act.wait_ge(qs_full.sem, qs_full.at(n, c))
                        for h in range(2):
                            last = nc.scalar.activation(qse[:, h, :], QSB[:, 128 * h:128 * (h + 1)], ACT.Copy,
                                                        scale=sc[par][:, 0, h, c:c + 1])
                        last.then_inc(qse_ready.sem, 1)
                    between()
                    act.wait_ge(xr_full.sem, xr_full.at(n, c + 1))
                    nc.scalar.activation(uu[:, :, :].rearrange("p a b -> p (a b)"), XRB[:, 0:256],
                                         ACT.Copy).then_inc(u_ready.sem, 1)
                    if c:
                        square_sums(n, par, c - 1)
                    between()
                    if c >= 2:
                        copy_out(n, c - 2)
                    between()
                square_sums(n, par, NC - 1)
                copy_out(n, NC - 2)
                between()
                copy_out(n, NC - 1)

            act.wait_ge(flag("tables_ready"), 1)
            nc.scalar.activation(sm[:, 4:6], sm[:, 2:4], ACT.Silu)
            pairs(act, front, scan)

            to_hT(1)
            act.wait_ge(flag("logits_shifted"), 1)
            nc.scalar.activation(pv[:, :, 0:NE], lg, ACT.Exp).then_inc(flag("exp_logits"), 1)
            with act.Fori(0, NT // 2) as i:
                for par in range(2):
                    e = i * 2 + par
                    for q in range(2):
                        act.wait_ge(mfull.sem, mfull.at(e, 2 * q + 1))
                        act.wait_ge(g_ready.sem, g_ready.at(e, 0))
                        nc.scalar.activation(sg[q], bank[2 * q][:, :], ACT.Silu).then_inc(sg_ready.sem, 1)

        V = nc.vector

        @block.vector
        def _(dve):
            def then(ins):
                link(dve, "dve_step", ins)

            def norm_rows(part, src):
                for c in range(NC):
                    last = V.bn_stats(stat[:, c, :], src[:, c, :])
                then(last)
                for c in range(NC):
                    last = V.bn_aggr(mv[:, c, :], stat[:, c, :])
                last.then_inc(flag(f"variances{part}"), 1)
                dve.wait_ge(flag(f"variances{part}"), 1)
                dve.wait_ge(flag(f"rstd{part}"), 1)
                for c in range(NC):
                    V.tensor_scalar(xs[:, c, :], src[:, c, :], mv[:, c, 0:1], rstd[:, c:c + 1], ALU.subtract,
                                    ALU.mult).then_inc(flag(f"rows_normed{part}"), 1)

            V.memset(half[:, 0, :], 0.5)
            V.memset(half[:, 1, :], -0.5)
            V.memset(nhalf, -0.5)
            for i in range(2):
                V.memset(xpad[i][:, 0:3], 0.0)
            for i in range(2):
                last = V.memset(xf[i][HB:C, :, 0:HB], 0.0)
            last = V.memset(zero32, 0.0)
            then(last)
            V.tensor_copy(half[:, 0, 0:1], half[:, 0, 1:2]).then_inc(flag("exponents_ready"), 1)
            dve.wait_ge(flag("silu_c"), 1)
            V.tensor_copy(scb, bc(scT.unsqueeze(2), [128, KT, 128])).then_inc(flag("silu_c_spread"), 1)
            dve.wait_ge(flag("x_loaded"), 16)
            norm_rows(0, xs)
            dve.wait_ge(flag("mod_columns"), 1)
            mb = MODB[:, 0:8].rearrange("p (a b) -> p a b", a=4)
            mc = modc[:, :].rearrange("p (a b) -> p a b", a=4)
            V.tensor_copy(mc[:, 0:4:2, :], mb[:, 0:4:2, :])
            V.tensor_scalar(mc[:, 1:4:2, :], mb[:, 1:4:2, :], 1.0, None, ALU.add)
            dve.wait_ge(flag("gate_rows"), 1)
            g_all = gate[:, :, :].rearrange("p a b -> p (a b)")
            sign = lt[:, 0:4, :].rearrange("p a b -> p (a b)")
            mag = lt[:, 4:8, :].rearrange("p a b -> p (a b)")
            V.tensor_scalar(sign, GATEB[:, :], 0.0, 2.0, ALU.is_ge, ALU.mult)
            then(V.tensor_scalar(mag, GATEB[:, :], -1.0, None, ALU.mult))
            then(V.tensor_tensor(mag, GATEB[:, :], mag, ALU.max))
            then(V.tensor_scalar(mag, mag, 0.25, None, ALU.max))
            V.scalar_tensor_tensor(out=g_all, in0=sign, scalar=-1.0, in1=mag, op0=ALU.add,
                                   op1=ALU.mult).then_inc(flag("mods_stored"), 1)
            dve.wait_ge(flag("gates_projected"), 1)
            dve.wait_ge(flag("gates_loaded"), 32)
            ba = BAB[:, :].rearrange("p (c g k r) -> p c g k r", c=NC, g=NP, k=2)

            def by_head(t):
                return t.rearrange("p (c g r) -> p c g r", c=NC, g=NP)

            aa, neg, y, al, gg, bb = tmp[0], tmp[1], tmp[2], tmp[3], tmp[4], tmp[5]
            then(V.tensor_copy(by_head(aa), ba[:, :, :, 1, :]))
            then(V.tensor_tensor(aa.rearrange("p (c h) -> p c h", c=NC), aa.rearrange("p (c h) -> p c h", c=NC),
                                 bc(dtb.unsqueeze(1), [128, NC, NH]), ALU.add))
            then(V.tensor_scalar(neg, aa, -1.0, None, ALU.mult))
            then(V.tensor_tensor(neg, aa, neg, ALU.min))
            then(V.tensor_scalar(neg, neg, 1.0, None, ALU.mult))
            V.tensor_copy(gg, neg).then_inc(flag("neg_abs_ready"), 1)
            V.tensor_copy(by_head(bb), ba[:, :, :, 0, :]).then_inc(flag("b_copied"), 1)
            dve.wait_ge(flag("exp_ready"), 3)
            den, s2 = tmp[1], tmp[4]
            then(V.tensor_scalar(den, y, 2.0, None, ALU.add))
            then(V.reciprocal(den, den))
            then(V.tensor_tensor(y, y, den, ALU.mult))
            then(V.tensor_tensor(s2, y, y, ALU.mult))
            then(V.tensor_scalar(den, s2, 1.0 / 19, None, ALU.mult))
            for k in range(8, 0, -1):
                then(V.scalar_tensor_tensor(out=den, in0=den, scalar=1.0 / (2 * k + 1), in1=s2, op0=ALU.add,
                                            op1=ALU.mult))
            then(V.scalar_tensor_tensor(out=den, in0=den, scalar=1.0, in1=y, op0=ALU.add, op1=ALU.mult))
            then(V.tensor_scalar(aa, aa, 0.0, None, ALU.max))
            then(V.scalar_tensor_tensor(out=aa, in0=den, scalar=2.0, in1=aa, op0=ALU.mult, op1=ALU.add))
            V.tensor_tensor(gg.rearrange("p (c h) -> p c h", c=NC), aa.rearrange("p (c h) -> p c h", c=NC),
                            bc(tmp[6][:, 0:NH].unsqueeze(1), [128, NC, NH]), ALU.mult).then_inc(flag("g_ready"), 1)
            then(V.tensor_scalar(bb, tmp[7], 1.0, None, ALU.add))
            then(V.reciprocal(bb, bb))

            def table(kind):
                return tab[:, :, kind, :, :]

            def heads_first(t):
                return t.rearrange("p (c g r) -> p g r c", c=NC, g=NP)

            for r in range(2):
                last = V.tensor_copy(table(2)[:, :, r, :], heads_first(bb)[:, :, r, :])
            last.then_inc(flag("beta_stored"), 1)
            dve.wait_ge(flag("alpha_turned"), 1)
            for q in range(2):
                last = V.tensor_copy(alT[:, 4 * q:4 * q + 4, :].rearrange("p a b -> p (a b)"), bank[4 + q][0:NH, :])
            last.then_inc(flag("decays_ready"), 1)
            dve.wait_ge(flag("decays_ready"), 1)
            for c in range(NC):
                last = V.tensor_tensor_scan(eT[:, c, :], alT[:, c, :], zero32, 1.0, ALU.mult, ALU.add)
            last.then_inc(flag("products_ready"), 1)
            dve.wait_ge(flag("products_ready"), 1)
            V.tensor_copy(last32, eT[:, :, C - 1]).then_inc(flag("decays_ready"), 1)
            dve.wait_ge(flag("products_turned"), 1)
            eb = heads_first(bank[6][:, 0:NC * NH])
            for r in range(2):
                V.tensor_scalar(table(0)[:, :, r, :], eb[:, :, r, :], -1.0, None, ALU.mult)
            dve.wait_ge(flag("last_spread"), 16)
            V.tensor_copy(table(1), lastb.rearrange("p (g r c) -> p g r c", g=NP, r=2)).then_inc(
                flag("tables_ready"), 1)
            dve.wait_ge(flag("tables_ready"), 1)
            dve.wait_ge(flag("consts_loaded"), 16)

            def conv(n, m, par, t):
                dve.wait_ge(x_copied.sem, x_copied.at(n, 2 * t + 2))
                dve.wait_ge(silu_done.sem, silu_done.at(n, max(t - 1, 0)))
                if t == 0:
                    dve.wait_ge(cw_in[par].sem, cw_in[par].at(m, 48))
                a, src = cacc[t % 2][:, :], xpad[t % 2]
                V.tensor_scalar(a, src[:, 0:T], cw[par][:, t, 0:1], None, ALU.mult).then_inc(tap.sem, 1)
                for j in range(1, 4):
                    if j > 1 or t < 2:
                        yield
                    dve.wait_ge(tap.sem, tap.at(n, 3 * t + j))
                    V.scalar_tensor_tensor(out=a, in0=src[:, j:j + T], scalar=cw[par][:, t, j:j + 1], in1=a,
                                           op0=ALU.mult, op1=ALU.add).then_inc((tap if j < 3 else conv_done).sem, 1)

            def front(n, m, par):
                V.tensor_copy(sc[par][:, :, :, :].rearrange("p k r c -> p (k r c)"),
                              tab[:, bass.ds(n, 1), :, :, :].rearrange("p g k r c -> p (g k r c)")).then_inc(
                                  sc_ready.sem, 1)
                dve.wait_ge(al_in.sem, al_in.at(n, 16))
                for u in range(NU):
                    last = V.tensor_tensor_scan(lt[:, u, :], lt[:, u, :], ident, 0.0, ALU.mult, ALU.add)
                last.then_inc(lt_ready.sem, 1)
                yield
                for t in range(2):
                    for _ in conv(n, m, par, t):
                        pass
                    yield
                yield
                dve.wait_ge(full.sem, full.at(n, F_NORM + 1))
                V.tensor_scalar(nk[par][:, 0, :], ring(F_NORM, par)[:, 0:NC], 1e-6, None, ALU.add).then_inc(
                    nk_ready.sem, 1)
                dve.wait_ge(full.sem, full.at(n, F_NORM + 2))
                V.tensor_scalar(nk[par][:, 1, :], ring(F_NORM + 1, par)[:, 0:NC], 1e-6, float(C), ALU.add,
                                ALU.mult).then_inc(nk_ready.sem, 1)
                dve.wait_ge(nk_ready.sem, nk_ready.at(n, 1))
                V.reciprocal(nk[par][:, 2, :], nk[par][:, 0, :]).then_inc(s_ready.sem, 1)
                dve.wait_ge(s_ready.sem, s_ready.at(n, 1))
                dve.wait_ge(sc_ready.sem, sc_ready.at(n, 1))
                V.tensor_tensor(sj[:, :, :], sc[par][:, 2, :, :], bc(nk[par][:, 2:3, :], [128, 2, NC]),
                                ALU.mult).then_inc(s_ready.sem, 1)
                dve.wait_ge(s_ready.sem, s_ready.at(n, 2))
                dve.wait_ge(lt_ready.sem, lt_ready.at(n, 1))
                for j in range(4):
                    dve.wait_ge(full.sem, full.at(n, F_KK + j + 1))
                    for i in range(4):
                        c, h = 2 * j + i // 2, i % 2
                        u = NC * h + c
                        last = V.scalar_tensor_tensor(
                            out=am[par][:, u, :, :],
                            in0=ring(F_KK + j, par)[:, 256 * (c % 2):256 * (c % 2 + 1)].rearrange(
                                "p (a b) -> p a b", a=2),
                            scalar=sj[:, h, c:c + 1], in1=bc(lt[:, u:u + 1, :], [128, 2, C]),
                            op0=ALU.mult, op1=ALU.mult)
                    last.then_inc(am_ready.sem, 1)
                    if j == 1:
                        yield
                yield from invert(n, m, par)

            def scale_keys(n, par):
                V.tensor_tensor(wl[:, :, :], sj[:, :, :],
                                lt[:, :, C - 1].rearrange("p (h c) -> p h c", h=2), ALU.mult).then_inc(wl_ready.sem, 1)
                dve.wait_ge(wl_ready.sem, wl_ready.at(n, 1))
                for j in range(2):
                    dve.wait_ge(full.sem, full.at(n, F_KT + j + 1))
                    for h in range(2):
                        last = V.tensor_tensor(
                            km[par][:, NC * h + 4 * j:NC * h + 4 * j + 4, :],
                            ring(F_KT + j, par)[:, :].rearrange("p (c d) -> p c d", c=4),
                            bc(wl[:, h, 4 * j:4 * j + 4].unsqueeze(2), [128, 4, C]), ALU.mult)
                    last.then_inc(km_done.sem, 1)

            def invert(n, m, par):
                nb, row_i, prod = yc[:, :, 0:2 * BB], yc[:, :, 2 * BB:3 * BB], yc[:, :, 3 * BB:4 * BB]
                z, n16 = xc[:, :, 0:BB], xc[:, :, BB:2 * BB]
                dve.wait_ge(am_ready.sem, am_ready.at(n, 4))
                for lo in range(0, 128, 2 * BB):
                    hi = lo + 2 * BB
                    V.tensor_tensor(nb[lo:hi], am[par][lo:hi, :, 0, lo:hi],
                                    bc(cst[lo:hi, C_BASE:C_BASE + 2 * BB].unsqueeze(1), [2 * BB, NU, 2 * BB]),
                                    ALU.mult).then_inc(base.sem, 1)
                V.tensor_copy(z, bc(cst[:, C_ID16:C_ID16 + BB].unsqueeze(1), [128, NU, BB])).then_inc(base.sem, 1)
                dve.wait_ge(base.sem, base.at(n, 5))
                V.tensor_tensor(n16, nb[:, :, 0:BB], nb[:, :, BB:2 * BB], ALU.add).then_inc(base.sem, 1)
                yield
                for k, i in enumerate(range(BB - 1, 0, -1)):
                    w = BB - i
                    dve.wait_ge(base.sem, base.at(n, 6 + 3 * k))
                    hold(dve, "dve_held")
                    V.stream_shuffle(row_i[:, :, 0:w], z[:, :, i:BB],
                                     [BB * (p // BB) + i for p in range(2 * BB)]).then_inc(base.sem, 1)
                    dve.wait_ge(base.sem, base.at(n, 7 + 3 * k))
                    V.tensor_tensor(prod[:, :, 0:w], row_i[:, :, 0:w], bc(n16[:, :, i:i + 1], [128, NU, w]),
                                    ALU.mult).then_inc(base.sem, 1)
                    dve.wait_ge(base.sem, base.at(n, 8 + 3 * k))
                    V.tensor_tensor(z[:, :, i:BB], z[:, :, i:BB], prod[:, :, 0:w], ALU.add).then_inc(base.sem, 1)
                    if k in (2, 5, 8, 10, 12):
                        yield
                dve.wait_ge(base.sem, base.at(n, 6 + 3 * (BB - 1)))
                V.tensor_tensor(xt[:, :, :].rearrange("p u (b c) -> p u b c", c=BB),
                                bc(z.unsqueeze(2), [128, NU, HB // BB, BB]),
                                bc(cst[:, C_PLACE:C_PLACE + HB].rearrange("p (b c) -> p b c", c=BB).unsqueeze(1),
                                   [128, NU, HB // BB, BB]), ALU.mult).then_inc(inv.sem, 1)
                yield
                scale_keys(n, par)
                taps = (_ for t in (2, 3) for _ in conv(n, m, par, t))
                next(taps, None)
                yield
                for lvl in range(LEVELS):
                    f0 = F_LEVEL + 6 * lvl

                    def filled(k):
                        return ring(f0 + k, par)[:, :].rearrange("p (u c) -> p u c", u=UG)

                    for g in range(2):
                        dve.wait_ge(full.sem, full.at(n, f0 + g + 1))
                        V.tensor_tensor(yc[:, UG * g:UG * (g + 1), :], filled(g), mask(0, 128, lvl, UG),
                                        ALU.mult).then_inc(inv.sem, 1)
                    next(taps, None)
                    yield
                    for g in range(2):
                        us = slice(UG * g, UG * (g + 1))
                        dve.wait_ge(full.sem, full.at(n, f0 + 4 + 2 * g))
                        if lvl < LEVELS - 1:
                            last = V.tensor_tensor(xt[:, us, :], filled(2 + 2 * g), xt[:, us, :], ALU.add)
                        else:
                            for lo in (0, HB):
                                last = V.tensor_tensor(xf[par][lo:lo + HB, us, lo:lo + HB],
                                                       filled(2 + 2 * g)[lo:lo + HB], xt[lo:lo + HB, us, :], ALU.add)
                        last.then_inc(inv.sem, 1)
                        V.tensor_tensor(xc[:, us, :], filled(3 + 2 * g), xc[:, us, :], ALU.add).then_inc(inv.sem, 1)
                        next(taps, None)
                        yield
                for _ in taps:
                    pass

            def add_out(n, c):
                dve.wait_ge(wo_full.sem, wo_full.at(n, c + 1))
                V.tensor_tensor(acc[:, c, :], OGB[:, 256:512], acc[:, c, :], ALU.add).then_inc(acc_done.sem, 1)

            def scan(n, par, between):
                between()
                for c in range(NC):
                    if c:
                        dve.wait_ge(ks_full.sem, ks_full.at(n, c))
                        if c == 1:
                            dve.wait_ge(vp_done.sem, vp_done.at(n, 4))
                        for h in range(2):
                            last = V.scalar_tensor_tensor(out=rr[:, h, :], in0=KSB[:, 128 * h:128 * (h + 1)],
                                                          scalar=sc[par][:, 0, h, c:c + 1], in1=vp[par][:, c, h, :],
                                                          op0=ALU.mult, op1=ALU.add)
                        last.then_inc(r_ready.sem, 1)
                    if c >= 3:
                        add_out(n, c - 3)
                    between()
                    between()
                    if c < NC - 1:
                        dve.wait_ge(ku_full.sem, ku_full.at(n, c + 1))
                        for h in range(2):
                            ku = KSB[:, 256 + 128 * h:256 + 128 * (h + 1)]
                            if c == 0:
                                last = V.tensor_copy(st[:, h, :], ku)
                            else:
                                last = V.scalar_tensor_tensor(out=st[:, h, :], in0=st[:, h, :],
                                                              scalar=sc[par][:, 1, h, c:c + 1], in1=ku,
                                                              op0=ALU.mult, op1=ALU.add)
                        last.then_inc(st_ready.sem, 1)
                    dve.wait_ge(pu_full.sem, pu_full.at(n, c + 1))
                    dve.wait_ge(o2_ready.sem, o2_ready.at(n, max(c - 1, 0)))
                    pu = QSB[:, 256:512].rearrange("p (a b) -> p a b", a=2)
                    if c == 0:
                        last = V.tensor_copy(o1[0][:, :, :], pu)
                    else:
                        dve.wait_ge(qse_ready.sem, qse_ready.at(n, c))
                        last = V.tensor_tensor(o1[c % 2][:, :, :], pu, qse[:, :, :], ALU.subtract)
                    last.then_inc(o1_ready.sem, 1)
                    between()
                for c in range(NC - 3, NC):
                    add_out(n, c)

            dve.wait_ge(flag("acc_cleared"), 1)
            pairs(dve, front, scan)

            dve.wait_ge(flag("x_loaded"), 32)
            dve.wait_ge(acc_done.sem, acc_done.at(NP, 0))
            then(V.tensor_tensor(acc[:, :, :], acc[:, :, :], bc(gate[:, 0:1, :], [128, NC, D]), ALU.mult))
            then(V.tensor_tensor(acc[:, :, :], acc[:, :, :], xs, ALU.add))
            norm_rows(1, acc)
            dve.wait_ge(flag("logits_full"), 1)
            lb = bank[4][:, 0:NC * NE].rearrange("p (c e) -> p c e", c=NC)
            then(V.tensor_reduce(row, lb, AX.X, ALU.max))
            V.tensor_tensor(lg, lb, bc(row.unsqueeze(2), [128, NC, NE]), ALU.subtract).then_inc(
                flag("logits_shifted"), 1)
            dve.wait_ge(flag("exp_logits"), 1)
            then(V.tensor_reduce(row, pv[:, :, 0:NE], AX.X, ALU.add))
            then(V.reciprocal(row, row))
            then(V.tensor_tensor(pv[:, :, 0:NE], pv[:, :, 0:NE], bc(row.unsqueeze(2), [128, NC, NE]), ALU.mult))
            for c in range(NC):
                last = V.max(top[:, c, :], pv[:, c, 0:NE])
            then(last)
            V.memset(pv[:, :, NE:WP], -1.0)
            then(V.memset(top[:, :, TOPK:8], -1.0))
            for c in range(NC):
                last = V.match_replace(rep[:, c, :], top[:, c, :], pv[:, c, :], -2.0)
            then(last)
            then(V.scalar_tensor_tensor(out=lg, in0=rep[:, :, 0:NE], scalar=-1.5, in1=pv[:, :, 0:NE], op0=ALU.is_lt,
                                        op1=ALU.mult))
            then(V.tensor_reduce(row, lg, AX.X, ALU.add))
            then(V.reciprocal(row, row))
            then(V.tensor_scalar(row, row, TOPK / (TOPK + 1.0), None, ALU.mult))
            V.tensor_tensor(cwt[:, 0:NE, :].rearrange("p e c -> p c e"), lg, bc(row.unsqueeze(2), [128, NC, NE]),
                            ALU.mult)
            V.memset(cwt[:, NE:NT, :], 1.0 / (TOPK + 1.0)).then_inc(flag("router_done"), 1)
            dve.wait_ge(flag("router_done"), 1)
            dve.wait_ge(flag("acc2_cleared"), 1)

            with dve.Fori(0, NT // 2) as i:
                for par in range(2):
                    e = i * 2 + par
                    V.tensor_copy(cwe[par], cwt[:, bass.ds(e, 1), :].rearrange("p a c -> p (a c)")).then_inc(
                        cwe_ready.sem, 1)
                    for q in range(2):
                        dve.wait_ge(mfull.sem, mfull.at(e, 2 * q + 2))
                        dve.wait_ge(sg_ready.sem, sg_ready.at(e, q + 1))
                        V.tensor_tensor(gT[:, 512 * q:512 * (q + 1)], bank[2 * q + 1][:, :], sg[q],
                                        ALU.mult).then_inc(g_ready.sem, 1)
                    dve.wait_ge(cwe_ready.sem, cwe_ready.at(e, 1))
                    dve.wait_ge(down_done.sem, down_done.at(e, 0))
                    for c in range(NC):
                        dve.wait_ge(mfull.sem, mfull.at(e, 4 + c // 2 + 1))
                        V.scalar_tensor_tensor(out=acc2[:, c, :], in0=bank[4 + c // 2][:, D * (c % 2):D * (c % 2 + 1)],
                                               scalar=cwe[par][:, c:c + 1], in1=acc2[:, c, :], op0=ALU.mult,
                                               op1=ALU.add).then_inc(down_done.sem, 1)
            dve.wait_ge(down_done.sem, down_done.at(NT, 0))
            then(V.tensor_tensor(acc2, acc2, bc(gate[:, 1:2, :], [128, NC, D]), ALU.mult))
            V.tensor_tensor(fin, acc2, acc[:, :, :], ALU.add).then_inc(flag("out_ready"), 1)

        @block.gpsimd
        def _(pool):
            P = nc.gpsimd
            for r in rounds:
                pool.sem_inc(r.sem, 1)
            P.memset(acc[:, :, :], 0.0).then_inc(flag("acc_cleared"), 1)

            def rstds(part):
                pool.wait_ge(flag(f"variances{part}"), 1)
                link(pool, "pool_step", P.tensor_scalar(rstd, mv[:, :, 1], 1e-5, None, ALU.add))
                P.tensor_tensor(rstd, rstd, nhalf, ALU.pow).then_inc(flag(f"rstd{part}"), 1)

            pool.wait_ge(flag("exponents_ready"), 1)
            rstds(0)
            pool.wait_ge(flag("tables_ready"), 1)
            pool.wait_ge(flag("nw_loaded"), 16)

            def front(n, m, par):
                pool.wait_ge(wo_in[par].sem, wo_in[par].at(m, 16))
                hold(pool, "pool_held")
                P.tensor_scalar(wo[par][:, :, :], wo[par][:, :, :], nw[:, :], None, ALU.mult).then_inc(won_ready.sem, 1)
                yield
                for w in range(2):
                    pool.wait_ge(silu_done.sem, silu_done.at(n, w + 1))
                    src = kq[par][:, :, w, :]
                    P.tensor_tensor(vT[:, w, :].rearrange("p (c t) -> p c t", c=NC), src, src,
                                    ALU.mult).then_inc(sq_ready.sem, 1)
                yield
                pool.wait_ge(nk_ready.sem, nk_ready.at(n, 2))
                for w in range(2):
                    P.tensor_tensor(nk[par][:, 3 + w, :], nk[par][:, w, :], half[:, w, :],
                                    ALU.pow).then_inc(rs_ready.sem, 1)

            def scan(n, par, between):
                pool.wait_ge(z_ready.sem, z_ready.at(n, 4))
                pool.wait_ge(rs_ready.sem, rs_ready.at(n, 2))
                between()
                for c in range(NC):
                    pool.wait_ge(o1_ready.sem, o1_ready.at(n, c + 1))
                    pool.wait_ge(og_full.sem, og_full.at(n, max(c - 1, 0)))
                    P.tensor_tensor(o2[c % 2][:, :, :], o1[c % 2][:, :, :],
                                    sz[par][:, c, :].rearrange("p (a b) -> p a b", a=2), ALU.mult).then_inc(
                                        o2_ready.sem, 1)
                    if c == 0:
                        between()
                    sq, t1, t2, t3 = (ss[:, c % 2, k, :] for k in range(4))
                    pool.wait_ge(ss_ready.sem, ss_ready.at(n, 2 * c + 2))
                    hold(pool, "pool_held")
                    P.tensor_scalar(t1, sq, 1.0 / C, 1e-6, ALU.mult, ALU.add).then_inc(f_step.sem, 1)
                    pool.wait_ge(f_step.sem, f_step.at(n, 3 * c + 1))
                    P.tensor_tensor(t2, t1, half[:, 1, 0:2], ALU.pow).then_inc(f_step.sem, 1)
                    pool.wait_ge(f_step.sem, f_step.at(n, 3 * c + 2))
                    hold(pool, "pool_held")
                    P.tensor_scalar(t3, t2, nk[par][:, 4, c:c + 1], None, ALU.mult).then_inc(f_step.sem, 1)
                    pool.wait_ge(f_step.sem, f_step.at(n, 3 * c + 3))
                    P.tensor_tensor(o2[c % 2][:, :, :], o2[c % 2][:, :, :], bc(t3.unsqueeze(2), [128, 2, C]),
                                    ALU.mult).then_inc(o3_ready.sem, 1)
                    if c == 0:
                        between()

            pairs(pool, front, scan)
            pool.wait_ge(acc_done.sem, acc_done.at(NP, 0))
            P.memset(acc2, 0.0).then_inc(flag("acc2_cleared"), 1)
            rstds(1)


_INS = ["L0_attn_hidden_states", "L0_attn_W_qkvz", "L0_attn_W_ba", "L0_attn_conv_w", "L0_attn_dt_bias",
        "L0_attn_A_log", "L0_attn_norm_weight", "L0_attn_W_out", "L0_ffn_w_router", "L0_ffn_we1", "L0_ffn_we3",
        "L0_ffn_we2", "L0_ffn_ws1", "L0_ffn_ws3", "L0_ffn_ws2", "L0_c", "L0_wmod"]


def constants():
    c = np.zeros((128, C_N), np.float32)
    c[:, C_ID:C_ID + 128] = np.eye(128)
    p, q = np.arange(128)[:, None] % HB, np.arange(HB)[None, :]
    c[:, C_ID64:C_ID64 + HB] = p == q
    for lvl in range(LEVELS):
        b = BB * 2 ** lvl
        c[:, C_MASK + HB * lvl:C_MASK + HB * (lvl + 1)] = -1.0 * ((p // (2 * b) == q // (2 * b)) & (p // b > q // b))
    c[:, C_ONE] = 1.0
    r16, r32, q32 = p % BB, p % (2 * BB), q[:, 0:2 * BB]
    c[:, C_ID16:C_ID16 + BB] = r16 == q[:, 0:BB]
    c[:, C_BASE:C_BASE + 2 * BB] = -1.0 * ((r32 // BB == q32 // BB) & (r32 < q32))
    c[:, C_PLACE:C_PLACE + HB] = p // BB == q // BB
    return c


def kernel(**inputs):
    import concourse.bacc as _bacc
    from concourse.bass_utils import run_bass_kernel_spmd as _run

    nc = _bacc.Bacc("TRN2", target_bir_lowering=False, num_devices=1)
    arrays, args = {}, []
    for name in _INS:
        a = np.ascontiguousarray(inputs[name])
        arrays[f"in_{name}"] = a
        args.append(nc.dram_tensor(f"in_{name}", a.shape, F32, kind="ExternalInput").ap())
    arrays["in_constants"] = constants()
    args.append(nc.dram_tensor("in_constants", (128, C_N), F32, kind="ExternalInput").ap())
    args.append(nc.dram_tensor("decays", (NH, NC, C), F32, kind="Internal").ap())
    args.append(nc.dram_tensor("last_decays", (NH, NC), F32, kind="Internal").ap())
    args.append(nc.dram_tensor("out_0", (1, T, D), F32, kind="ExternalOutput").ap())
    adaln_block(nc, *args)
    r = _run(nc, [arrays], core_ids=[0])
    return r.results[0]["out_0"]
```

```python
import numpy as np
import concourse.bass as bass
from concourse import mybir
from contextlib import ExitStack

F32 = mybir.dt.float32
ALU = mybir.AluOpType
ACT = mybir.ActivationFunctionType
AX = mybir.AxisListType

T, D = 1024, 256
C = 128
NC = T // C
KT = D // 128
NP = 16
NH = 2 * NP
PW = 768
QCOL, KCOL, VCOL, ZCOL = 0, 128, 256, 512
NE, NS, TOPK = 16, 4, 4
HB = 64
BB = 16
LEVELS = 2
UG = 8
NU = 2 * NC
FILLS = 40
RING = 4
NT = NE + NS
MFILLS = 8
DVE_OUT = 6
F_K, F_QV, F_NK, F_KK, F_NQ, F_V1, F_Z, F_KT, F_Z3, F_LEVEL = 0, 10, 14, 15, 19, 20, 22, 25, 27, 28
F_LAST = FILLS + 2
F_VT = F_LAST + 2
F_END = F_VT + 6
BASE_YIELDS = (1, 3, 5, 6, 7, 8, 9, 10, 11, 12, 13, 14)
C_ID, C_MASK = 0, 128
C_ONE = C_MASK + HB * LEVELS
C_ID16 = C_ONE + 1
C_BASE = C_ID16 + BB
C_PLACE = C_BASE + 2 * BB
C_N = C_PLACE + HB


def turns(k):
    return 1 if k < BB // 2 - 1 else 2


class Count:

    def __init__(self, sem, per):
        self.sem, self.per = sem, per

    def at(self, n, k):
        return n * self.per + (k + 1)


def adaln_block(nc, x, w_qkvz, w_ba, conv_w, dt_bias, a_log, norm_w, w_out, w_router, we1, we3, we2,
                ws1, ws3, ws2, c_in, wmod, consts, d_alpha, d_last, out):
    ctx = ExitStack()
    with ctx:
        def sb(name, shape):
            return ctx.enter_context(nc.sbuf_tensor(name, shape, F32))

        def sem(name):
            return ctx.enter_context(nc.semaphore(name))

        rounds = []

        def counted(name, per):
            rounds.append(Count(sem(name), per))
            return rounds[-1]

        cst = sb("cst", [128, C_N])
        hT = sb("hT", [128, KT, T])
        wq = [sb(f"wq{i}", [128, KT, PW]) for i in range(2)]
        cw = [sb(f"cw{i}", [128, 4, 4]) for i in range(2)]
        wo = [sb(f"wo{i}", [128, 2, D]) for i in range(2)]
        xpad = [sb(f"xpad{i}", [128, T + 3]) for i in range(2)]
        cacc = [sb(f"cacc{i}", [128, T]) for i in range(2)]
        kq = [sb(f"kq{i}", [128, NC, 2, C]) for i in range(2)]
        vT = sb("vT", [128, 2, T])
        sz = [sb(f"sz{i}", [128, NC, 2 * C]) for i in range(2)]
        lt = sb("lt", [128, NU, C])
        am = [sb(f"am{i}", [128, NU, 2, C]) for i in range(2)]
        km = [sb(f"km{i}", [128, NU, C]) for i in range(2)]
        vp = [sb(f"vp{i}", [128, NC, 2, C]) for i in range(2)]
        xf = [sb(f"xf{i}", [128, NU, C]) for i in range(2)]
        xt = sb("xt", [128, NU, HB])
        xc = sb("xc", [128, NU, HB])
        yc = sb("yc", [128, NU, HB])
        acc = sb("acc", [128, NC, D])
        st = sb("st", [128, 2, C])
        rr = sb("rr", [128, 2, C])
        uu = sb("uu", [128, 2, C])
        qse = sb("qse", [128, 2, C])
        o1 = [sb(f"o1{i}", [128, 2, C]) for i in range(2)]
        o2 = [sb(f"o2{i}", [128, 2, C]) for i in range(2)]
        ogt = sb("ogt", [128, 2, C])
        junk = sb("junk", [128, 2, C])
        tab = sb("tab", [128, NP, 3, 2, NC])
        sc = [sb(f"sc{i}", [128, 3, 2, NC]) for i in range(2)]
        nk = [sb(f"nk{i}", [128, 5, NC]) for i in range(2)]
        sj = sb("sj", [128, 2, NC])
        wl = sb("wl", [128, 2, NC])
        half = sb("half", [128, 2, NC])
        ss = sb("ss", [128, 2, 4, 2])
        nw = sb("nw", [128, 1])
        sm = sb("sm", [128, 128])
        modc = sb("modc", [128, 8])
        gate = sb("gate", [128, 2, D])
        bank = [ctx.enter_context(nc.psum_tensor(f"bank{i}", [128, 512], F32)) for i in range(8)]
        KSB, XRB, QSB, OGB = bank[4], bank[5], bank[6], bank[7]

        ident = cst[:, C_ID:C_ID + 128]
        ones = cst[:, C_ONE:C_ONE + 1]

        def bc(ap, shape):
            return ap.broadcast_to(shape)

        def mask(lo, hi, lvl, units):
            m = cst[lo:hi, C_MASK + HB * lvl:C_MASK + HB * (lvl + 1)]
            return bc(m.unsqueeze(1), [hi - lo, units, HB])

        flags = {}

        def flag(name):
            if name not in flags:
                flags[name] = sem(name)
            return flags[name]

        steps = {}

        def link(eng, name, ins):
            steps[name] = steps.get(name, 0) + 1
            ins.then_inc(flag(name), 1)
            eng.wait_ge(flag(name), steps[name])

        def hold(eng, name):
            eng.sem_inc(flag(name), 1)

        w_in = [counted(f"w_loaded{i}", 16) for i in range(2)]
        cw_in = [counted(f"taps_loaded{i}", 48) for i in range(2)]
        wo_in = [counted(f"wout_loaded{i}", 16) for i in range(2)]
        al_in = counted("decays_loaded", 16)
        full = counted("bank_filled", FILLS)
        x_copied = counted("projection_copied", 8)
        z_ready = counted("z_ready", 4)
        conv_done = counted("conv_done", 4)
        tap = counted("tap_added", 8)
        silu_done = counted("silu_done", 4)
        sq_ready = counted("squares_ready", 2)
        sc_ready = counted("scalars_ready", 1)
        nk_ready = counted("norms_ready", 2)
        rs_ready = counted("roots_ready", 2)
        s_ready = counted("s_ready", 2)
        lt_ready = counted("decay_products_ready", 1)
        am_ready = counted("attention_matrices_ready", 4)
        wl_ready = counted("key_scales_ready", 1)
        km_done = counted("keys_scaled", 2)
        vp_done = counted("values_scaled", 4)
        nb_ready = counted("blocks_gathered", 2)
        base = counted("substitution_steps", 3 + 3 * sum(turns(k) for k in range(BB - 1)))
        inv = counted("inverse_parts", 4 + 6 * LEVELS)
        last_copied = counted("last_blocks_copied", 4)
        won_ready = counted("wout_scaled", 1)
        ks_full, qs_full, ku_full = (counted(f"{w}_full", NC - 1) for w in ("ks", "qs", "ku"))
        xr_full, pu_full, og_full, wo_full = (counted(f"{w}_full", NC) for w in ("xr", "pu", "og", "wo"))
        r_ready, st_ready, qse_ready, o1_ready = (
            counted(f"{w}_ready", NC - 1) for w in ("r", "state", "qse", "o1"))
        pu_copied, u_ready, ogt_ready, o2_ready, o3_ready, acc_done = (
            counted(w, NC) for w in ("pu_copied", "u_ready", "ogt_ready", "o2_ready", "o3_ready", "acc_done"))
        ss_ready = counted("ss_ready", 2 * NC)
        f_step = counted("scale_steps", 3 * NC)
        w13_in = [counted(f"w13_loaded{i}", 32) for i in range(2)]
        w2_in = [counted(f"w2_loaded{i}", 16) for i in range(2)]
        mfull = counted("moe_bank_filled", MFILLS)
        sg_ready = counted("silu_gate_ready", 2)
        g_ready = counted("hidden_ready", 2)
        cwe_ready = counted("weights_ready", 1)
        down_done = counted("down_added", NC)

        def drained(f):
            if f < F_K + 2:
                return x_copied, f + 1
            if f < F_NK:
                return x_copied, 2 + f - F_QV + 1
            if f == F_NK:
                return nk_ready, 1
            if f < F_NQ:
                return am_ready, f - F_KK + 1
            if f == F_NQ:
                return nk_ready, 2
            if f < F_Z:
                return x_copied, 6 + f - F_V1 + 1
            if f < F_KT:
                return z_ready, f - F_Z + 1
            if f < F_Z3:
                return km_done, f - F_KT + 1
            if f == F_Z3:
                return z_ready, 4
            if f < F_LAST:
                return inv, 4 + f - F_LEVEL + 1
            if f < F_VT:
                return last_copied, f - F_LAST + 1
            if f < F_VT + 4:
                return vp_done, f - F_VT + 1
            return last_copied, 2 + f - F_VT - 4 + 1

        def ring(f, par):
            return bank[(f + FILLS * par) % RING]

        def projection(t, q):
            return (F_K, F_QV, F_QV + 2, F_V1)[t] + q

        def z_fill(j):
            return F_Z + j if j < 3 else F_Z3

        def pairs(eng, begin, early, front, finish, scan, first, last_scan):
            def whole(part):
                for _ in part:
                    pass

            def both(n, before, m, par, after):
                def parts():
                    yield from front(n, m, par)
                    if after is not None:
                        begin(n + 1, after, 1 - par)
                    yield from finish(n, par)
                    if after is not None:
                        yield from early(n + 1, 1 - par)

                work = parts()
                scan(before, 1 - par, lambda: next(work, None))
                whole(work)

            whole(first)
            whole(front(0, 0, 0))
            begin(1, 0, 1)
            whole(finish(0, 0))
            whole(early(1, 1))
            with eng.Fori(0, NP // 2 - 1) as i:
                both(i * 2 + 1, i * 2, i, 1, i + 1)
                both(i * 2 + 2, i * 2 + 1, i + 1, 0, i + 1)
            both(NP - 1, NP - 2, NP // 2 - 1, 1, None)
            last_scan()

        w_v = w_qkvz.rearrange("(k p) m -> p k m", p=128)
        wo_v = w_out.rearrange("(h p) m -> p h m", p=128)
        cw_v = conv_w.rearrange("(t p) j -> p t j", p=128)
        x_v = x.rearrange("b (c p) d -> p (b c) d", p=128)
        out_v = out.rearrange("b (c p) d -> p (b c) d", p=128)
        al_v = d_alpha.rearrange("(g h) c t -> g (h c) t", h=2)

        xs = vT[:, :, :].rearrange("p a (b d) -> p (a b) d", d=D)
        wmod_sb = am[0][:, :, :, :].rearrange("p u a c -> p (u a c)")[:, 0:KT * 6 * D].rearrange(
            "p (k m) -> p k m", k=KT)
        wba_sb = km[0][:, 0, :].rearrange("p (k m) -> p k m", k=KT)
        dtb, alg = km[0][:, 1, 0:NH], km[0][:, 1, NH:2 * NH]
        scb = km[0][:, 2:4, :]
        zero32 = km[0][0:NH, 4, :]
        last32 = km[0][0:NH, 5, 0:NC]
        lastb = km[0][:, 6:8, :].rearrange("p a b -> p (a b)")
        cT, scT = sm[:, 0:2], sm[:, 2:4]
        stat = sm[:, 4:52].rearrange("p (c k) -> p c k", k=6)
        mv = sm[:, 52:68].rearrange("p (c k) -> p c k", k=2)
        rstd, nhalf = sm[:, 68:76], sm[:, 76:84]
        tmp = [vp[0][:, i, :, :].rearrange("p a b -> p (a b)") for i in range(NC)]
        alT = xf[1][0:NH, 0:NC, :]
        eT = xf[1][0:NH, NC:2 * NC, :]
        wr_sb = km[0][:, 0, 0:KT * NE].rearrange("p (k m) -> p k m", k=KT)
        WP = NE + TOPK
        lg = km[0][:, 1, :].rearrange("p (c e) -> p c e", c=NC)
        pv = km[0][:, 2:4, :].rearrange("p a b -> p (a b)")[:, 0:NC * WP].rearrange("p (c e) -> p c e", c=NC)
        rep = km[0][:, 4:6, :].rearrange("p a b -> p (a b)")[:, 0:NC * WP].rearrange("p (c e) -> p c e", c=NC)
        top = km[0][:, 6, 0:NC * 8].rearrange("p (c e) -> p c e", c=NC)
        cwt = km[0][:, 8:10, :].rearrange("p a b -> p (a b)")[:, 0:NT * NC].rearrange("p (e c) -> p e c", c=NC)
        row = km[0][:, 10, 0:NC]
        w13 = [km[1][:, 4 * i:4 * i + 4, :].rearrange("p (w k) h -> p w k h", w=2) for i in range(2)]
        w2 = [km[1][:, 8 + 2 * i:10 + 2 * i, :].rearrange("p a b -> p (a b)") for i in range(2)]
        cwe = [km[0][:, 11 + i, 0:NC] for i in range(2)]
        sg = [cacc[0][:, 512 * i:512 * i + 512] for i in range(2)]
        gT = cacc[1]
        acc2 = kq[0][:, :, :, :].rearrange("p c a b -> p c (a b)")
        fin = kq[1][:, :, :, :].rearrange("p c a b -> p c (a b)")
        BAB, MODB, GATEB = bank[4], bank[5], bank[6]

        block = ctx.enter_context(nc.Block())

        @block.sync
        def _(sp):
            sp.dma_start(xs, x_v).then_inc(flag("x_loaded"), 16)
            sp.dma_start(cst[:, :], consts).then_inc(flag("consts_loaded"), 16)
            sp.dma_start(cT, c_in.rearrange("a (k p) -> p (a k)", p=128), allow_slow_non_contiguous=True).then_inc(flag("c_loaded"), 16)
            sp.dma_start(wmod_sb, wmod.rearrange("(k p) m -> p k m", p=128)).then_inc(flag("wmod_loaded"), 16)
            sp.dma_start(wba_sb, w_ba.rearrange("(k p) m -> p k m", p=128)).then_inc(flag("wba_loaded"), 16)
            sp.dma_start(dtb, bc(dt_bias.unsqueeze(0), [128, NH])).then_inc(flag("gates_loaded"), 16)
            sp.dma_start(alg, bc(a_log.unsqueeze(0), [128, NH])).then_inc(flag("gates_loaded"), 16)
            sp.dma_start(nw[:, :], norm_w.unsqueeze(1)).then_inc(flag("nw_loaded"), 16)

            def weights(n, par):
                m = n if isinstance(n, int) else None
                if m is None:
                    sp.wait_ge(full.sem, full.at(n, F_LEVEL - 2 * FILLS))
                    hold(sp, "sp_held")
                sp.dma_start(wq[par][:, :, :], w_v[:, :, bass.ds(n * PW, PW)]).then_inc(w_in[par].sem, 16)
                if m is None:
                    sp.wait_ge(conv_done.sem, conv_done.at(n, -4))
                    hold(sp, "sp_held")
                sp.dma_start(cw[par][:, 0:1, :], cw_v[:, bass.ds(n + NP, 1), :]).then_inc(cw_in[par].sem, 16)
                sp.dma_start(cw[par][:, 1:2, :], cw_v[:, bass.ds(n, 1), :]).then_inc(cw_in[par].sem, 16)
                sp.dma_start(cw[par][:, 2:4, :], cw_v[:, bass.ds(n * 2 + 2 * NP, 2), :]).then_inc(
                    cw_in[par].sem, 16)
                if m is None:
                    decays(n)
                    sp.wait_ge(wo_full.sem, wo_full.at(n, -NC))
                    hold(sp, "sp_held")
                sp.dma_start(wo[par][:, :, :], wo_v[:, bass.ds(n * 2, 2), :]).then_inc(wo_in[par].sem, 16)

            def decays(n):
                sp.wait_ge(am_ready.sem, am_ready.at(n, 0))
                hold(sp, "sp_held")
                sp.wait_ge(wl_ready.sem, wl_ready.at(n, 0))
                hold(sp, "sp_held")
                sp.dma_start(lt[:, :, :], bc(al_v[bass.ds(n, 1)], [128, NU, C])).then_inc(al_in.sem, 16)

            weights(0, 0)
            weights(1, 1)
            sp.wait_ge(flag("decays_ready"), 2)
            sp.dma_start(d_alpha.rearrange("h c t -> h (c t)"),
                         alT.rearrange("h c t -> h (c t)")).then_inc(flag("decays_in_dram"), 16)
            sp.dma_start(d_last, last32).then_inc(flag("last_in_dram"), 16)
            sp.wait_ge(flag("last_in_dram"), 16)
            sp.dma_start(lastb, bc(d_last.rearrange("h c -> (h c)").unsqueeze(0), [128, NH * NC])).then_inc(
                flag("last_spread"), 16)
            sp.wait_ge(flag("decays_in_dram"), 16)
            decays(0)
            decays(1)
            with sp.Fori(1, NP // 2) as i:
                for par in range(2):
                    weights(i * 2 + par, par)

            sp.wait_ge(full.sem, full.at(NP - 1, F_END))
            sp.dma_start(xs, x_v).then_inc(flag("x_loaded"), 16)
            sp.wait_ge(acc_done.sem, acc_done.at(NP, 0))
            sp.dma_start(wr_sb, w_router.rearrange("(k p) m -> p k m", p=128)).then_inc(flag("wr_loaded"), 16)

            def expert(e, par, w1, w3, w2s, free):
                if free:
                    sp.wait_ge(mfull.sem, mfull.at(e, 4 - 2 * MFILLS))
                    hold(sp, "sp_held")
                sp.dma_start(w13[par][:, 0:1], w1).then_inc(w13_in[par].sem, 16)
                sp.dma_start(w13[par][:, 1:2], w3).then_inc(w13_in[par].sem, 16)
                if free:
                    sp.wait_ge(mfull.sem, mfull.at(e, -MFILLS))
                    hold(sp, "sp_held")
                sp.dma_start(w2[par].unsqueeze(1), w2s).then_inc(w2_in[par].sem, 16)

            e1, e3 = (w.rearrange("e (k p) h -> p e k h", p=128) for w in (we1, we3))
            e2 = we2.rearrange("e h d -> h e d")
            s1, s3 = (w.rearrange("(k p) (s h) -> p s k h", p=128, h=128) for w in (ws1, ws3))
            s2 = ws2.rearrange("(s h) d -> h s d", h=128)

            def routed(e, par, free):
                one = bass.ds(e, 1)
                expert(e, par, e1[:, one], e3[:, one], e2[:, one], free)

            routed(0, 0, False)
            routed(1, 1, False)
            with sp.Fori(1, NE // 2) as i:
                for par in range(2):
                    routed(i * 2 + par, par, True)
            for s in range(NS):
                expert(NE + s, s % 2, s1[:, s:s + 1], s3[:, s:s + 1], s2[:, s:s + 1], True)
            for lo, hi in ((0, DVE_OUT // 2), (DVE_OUT // 2, DVE_OUT)):
                sp.wait_ge(flag("out_ready"), hi)
                sp.dma_start(out_v[:, lo:hi, :], fin[:, lo:hi, :]).then_inc(flag("out_stored"), 16)
            sp.wait_ge(flag("pool_out_ready"), NC - DVE_OUT)
            sp.dma_start(out_v[:, DVE_OUT:NC, :], fin[:, DVE_OUT:NC, :]).then_inc(flag("out_stored"), 16)
            sp.wait_ge(flag("out_stored"), 48)

        PE = nc.tensor

        @block.tensor
        def _(pe):
            def transposed_rows(part, src):
                for k in range(KT):
                    for q in range(2):
                        b = 2 * k + q
                        for c in range(4):
                            if k == 0:
                                pe.wait_ge(flag(f"rows_normed{part}"), 4 * q + c + 1)
                            last = PE.transpose(bank[b][:, 128 * c:128 * (c + 1)],
                                                src[:, 4 * q + c, 128 * k:128 * (k + 1)], ident)
                        last.then_inc(flag(f"rows_turned{part}"), 1)

            pe.wait_ge(flag("wmod_loaded"), 16)
            pe.wait_ge(flag("silu_c"), 1)
            for j, slot in enumerate((0, 1, 3, 4)):
                for h in range(2):
                    for k in range(KT):
                        at = slot * D + 128 * h
                        last = PE.matmul(MODB[:, 2 * j + h:2 * j + h + 1], wmod_sb[:, k, at:at + 128],
                                         scT[:, k:k + 1], start=(k == 0), stop=(k == KT - 1))
            last.then_inc(flag("mod_columns"), 1)
            pe.wait_ge(flag("silu_c_spread"), 1)
            for j, slot in enumerate((2, 5)):
                for k in range(KT):
                    last = PE.matmul(GATEB[:, D * j:D * (j + 1)], scb[:, k, :],
                                     wmod_sb[:, k, slot * D:(slot + 1) * D], start=(k == 0), stop=(k == KT - 1))
            last.then_inc(flag("gate_rows"), 1)
            pe.wait_ge(flag("consts_loaded"), 16)
            transposed_rows(0, xs)
            pe.wait_ge(flag("hT_ready0"), 4)
            pe.wait_ge(flag("wba_loaded"), 16)
            for c in range(NC):
                for k in range(KT):
                    last = PE.matmul(BAB[:, 64 * c:64 * (c + 1)], hT[:, k, C * c:C * (c + 1)], wba_sb[:, k, :],
                                     start=(k == 0), stop=(k == KT - 1))
            last.then_inc(flag("gates_projected"), 1)
            def fill(n, par, f):
                before, f0 = 0, f - RING
                if f0 < F_K or F_K + 2 <= f0 < F_QV:
                    before, f0 = -1, f0 + FILLS
                elif FILLS <= f0 < F_LAST:
                    before, f0 = 1, f0 - FILLS
                first, last = isinstance(n, int) and n == 0, isinstance(n, int) and n == NP - 1
                if before < 0 and first:
                    ev, k, before = x_copied, f0 - F_VT - 4 + 1, 0
                    if k < 1:
                        return ring(f, par)
                elif before > 0 and last:
                    return ring(f, par)
                else:
                    ev, k = drained(f0)
                if ev is not inv or before:
                    pe.wait_ge(ev.sem, ev.at(n + before, k))
                return ring(f, par)

            def project(n, par, t, q):
                col = (KCOL, QCOL, VCOL, VCOL + 128)[t]
                b = fill(n, par, projection(t, q))
                for k in range(KT):
                    last = PE.matmul(b[:, :], wq[par][:, k, col:col + 128], hT[:, k, 512 * q:512 * (q + 1)],
                                     start=(k == 0), stop=(k == KT - 1))
                    if k < KT - 1 and t == 3:
                        yield
                last.then_inc(full.sem, 1)

            def project_z(n, par, j):
                b = fill(n, par, z_fill(j))
                for c in (2 * j, 2 * j + 1):
                    for k in range(KT):
                        last = PE.matmul(b[:, D * (c % 2):D * (c % 2 + 1)], hT[:, k, C * c:C * (c + 1)],
                                         wq[par][:, k, ZCOL:ZCOL + D], start=(k == 0), stop=(k == KT - 1))
                    if c % 2 == 0:
                        yield
                last.then_inc(full.sem, 1)

            def norms(n, par, w):
                b = fill(n, par, (F_NK, F_NQ)[w])
                pe.wait_ge(sq_ready.sem, sq_ready.at(n, w + 1))
                for c in range(NC):
                    last = PE.matmul(b[:, c:c + 1], vT[:, w, C * c:C * (c + 1)], ones, start=True, stop=True)
                last.then_inc(full.sem, 1)

            def products(n, par, j):
                pe.wait_ge(silu_done.sem, silu_done.at(n, 2))
                b = fill(n, par, F_KK + j)
                for c in (2 * j, 2 * j + 1):
                    last = PE.matmul(b[:, 256 * (c % 2):256 * (c % 2 + 1)], kq[par][:, c, 0, :],
                                     kq[par][:, c, :, :].rearrange("p a b -> p (a b)"), start=True, stop=True)
                last.then_inc(full.sem, 1)

            def begin(n, m, par):
                pe.wait_ge(w_in[par].sem, w_in[par].at(m, 16))
                for q in range(2):
                    for _ in project(n, par, 0, q):
                        pass

            def early(n, par):
                if isinstance(n, int) and n == 0:
                    pe.wait_ge(full.sem, full.at(0, 2))
                    pe.sem_inc(full.sem, F_QV - 2)
                for t, q in ((1, 0), (1, 1), (2, 0), (2, 1)):
                    yield from project(n, par, t, q)
                    if q:
                        yield
                norms(n, par, 0)
                products(n, par, 0)
                products(n, par, 1)

            def front(n, m, par):
                products(n, par, 2)
                products(n, par, 3)
                yield
                norms(n, par, 1)
                yield
                yield from project(n, par, 3, 0)
                yield
                yield
                for _ in project(n, par, 3, 1):
                    pass
                yield
                for j in range(3):
                    yield from project_z(n, par, j)
                    yield
                for j in range(2):
                    b = fill(n, par, F_KT + j)
                    for c in range(4):
                        last = PE.transpose(b[:, 128 * c:128 * (c + 1)], kq[par][:, 4 * j + c, 0, :], ident)
                    last.then_inc(full.sem, 1)
                    yield
                    yield
                yield from project_z(n, par, 3)
                yield
                yield from invert(n, par)

            def blocks(b, g, lhs, rhs):
                hold(pe, "pe_held")
                for i in range(UG):
                    u = UG * g + i
                    for lo in (0, HB):
                        last = PE.matmul(b[lo:lo + HB, HB * i:HB * (i + 1)], lhs(u, lo), rhs(u, lo),
                                         start=True, stop=True)
                last.then_inc(full.sem, 1)

            def invert(n, par):
                def a_of(u, lo):
                    return am[par][lo:lo + HB, u, 0, lo:lo + HB]

                def of(t):
                    return lambda u, lo: t[lo:lo + HB, u, :]

                for lvl in range(LEVELS):
                    f0, done = F_LEVEL + 6 * lvl, 4 + 6 * lvl
                    for g in range(2):
                        b = fill(n, par, f0 + g)
                        pe.wait_ge(inv.sem, inv.at(n, 3 + g if lvl == 0 else done - 6 + (4, 6)[g]))
                        blocks(b, g, a_of, of(xc))
                    yield
                    for g in range(2):
                        pe.wait_ge(inv.sem, inv.at(n, done + 1 + g))
                        b = fill(n, par, f0 + 2 + 2 * g)
                        blocks(b, g, of(yc), of(xt))
                        b = fill(n, par, f0 + 3 + 2 * g)
                        blocks(b, g, of(xt), of(yc))
                        yield

            def finish(n, par):
                if isinstance(n, int) and n == NP - 1:
                    pe.wait_ge(full.sem, full.at(n, FILLS))
                    pe.sem_inc(full.sem, F_LAST - FILLS)
                for g in range(2):
                    b = fill(n, par, F_LAST + g)
                    pe.wait_ge(inv.sem, inv.at(n, 4 + 6 * LEVELS - 6 + (5, 6)[g]))
                    hold(pe, "pe_held")
                    for i in range(UG):
                        u = UG * g + i
                        last = PE.matmul(b[HB:C, HB * i:HB * (i + 1)], am[par][0:HB, u, 0, HB:C], xc[0:HB, u, :],
                                         start=True, stop=True)
                    last.then_inc(full.sem, 1)
                yield
                pe.wait_ge(silu_done.sem, silu_done.at(n, 4))
                for j in range(4):
                    b = fill(n, par, F_VT + j)
                    for i in range(4):
                        c, h = 2 * j + i // 2, i % 2
                        last = PE.transpose(b[:, 128 * i:128 * (i + 1)], vT[:, h, C * c:C * (c + 1)], ident)
                    last.then_inc(full.sem, 1)
                for g in range(2):
                    b = fill(n, par, F_VT + 4 + g)
                    pe.wait_ge(last_copied.sem, last_copied.at(n, g + 1))
                    hold(pe, "pe_held")
                    for i in range(UG):
                        u = UG * g + i
                        last = PE.matmul(b[0:HB, HB * i:HB * (i + 1)], yc[HB:C, u, :], xf[par][HB:C, u, HB:C],
                                         start=True, stop=True)
                    last.then_inc(full.sem, 1)
                yield

            def turn_out(n, c):
                pe.wait_ge(o3_ready.sem, o3_ready.at(n, c + 1))
                pe.wait_ge(acc_done.sem, acc_done.at(n, c))
                for h in range(2):
                    last = PE.transpose(OGB[:, 128 * h:128 * (h + 1)], o2[c % 2][:, h, :], ident)
                last.then_inc(og_full.sem, 1)

            def project_out(n, par, c):
                pe.wait_ge(ogt_ready.sem, ogt_ready.at(n, c + 1))
                pe.wait_ge(won_ready.sem, won_ready.at(n, 1))
                for h in range(2):
                    last = PE.matmul(OGB[:, 256:512], ogt[:, h, :], wo[par][:, h, :], start=(h == 0), stop=(h == 1))
                last.then_inc(wo_full.sem, 1)

            def scan(n, par, between):
                state = st[:, :, :].rearrange("p a b -> p (a b)")
                pe.wait_ge(km_done.sem, km_done.at(n, 2))
                pe.wait_ge(vp_done.sem, vp_done.at(n, 4))
                pe.wait_ge(last_copied.sem, last_copied.at(n, 4))
                for c in range(NC):
                    if c:
                        pe.wait_ge(st_ready.sem, st_ready.at(n, c))
                        PE.matmul(KSB[:, 0:256], kq[par][:, c, 0, :], state, start=True, stop=True).then_inc(
                            ks_full.sem, 1)
                        pe.wait_ge(pu_copied.sem, pu_copied.at(n, c))
                        PE.matmul(QSB[:, 0:256], kq[par][:, c, 1, :], state, start=True, stop=True).then_inc(
                            qs_full.sem, 1)
                    if c >= 3:
                        project_out(n, par, c - 3)
                    between()
                    if c:
                        pe.wait_ge(r_ready.sem, r_ready.at(n, c))
                    pe.wait_ge(u_ready.sem, u_ready.at(n, c))
                    for h in range(2):
                        last = PE.matmul(XRB[:, 128 * h:128 * (h + 1)], xf[par][:, NC * h + c, :],
                                         rr[:, h, :] if c else vp[par][:, c, h, :], start=True, stop=True)
                    last.then_inc(xr_full.sem, 1)
                    between()
                    pe.wait_ge(u_ready.sem, u_ready.at(n, c + 1))
                    if c < NC - 1:
                        if c == 0:
                            pe.wait_ge(st_ready.sem, st_ready.at(n, 0))
                        for h in range(2):
                            last = PE.matmul(KSB[:, 256 + 128 * h:256 + 128 * (h + 1)], km[par][:, NC * h + c, :],
                                             uu[:, h, :], start=True, stop=True)
                        last.then_inc(ku_full.sem, 1)
                    if c:
                        pe.wait_ge(qse_ready.sem, qse_ready.at(n, c))
                    else:
                        pe.wait_ge(pu_copied.sem, pu_copied.at(n, 0))
                    for h in range(2):
                        last = PE.matmul(QSB[:, 256 + 128 * h:256 + 128 * (h + 1)], am[par][:, NC * h + c, 1, :],
                                         uu[:, h, :], start=True, stop=True)
                    last.then_inc(pu_full.sem, 1)
                    if c >= 2:
                        turn_out(n, c - 2)
                    between()
                for c in range(NC - 3, NC):
                    project_out(n, par, c)
                    if c < NC - 1:
                        between()
                        turn_out(n, c + 1)
                        between()

            begin(0, 0, 0)
            first = early(0, 0)
            next(first)
            pe.wait_ge(flag("alpha_ready"), 1)
            pe.wait_ge(flag("beta_stored"), 1)
            pe.wait_ge(flag("mods_stored"), 1)
            for c in range(NC):
                last = PE.transpose(bank[4 + c // 4][0:NH, 128 * (c % 4):128 * (c % 4 + 1)],
                                    tmp[3][:, NH * c:NH * (c + 1)], ident)
            last.then_inc(flag("alpha_turned"), 1)
            pe.wait_ge(flag("products_ready"), 1)
            for c in range(NC):
                last = PE.transpose(bank[6][:, NH * c:NH * (c + 1)], eT[:, c, :], ident[0:NH, 0:NH])
            last.then_inc(flag("products_turned"), 1)
            pe.wait_ge(flag("tables_ready"), 1)

            pairs(pe, begin, early, front, finish, scan, first, lambda: scan(NP - 1, 1, lambda: None))

            transposed_rows(1, xs)
            pe.wait_ge(flag("hT_ready1"), 4)
            pe.wait_ge(flag("wr_loaded"), 16)
            for c in range(NC):
                for k in range(KT):
                    last = PE.matmul(bank[4][:, NE * c:NE * (c + 1)], hT[:, k, C * c:C * (c + 1)], wr_sb[:, k, :],
                                     start=(k == 0), stop=(k == KT - 1))
            last.then_inc(flag("logits_full"), 1)
            pe.wait_ge(flag("logits_shifted"), 1)

            def hidden_tile(e, m, par):
                pe.wait_ge(w13_in[par].sem, w13_in[par].at(m, 32))
                pe.wait_ge(g_ready.sem, g_ready.at(e, 0))
                for q in range(2):
                    for w in range(2):
                        for k in range(KT):
                            last = PE.matmul(bank[2 * q + w][:, :], w13[par][:, w, k, :],
                                             hT[:, k, 512 * q:512 * (q + 1)], start=(k == 0), stop=(k == KT - 1))
                        last.then_inc(mfull.sem, 1)
                pe.wait_ge(w2_in[par].sem, w2_in[par].at(m, 16))
                pe.wait_ge(down_done.sem, down_done.at(e, 0))
                for j in range(4):
                    pe.wait_ge(g_ready.sem, g_ready.at(e, 1 + j // 2))
                    for i in range(2):
                        c = 2 * j + i
                        last = PE.matmul(bank[4 + j][:, D * i:D * (i + 1)], gT[:, C * c:C * (c + 1)], w2[par],
                                         start=True, stop=True)
                    last.then_inc(mfull.sem, 1)

            with pe.Fori(0, NT // 2) as i:
                for par in range(2):
                    hidden_tile(i * 2 + par, i, par)

        @block.scalar
        def _(act):
            act.wait_ge(flag("c_loaded"), 16)
            nc.scalar.activation(scT, cT, ACT.Silu).then_inc(flag("silu_c"), 1)

            def to_hT(part):
                act.wait_ge(flag("mods_stored"), 1)
                for k in range(KT):
                    for q in range(2):
                        act.wait_ge(flag(f"rows_turned{part}"), 2 * k + q + 1)
                        nc.scalar.activation(hT[:, k, 512 * q:512 * (q + 1)], bank[2 * k + q][:, :], ACT.Identity,
                                             bias=modc[:, 4 * part + k:4 * part + k + 1],
                                             scale=modc[:, 4 * part + 2 + k:4 * part + 3 + k]).then_inc(
                                                 flag(f"hT_ready{part}"), 1)

            to_hT(0)
            act.wait_ge(flag("neg_abs_ready"), 1)
            nc.scalar.activation(tmp[2], tmp[1], ACT.Exp).then_inc(flag("exp_ready"), 1)
            act.wait_ge(flag("gates_loaded"), 32)
            nc.scalar.activation(tmp[6][:, 0:NH], alg, ACT.Exp).then_inc(flag("exp_ready"), 1)
            act.wait_ge(flag("b_copied"), 1)
            nc.scalar.activation(tmp[7], tmp[5], ACT.Exp, scale=-1.0).then_inc(flag("exp_ready"), 1)
            def copy_projection(n, par, t, q):
                if q == 0:
                    act.wait_ge(conv_done.sem, conv_done.at(n, max(t - 1, 0)))
                    act.wait_ge(silu_done.sem, silu_done.at(n, max(t - 1, 0)))
                act.wait_ge(full.sem, full.at(n, projection(t, q) + 1))
                b = ring(projection(t, q), par)[:, :]
                nc.scalar.activation(xpad[t % 2][:, 3 + 512 * q:3 + 512 * (q + 1)], b, ACT.Copy)
                nc.scalar.activation(cacc[t % 2][:, 512 * q:512 * (q + 1)], b, ACT.Copy,
                                     scale=cw[par][:, t, 3:4]).then_inc(x_copied.sem, 1)

            def silu(n, par, t):
                act.wait_ge(conv_done.sem, conv_done.at(n, t + 1))
                dst = kq[par][:, :, t, :] if t < 2 else vT[:, t - 2, :]
                src = cacc[t % 2][:, :]
                nc.scalar.activation(dst, src.rearrange("p (c t) -> p c t", c=NC) if t < 2 else src,
                                     ACT.Silu).then_inc(silu_done.sem, 1)

            def square(n, par, w):
                act.wait_ge(silu_done.sem, silu_done.at(n, w + 1))
                nc.scalar.activation(vT[:, w, :].rearrange("p (c t) -> p c t", c=NC), kq[par][:, :, w, :],
                                     ACT.Square).then_inc(sq_ready.sem, 1)

            def scale_keys(n, par, j, h):
                act.wait_ge(wl_ready.sem, wl_ready.at(n, 1))
                act.wait_ge(full.sem, full.at(n, F_KT + j + 1))
                for i in range(4):
                    c = 4 * j + i
                    last = nc.scalar.activation(km[par][:, NC * h + c, :],
                                                ring(F_KT + j, par)[:, 128 * i:128 * (i + 1)],
                                                ACT.Copy, scale=wl[:, h, c:c + 1])
                if h:
                    last.then_inc(km_done.sem, 1)

            def gather_blocks(n, par, q):
                act.wait_ge(am_ready.sem, am_ready.at(n, 2 * q + 2))
                for lo in range(0, 128, 2 * BB):
                    hi = lo + 2 * BB
                    last = nc.scalar.activation(
                        yc[lo:hi, :, 0:2 * BB].rearrange("p (h c) i -> p h c i", h=2)[:, :, 4 * q:4 * q + 4, :],
                        am[par][lo:hi, :, 0, lo:hi].rearrange("p (h c) i -> p h c i", h=2)[:, :, 4 * q:4 * q + 4, :],
                        ACT.Copy)
                last.then_inc(nb_ready.sem, 1)

            def silu_z(n, par, j):
                act.wait_ge(full.sem, full.at(n, z_fill(j) + 1))
                nc.scalar.activation(sz[par][:, 2 * j:2 * j + 2, :].rearrange("p a b -> p (a b)"),
                                     ring(z_fill(j), par)[:, :], ACT.Silu).then_inc(z_ready.sem, 1)

            def begin(n, m, par):
                act.wait_ge(cw_in[par].sem, cw_in[par].at(m, 48))
                copy_projection(n, par, 0, 0)
                copy_projection(n, par, 0, 1)

            def early(n, par):
                copy_projection(n, par, 1, 0)
                copy_projection(n, par, 1, 1)
                silu(n, par, 0)
                square(n, par, 0)
                yield
                copy_projection(n, par, 2, 0)
                silu(n, par, 1)
                copy_projection(n, par, 2, 1)

            def front(n, m, par):
                square(n, par, 1)
                yield
                yield
                gather_blocks(n, par, 0)
                yield
                yield
                gather_blocks(n, par, 1)
                copy_projection(n, par, 3, 0)
                yield
                copy_projection(n, par, 3, 1)
                yield
                for j in range(3):
                    yield
                    silu_z(n, par, j)
                    yield
                yield
                scale_keys(n, par, 0, 0)
                yield
                scale_keys(n, par, 0, 1)
                yield
                yield
                scale_keys(n, par, 1, 0)
                yield
                scale_keys(n, par, 1, 1)
                silu_z(n, par, 3)
                yield
                yield
                yield
                silu(n, par, 2)
                yield
                yield
                yield
                silu(n, par, 3)
                yield

            def finish(n, par):
                for g in range(2):
                    act.wait_ge(full.sem, full.at(n, F_LAST + g + 1))
                    nc.scalar.activation(yc[HB:C, UG * g:UG * (g + 1), :].rearrange("p a b -> p (a b)"),
                                         ring(F_LAST + g, par)[HB:C, :], ACT.Copy, scale=-1.0).then_inc(
                                             last_copied.sem, 1)
                act.wait_ge(rs_ready.sem, rs_ready.at(n, 2))
                for j in range(4):
                    if j == 2:
                        yield
                    act.wait_ge(full.sem, full.at(n, F_VT + j + 1))
                    for i in range(2):
                        c = 2 * j + i
                        last = nc.scalar.activation(
                            vp[par][:, c, :, :].rearrange("p a b -> p (a b)"),
                            ring(F_VT + j, par)[:, 256 * i:256 * (i + 1)], ACT.Copy, scale=nk[par][:, 3, c:c + 1])
                    last.then_inc(vp_done.sem, 1)
                for g in range(2):
                    act.wait_ge(full.sem, full.at(n, F_VT + 4 + g + 1))
                    nc.scalar.activation(
                        xf[par][0:HB, UG * g:UG * (g + 1), HB:C],
                        ring(F_VT + 4 + g, par)[0:HB, :].rearrange("p (u c) -> p u c", u=UG),
                        ACT.Copy).then_inc(last_copied.sem, 1)
                yield

            def copy_out(n, c):
                act.wait_ge(og_full.sem, og_full.at(n, c + 1))
                nc.scalar.activation(ogt[:, :, :].rearrange("p a b -> p (a b)"), OGB[:, 0:256],
                                     ACT.Copy).then_inc(ogt_ready.sem, 1)

            def square_sums(n, par, c):
                act.wait_ge(o2_ready.sem, o2_ready.at(n, c + 1))
                act.wait_ge(ss_ready.sem, ss_ready.at(n, 2 * c))
                for h in range(2):
                    nc.scalar.activation(junk[:, h, :], o2[c % 2][:, h, :], ACT.Square, scale=nk[par][:, 4, c:c + 1],
                                         accum_out=ss[:, c % 2, 0, h:h + 1]).then_inc(ss_ready.sem, 1)

            def scan(n, par, between):
                for c in range(NC):
                    if c:
                        act.wait_ge(qs_full.sem, qs_full.at(n, c))
                        act.wait_ge(o1_ready.sem, o1_ready.at(n, c - 1))
                        for h in range(2):
                            last = nc.scalar.activation(qse[:, h, :], QSB[:, 128 * h:128 * (h + 1)], ACT.Copy,
                                                        scale=sc[par][:, 0, h, c:c + 1])
                        last.then_inc(qse_ready.sem, 1)
                    between()
                    act.wait_ge(xr_full.sem, xr_full.at(n, c + 1))
                    nc.scalar.activation(uu[:, :, :].rearrange("p a b -> p (a b)"), XRB[:, 0:256],
                                         ACT.Copy).then_inc(u_ready.sem, 1)
                    if c:
                        square_sums(n, par, c - 1)
                    between()
                    act.wait_ge(pu_full.sem, pu_full.at(n, c + 1))
                    act.wait_ge(o2_ready.sem, o2_ready.at(n, max(c - 1, 0)))
                    nc.scalar.activation(o1[c % 2][:, :, :].rearrange("p a b -> p (a b)"), QSB[:, 256:512],
                                         ACT.Copy).then_inc(pu_copied.sem, 1)
                    if c >= 2:
                        copy_out(n, c - 2)
                    between()
                between()
                square_sums(n, par, NC - 1)
                copy_out(n, NC - 2)
                between()
                between()
                copy_out(n, NC - 1)
                between()

            begin(0, 0, 0)
            act.wait_ge(flag("g_ready"), 1)
            nc.scalar.activation(tmp[3], tmp[4], ACT.Exp, scale=-1.0).then_inc(flag("alpha_ready"), 1)
            act.wait_ge(flag("tables_ready"), 1)
            nc.scalar.activation(sm[:, 4:6], sm[:, 2:4], ACT.Silu)
            pairs(act, begin, early, front, finish, scan, early(0, 0), lambda: scan(NP - 1, 1, lambda: None))

            to_hT(1)
            act.wait_ge(flag("logits_shifted"), 1)
            nc.scalar.activation(pv[:, :, 0:NE], lg, ACT.Exp).then_inc(flag("exp_logits"), 1)
            with act.Fori(0, NT // 2) as i:
                for par in range(2):
                    e = i * 2 + par
                    for q in range(2):
                        act.wait_ge(mfull.sem, mfull.at(e, 2 * q + 1))
                        act.wait_ge(g_ready.sem, g_ready.at(e, 0))
                        nc.scalar.activation(sg[q], bank[2 * q][:, :], ACT.Silu).then_inc(sg_ready.sem, 1)

        V = nc.vector

        @block.vector
        def _(dve):
            def then(ins):
                link(dve, "dve_step", ins)

            def norm_rows(part, src):
                if part == 0:
                    for c in range(NC):
                        last = V.bn_stats(stat[:, c, :], src[:, c, :])
                    then(last)
                for c in range(NC):
                    last = V.bn_aggr(mv[:, c, :], stat[:, c, :])
                last.then_inc(flag(f"variances{part}"), 1)
                dve.wait_ge(flag(f"variances{part}"), 1)
                dve.wait_ge(flag(f"rstd{part}"), 1)
                for c in range(NC):
                    V.tensor_scalar(xs[:, c, :], src[:, c, :], mv[:, c, 0:1], rstd[:, c:c + 1], ALU.subtract,
                                    ALU.mult).then_inc(flag(f"rows_normed{part}"), 1)

            V.memset(half[:, 0, :], 0.5)
            V.memset(half[:, 1, :], -0.5)
            V.memset(nhalf, -0.5)
            for i in range(2):
                V.memset(xpad[i][:, 0:3], 0.0)
            for i in range(2):
                last = V.memset(xf[i][HB:C, :, 0:HB], 0.0)
            last = V.memset(zero32, 0.0)
            then(last)
            V.tensor_copy(half[:, 0, 0:1], half[:, 0, 1:2]).then_inc(flag("exponents_ready"), 1)
            dve.wait_ge(flag("silu_c"), 1)
            V.tensor_copy(scb, bc(scT.unsqueeze(2), [128, KT, 128])).then_inc(flag("silu_c_spread"), 1)
            dve.wait_ge(flag("x_loaded"), 16)
            norm_rows(0, xs)
            dve.wait_ge(flag("mod_columns"), 1)
            mb = MODB[:, 0:8].rearrange("p (a b) -> p a b", a=4)
            mc = modc[:, :].rearrange("p (a b) -> p a b", a=4)
            V.tensor_copy(mc[:, 0:4:2, :], mb[:, 0:4:2, :])
            V.tensor_scalar(mc[:, 1:4:2, :], mb[:, 1:4:2, :], 1.0, None, ALU.add)
            dve.wait_ge(flag("gate_rows"), 1)
            g_all = gate[:, :, :].rearrange("p a b -> p (a b)")
            sign = lt[:, 0:4, :].rearrange("p a b -> p (a b)")
            mag = lt[:, 4:8, :].rearrange("p a b -> p (a b)")
            V.tensor_scalar(sign, GATEB[:, :], 0.0, 2.0, ALU.is_ge, ALU.mult)
            then(V.tensor_scalar(mag, GATEB[:, :], -1.0, None, ALU.mult))
            then(V.tensor_tensor(mag, GATEB[:, :], mag, ALU.max))
            then(V.tensor_scalar(mag, mag, 0.25, None, ALU.max))
            V.scalar_tensor_tensor(out=g_all, in0=sign, scalar=-1.0, in1=mag, op0=ALU.add,
                                   op1=ALU.mult).then_inc(flag("mods_stored"), 1)
            dve.wait_ge(flag("gates_projected"), 1)
            dve.wait_ge(flag("gates_loaded"), 32)
            ba = BAB[:, :].rearrange("p (c g k r) -> p c g k r", c=NC, g=NP, k=2)

            def by_head(t):
                return t.rearrange("p (c g r) -> p c g r", c=NC, g=NP)

            aa, neg, y, al, gg, bb = tmp[0], tmp[1], tmp[2], tmp[3], tmp[4], tmp[5]
            then(V.tensor_copy(by_head(aa), ba[:, :, :, 1, :]))
            then(V.tensor_tensor(aa.rearrange("p (c h) -> p c h", c=NC), aa.rearrange("p (c h) -> p c h", c=NC),
                                 bc(dtb.unsqueeze(1), [128, NC, NH]), ALU.add))
            then(V.tensor_scalar(neg, aa, -1.0, None, ALU.mult))
            then(V.tensor_tensor(neg, aa, neg, ALU.min))
            then(V.tensor_scalar(neg, neg, 1.0, None, ALU.mult))
            V.tensor_copy(gg, neg).then_inc(flag("neg_abs_ready"), 1)
            V.tensor_copy(by_head(bb), ba[:, :, :, 0, :]).then_inc(flag("b_copied"), 1)
            dve.wait_ge(flag("exp_ready"), 3)
            den, s2 = tmp[1], tmp[4]
            then(V.tensor_scalar(den, y, 2.0, None, ALU.add))
            then(V.reciprocal(den, den))
            then(V.tensor_tensor(y, y, den, ALU.mult))
            then(V.tensor_tensor(s2, y, y, ALU.mult))
            then(V.tensor_scalar(den, s2, 1.0 / 19, None, ALU.mult))
            for k in range(8, 0, -1):
                then(V.scalar_tensor_tensor(out=den, in0=den, scalar=1.0 / (2 * k + 1), in1=s2, op0=ALU.add,
                                            op1=ALU.mult))
            then(V.scalar_tensor_tensor(out=den, in0=den, scalar=1.0, in1=y, op0=ALU.add, op1=ALU.mult))
            then(V.tensor_scalar(aa, aa, 0.0, None, ALU.max))
            then(V.scalar_tensor_tensor(out=aa, in0=den, scalar=2.0, in1=aa, op0=ALU.mult, op1=ALU.add))
            V.tensor_tensor(gg.rearrange("p (c h) -> p c h", c=NC), aa.rearrange("p (c h) -> p c h", c=NC),
                            bc(tmp[6][:, 0:NH].unsqueeze(1), [128, NC, NH]), ALU.mult).then_inc(flag("g_ready"), 1)
            then(V.tensor_scalar(bb, tmp[7], 1.0, None, ALU.add))
            then(V.reciprocal(bb, bb))

            def table(kind):
                return tab[:, :, kind, :, :]

            def heads_first(t):
                return t.rearrange("p (c g r) -> p g r c", c=NC, g=NP)

            for r in range(2):
                last = V.tensor_copy(table(2)[:, :, r, :], heads_first(bb)[:, :, r, :])
            last.then_inc(flag("beta_stored"), 1)
            dve.wait_ge(flag("alpha_turned"), 1)
            for q in range(2):
                last = V.tensor_copy(alT[:, 4 * q:4 * q + 4, :].rearrange("p a b -> p (a b)"), bank[4 + q][0:NH, :])
            last.then_inc(flag("decays_ready"), 1)
            dve.wait_ge(flag("decays_ready"), 1)
            for c in range(NC):
                last = V.tensor_tensor_scan(eT[:, c, :], alT[:, c, :], zero32, 1.0, ALU.mult, ALU.add)
            last.then_inc(flag("products_ready"), 1)
            dve.wait_ge(flag("products_ready"), 1)
            V.tensor_copy(last32, eT[:, :, C - 1]).then_inc(flag("decays_ready"), 1)
            dve.wait_ge(flag("products_turned"), 1)
            eb = heads_first(bank[6][:, 0:NC * NH])
            for r in range(2):
                V.tensor_scalar(table(0)[:, :, r, :], eb[:, :, r, :], -1.0, None, ALU.mult)
            dve.wait_ge(flag("last_spread"), 16)
            V.tensor_copy(table(1), lastb.rearrange("p (g r c) -> p g r c", g=NP, r=2)).then_inc(
                flag("tables_ready"), 1)
            dve.wait_ge(flag("tables_ready"), 1)
            dve.wait_ge(flag("consts_loaded"), 16)

            def add_tap(n, par, t, j):
                if j == 0:
                    dve.wait_ge(x_copied.sem, x_copied.at(n, 2 * t + 2))
                else:
                    dve.wait_ge(tap.sem, tap.at(n, 2 * t + j))
                a = cacc[t % 2][:, :]
                V.scalar_tensor_tensor(out=a, in0=xpad[t % 2][:, j:j + T], scalar=cw[par][:, t, j:j + 1], in1=a,
                                       op0=ALU.mult, op1=ALU.add).then_inc((tap if j < 2 else conv_done).sem, 1)

            def begin(n, m, par):
                pass

            def finish(n, par):
                yield from ()

            def early(n, par):
                V.tensor_copy(sc[par][:, :, :, :].rearrange("p k r c -> p (k r c)"),
                              tab[:, bass.ds(n, 1), :, :, :].rearrange("p g k r c -> p (g k r c)")).then_inc(
                                  sc_ready.sem, 1)
                dve.wait_ge(al_in.sem, al_in.at(n, 16))
                for u in range(NU):
                    last = V.tensor_tensor_scan(lt[:, u, :], lt[:, u, :], ident, 0.0, ALU.mult, ALU.add)
                last.then_inc(lt_ready.sem, 1)
                yield
                for j in range(3):
                    add_tap(n, par, 0, j)
                yield
                yield
                for j in range(3):
                    add_tap(n, par, 1, j)
                dve.wait_ge(full.sem, full.at(n, F_NK + 1))
                V.tensor_scalar(nk[par][:, 0, :], ring(F_NK, par)[:, 0:NC], 1e-6, None, ALU.add).then_inc(
                    nk_ready.sem, 1)
                dve.wait_ge(nk_ready.sem, nk_ready.at(n, 1))
                V.reciprocal(nk[par][:, 2, :], nk[par][:, 0, :]).then_inc(s_ready.sem, 1)
                dve.wait_ge(s_ready.sem, s_ready.at(n, 1))
                dve.wait_ge(sc_ready.sem, sc_ready.at(n, 1))
                V.tensor_tensor(sj[:, :, :], sc[par][:, 2, :, :], bc(nk[par][:, 2:3, :], [128, 2, NC]),
                                ALU.mult).then_inc(s_ready.sem, 1)
                dve.wait_ge(s_ready.sem, s_ready.at(n, 2))
                dve.wait_ge(lt_ready.sem, lt_ready.at(n, 1))
                dve.wait_ge(km_done.sem, km_done.at(n, 0))
                V.tensor_tensor(wl[:, :, :], sj[:, :, :],
                                lt[:, :, C - 1].rearrange("p (h c) -> p h c", h=2), ALU.mult).then_inc(wl_ready.sem, 1)

            def front(n, m, par):
                for j in range(4):
                    dve.wait_ge(full.sem, full.at(n, F_KK + j + 1))
                    for i in range(4):
                        c, h = 2 * j + i // 2, i % 2
                        u = NC * h + c
                        last = V.scalar_tensor_tensor(
                            out=am[par][:, u, :, :],
                            in0=ring(F_KK + j, par)[:, 256 * (c % 2):256 * (c % 2 + 1)].rearrange(
                                "p (a b) -> p a b", a=2),
                            scalar=sj[:, h, c:c + 1], in1=bc(lt[:, u:u + 1, :], [128, 2, C]),
                            op0=ALU.mult, op1=ALU.mult)
                    last.then_inc(am_ready.sem, 1)
                    if j == 1:
                        dve.wait_ge(full.sem, full.at(n, F_NQ + 1))
                        V.tensor_scalar(nk[par][:, 1, :], ring(F_NQ, par)[:, 0:NC], 1e-6, float(C), ALU.add,
                                        ALU.mult).then_inc(nk_ready.sem, 1)
                    yield
                yield from invert(n, m, par)

            def invert(n, m, par):
                nb, row_i, prod = yc[:, :, 0:2 * BB], yc[:, :, 2 * BB:3 * BB], yc[:, :, 3 * BB:4 * BB]
                z, n16 = xc[:, :, 0:BB], xc[:, :, BB:2 * BB]
                V.tensor_copy(z, bc(cst[:, C_ID16:C_ID16 + BB].unsqueeze(1), [128, NU, BB])).then_inc(base.sem, 1)
                yield
                dve.wait_ge(nb_ready.sem, nb_ready.at(n, 2))
                V.tensor_tensor(nb, nb, bc(cst[:, C_BASE:C_BASE + 2 * BB].unsqueeze(1), [128, NU, 2 * BB]),
                                ALU.mult).then_inc(base.sem, 1)
                dve.wait_ge(base.sem, base.at(n, 2))
                V.tensor_tensor(n16, nb[:, :, 0:BB], nb[:, :, BB:2 * BB], ALU.add).then_inc(base.sem, 1)

                def done(k, op, g):
                    if k < 0:
                        return base.at(n, 3)
                    g = min(g, turns(k) - 1)
                    return base.at(n, 3 + 3 * sum(turns(j) for j in range(k)) + turns(k) * op + g + 1)

                for k, i in enumerate(range(BB - 1, 0, -1)):
                    w = BB - i
                    units = NU // turns(k)
                    groups = [slice(units * g, units * (g + 1)) for g in range(turns(k))]
                    for g, us in enumerate(groups):
                        dve.wait_ge(base.sem, done(k - 1, 2, g))
                        hold(dve, "dve_held")
                        V.stream_shuffle(row_i[:, us, 0:w], z[:, us, i:BB],
                                         [BB * (p // BB) + i for p in range(2 * BB)]).then_inc(base.sem, 1)
                    for g, us in enumerate(groups):
                        dve.wait_ge(base.sem, done(k, 0, g))
                        V.tensor_tensor(prod[:, us, 0:w], row_i[:, us, 0:w], bc(n16[:, us, i:i + 1], [128, units, w]),
                                        ALU.mult).then_inc(base.sem, 1)
                    for g, us in enumerate(groups):
                        dve.wait_ge(base.sem, done(k, 1, g))
                        V.tensor_tensor(z[:, us, i:BB], z[:, us, i:BB], prod[:, us, 0:w], ALU.add).then_inc(
                            base.sem, 1)
                    if k in BASE_YIELDS:
                        yield
                dve.wait_ge(base.sem, done(BB - 2, 2, 1))
                for g in range(2):
                    us = slice(UG * g, UG * (g + 1))
                    V.tensor_tensor(xt[:, us, :].rearrange("p u (b c) -> p u b c", c=BB),
                                    bc(z[:, us].unsqueeze(2), [128, UG, HB // BB, BB]),
                                    bc(cst[:, C_PLACE:C_PLACE + HB].rearrange("p (b c) -> p b c", c=BB).unsqueeze(1),
                                       [128, UG, HB // BB, BB]), ALU.mult).then_inc(inv.sem, 1)
                for g in range(2):
                    us = slice(UG * g, UG * (g + 1))
                    dve.wait_ge(inv.sem, inv.at(n, 2))
                    V.transpose(xc[:, us, :].rearrange("p a b -> p (a b)"),
                                xt[:, us, :].rearrange("p a b -> p (a b)")).then_inc(inv.sem, 1)
                yield
                for lvl in range(LEVELS):
                    f0 = F_LEVEL + 6 * lvl

                    def filled(k):
                        return ring(f0 + k, par)[:, :].rearrange("p (u c) -> p u c", u=UG)

                    for g in range(2):
                        dve.wait_ge(full.sem, full.at(n, f0 + g + 1))
                        V.tensor_tensor(yc[:, UG * g:UG * (g + 1), :], filled(g), mask(0, 128, lvl, UG),
                                        ALU.mult).then_inc(inv.sem, 1)
                    for t, j in (((2, 0), (2, 1)), ((3, 1),))[lvl]:
                        add_tap(n, par, t, j)
                    yield
                    for g in range(2):
                        us = slice(UG * g, UG * (g + 1))
                        dve.wait_ge(full.sem, full.at(n, f0 + 4 + 2 * g))
                        if lvl < LEVELS - 1:
                            last = V.tensor_tensor(xt[:, us, :], filled(2 + 2 * g), xt[:, us, :], ALU.add)
                        else:
                            for lo in (0, HB):
                                last = V.tensor_tensor(xf[par][lo:lo + HB, us, lo:lo + HB],
                                                       filled(2 + 2 * g)[lo:lo + HB], xt[lo:lo + HB, us, :], ALU.add)
                        last.then_inc(inv.sem, 1)
                        V.tensor_tensor(xc[:, us, :], filled(3 + 2 * g), xc[:, us, :], ALU.add).then_inc(inv.sem, 1)
                        if (lvl, g) in ((0, 0), (0, 1), (1, 0)):
                            add_tap(n, par, *((2, 2), (3, 0), (3, 2))[2 * lvl + g])
                        yield

            def add_out(n, c):
                dve.wait_ge(wo_full.sem, wo_full.at(n, c + 1))
                V.tensor_tensor(acc[:, c, :], OGB[:, 256:512], acc[:, c, :], ALU.add).then_inc(acc_done.sem, 1)

            def add_input(c):
                dve.wait_ge(flag("x_loaded"), 32)
                dve.wait_ge(acc_done.sem, acc_done.at(NP - 1, c + 1))
                then(V.tensor_tensor(acc[:, c, :], acc[:, c, :], gate[:, 0, :], ALU.mult))
                then(V.tensor_tensor(acc[:, c, :], acc[:, c, :], xs[:, c, :], ALU.add))
                then(V.bn_stats(stat[:, c, :], acc[:, c, :]))

            def scan(n, par, between, added=lambda c: None):
                for c in range(NC):
                    if c:
                        dve.wait_ge(ks_full.sem, ks_full.at(n, c))
                        if c == 1:
                            dve.wait_ge(vp_done.sem, vp_done.at(n, 4))
                        for h in range(2):
                            last = V.scalar_tensor_tensor(out=rr[:, h, :], in0=KSB[:, 128 * h:128 * (h + 1)],
                                                          scalar=sc[par][:, 0, h, c:c + 1], in1=vp[par][:, c, h, :],
                                                          op0=ALU.mult, op1=ALU.add)
                        last.then_inc(r_ready.sem, 1)
                    if c >= 3:
                        add_out(n, c - 3)
                        added(c - 3)
                    between()
                    between()
                    if c < NC - 1:
                        dve.wait_ge(ku_full.sem, ku_full.at(n, c + 1))
                        for h in range(2):
                            ku = KSB[:, 256 + 128 * h:256 + 128 * (h + 1)]
                            if c == 0:
                                last = V.tensor_copy(st[:, h, :], ku)
                            else:
                                last = V.scalar_tensor_tensor(out=st[:, h, :], in0=st[:, h, :],
                                                              scalar=sc[par][:, 1, h, c:c + 1], in1=ku,
                                                              op0=ALU.mult, op1=ALU.add)
                        last.then_inc(st_ready.sem, 1)
                    between()
                for c in range(NC - 3, NC):
                    add_out(n, c)
                    added(c)
                    if c < NC - 1:
                        between()
                        between()

            dve.wait_ge(flag("acc_cleared"), 1)
            pairs(dve, begin, early, front, finish, scan, early(0, 0),
                  lambda: scan(NP - 1, 1, lambda: None, add_input))

            norm_rows(1, acc)
            dve.wait_ge(flag("logits_full"), 1)
            lb = bank[4][:, 0:NC * NE].rearrange("p (c e) -> p c e", c=NC)
            then(V.tensor_reduce(row, lb, AX.X, ALU.max))
            V.tensor_tensor(lg, lb, bc(row.unsqueeze(2), [128, NC, NE]), ALU.subtract).then_inc(
                flag("logits_shifted"), 1)
            dve.wait_ge(flag("exp_logits"), 1)
            then(V.tensor_reduce(row, pv[:, :, 0:NE], AX.X, ALU.add))
            then(V.reciprocal(row, row))
            then(V.tensor_tensor(pv[:, :, 0:NE], pv[:, :, 0:NE], bc(row.unsqueeze(2), [128, NC, NE]), ALU.mult))
            for c in range(NC):
                last = V.max(top[:, c, :], pv[:, c, 0:NE])
            then(last)
            V.memset(pv[:, :, NE:WP], -1.0)
            then(V.memset(top[:, :, TOPK:8], -1.0))
            for c in range(NC):
                last = V.match_replace(rep[:, c, :], top[:, c, :], pv[:, c, :], -2.0)
            then(last)
            then(V.scalar_tensor_tensor(out=lg, in0=rep[:, :, 0:NE], scalar=-1.5, in1=pv[:, :, 0:NE], op0=ALU.is_lt,
                                        op1=ALU.mult))
            then(V.tensor_reduce(row, lg, AX.X, ALU.add))
            then(V.reciprocal(row, row))
            then(V.tensor_scalar(row, row, TOPK / (TOPK + 1.0), None, ALU.mult))
            V.tensor_tensor(cwt[:, 0:NE, :].rearrange("p e c -> p c e"), lg, bc(row.unsqueeze(2), [128, NC, NE]),
                            ALU.mult)
            V.memset(cwt[:, NE:NT, :], 1.0 / (TOPK + 1.0)).then_inc(flag("router_done"), 1)
            dve.wait_ge(flag("router_done"), 1)
            dve.wait_ge(flag("acc2_cleared"), 1)

            with dve.Fori(0, NT // 2) as i:
                for par in range(2):
                    e = i * 2 + par
                    V.tensor_copy(cwe[par], cwt[:, bass.ds(e, 1), :].rearrange("p a c -> p (a c)")).then_inc(
                        cwe_ready.sem, 1)
                    for q in range(2):
                        dve.wait_ge(mfull.sem, mfull.at(e, 2 * q + 2))
                        dve.wait_ge(sg_ready.sem, sg_ready.at(e, q + 1))
                        V.tensor_tensor(gT[:, 512 * q:512 * (q + 1)], bank[2 * q + 1][:, :], sg[q],
                                        ALU.mult).then_inc(g_ready.sem, 1)
                    dve.wait_ge(cwe_ready.sem, cwe_ready.at(e, 1))
                    dve.wait_ge(down_done.sem, down_done.at(e, 0))
                    for c in range(NC):
                        dve.wait_ge(mfull.sem, mfull.at(e, 4 + c // 2 + 1))
                        V.scalar_tensor_tensor(out=acc2[:, c, :], in0=bank[4 + c // 2][:, D * (c % 2):D * (c % 2 + 1)],
                                               scalar=cwe[par][:, c:c + 1], in1=acc2[:, c, :], op0=ALU.mult,
                                               op1=ALU.add).then_inc(down_done.sem, 1)
            dve.wait_ge(down_done.sem, down_done.at(NT, 0))
            for c in range(DVE_OUT):
                V.tensor_tensor(acc2[:, c, :], acc2[:, c, :], gate[:, 1, :], ALU.mult).then_inc(flag("dve_gated"), 1)
            for c in range(DVE_OUT):
                dve.wait_ge(flag("dve_gated"), c + 1)
                V.tensor_tensor(fin[:, c, :], acc2[:, c, :], acc[:, c, :], ALU.add).then_inc(flag("out_ready"), 1)

        @block.gpsimd
        def _(pool):
            P = nc.gpsimd
            for r in rounds:
                pool.sem_inc(r.sem, 1)
            P.memset(acc[:, :, :], 0.0).then_inc(flag("acc_cleared"), 1)

            def rstds(part):
                pool.wait_ge(flag(f"variances{part}"), 1)
                link(pool, "pool_step", P.tensor_scalar(rstd, mv[:, :, 1], 1e-5, None, ALU.add))
                P.tensor_tensor(rstd, rstd, nhalf, ALU.pow).then_inc(flag(f"rstd{part}"), 1)

            pool.wait_ge(flag("exponents_ready"), 1)
            rstds(0)
            pool.wait_ge(flag("tables_ready"), 1)
            pool.wait_ge(flag("nw_loaded"), 16)

            def begin(n, m, par):
                pass

            def early(n, par):
                yield from ()

            def finish(n, par):
                yield from ()

            def front(n, m, par):
                pool.wait_ge(wo_in[par].sem, wo_in[par].at(m, 16))
                hold(pool, "pool_held")
                P.tensor_scalar(wo[par][:, :, :], wo[par][:, :, :], nw[:, :], None, ALU.mult).then_inc(won_ready.sem, 1)
                yield
                pool.wait_ge(nk_ready.sem, nk_ready.at(n, 2))
                for w in range(2):
                    P.tensor_tensor(nk[par][:, 3 + w, :], nk[par][:, w, :], half[:, w, :],
                                    ALU.pow).then_inc(rs_ready.sem, 1)

            def scan(n, par, between):
                pool.wait_ge(z_ready.sem, z_ready.at(n, 4))
                pool.wait_ge(rs_ready.sem, rs_ready.at(n, 2))
                between()
                for c in range(NC):
                    pool.wait_ge(pu_copied.sem, pu_copied.at(n, c + 1))
                    if c:
                        pool.wait_ge(qse_ready.sem, qse_ready.at(n, c))
                        P.tensor_tensor(o1[c % 2][:, :, :], o1[c % 2][:, :, :], qse[:, :, :],
                                        ALU.subtract).then_inc(o1_ready.sem, 1)
                        pool.wait_ge(o1_ready.sem, o1_ready.at(n, c))
                    pool.wait_ge(og_full.sem, og_full.at(n, max(c - 1, 0)))
                    P.tensor_tensor(o2[c % 2][:, :, :], o1[c % 2][:, :, :],
                                    sz[par][:, c, :].rearrange("p (a b) -> p a b", a=2), ALU.mult).then_inc(
                                        o2_ready.sem, 1)
                    if c == 0:
                        between()
                    sq, t1, t2, t3 = (ss[:, c % 2, k, :] for k in range(4))
                    pool.wait_ge(ss_ready.sem, ss_ready.at(n, 2 * c + 2))
                    hold(pool, "pool_held")
                    P.tensor_scalar(t1, sq, 1.0 / C, 1e-6, ALU.mult, ALU.add).then_inc(f_step.sem, 1)
                    pool.wait_ge(f_step.sem, f_step.at(n, 3 * c + 1))
                    P.tensor_tensor(t2, t1, half[:, 1, 0:2], ALU.pow).then_inc(f_step.sem, 1)
                    pool.wait_ge(f_step.sem, f_step.at(n, 3 * c + 2))
                    hold(pool, "pool_held")
                    P.tensor_scalar(t3, t2, nk[par][:, 4, c:c + 1], None, ALU.mult).then_inc(f_step.sem, 1)
                    pool.wait_ge(f_step.sem, f_step.at(n, 3 * c + 3))
                    P.tensor_tensor(o2[c % 2][:, :, :], o2[c % 2][:, :, :], bc(t3.unsqueeze(2), [128, 2, C]),
                                    ALU.mult).then_inc(o3_ready.sem, 1)
                    if c == 0:
                        between()

            pairs(pool, begin, early, front, finish, scan, early(0, 0), lambda: scan(NP - 1, 1, lambda: None))
            pool.wait_ge(acc_done.sem, acc_done.at(NP, 0))
            P.memset(acc2, 0.0).then_inc(flag("acc2_cleared"), 1)
            rstds(1)
            pool.wait_ge(down_done.sem, down_done.at(NT, 0))
            for c in range(DVE_OUT, NC):
                P.tensor_tensor(acc2[:, c, :], acc2[:, c, :], gate[:, 1, :], ALU.mult).then_inc(
                    flag("pool_gated"), 1)
            for c in range(DVE_OUT, NC):
                pool.wait_ge(flag("pool_gated"), c - DVE_OUT + 1)
                P.tensor_tensor(fin[:, c, :], acc2[:, c, :], acc[:, c, :], ALU.add).then_inc(
                    flag("pool_out_ready"), 1)


_INS = ["L0_attn_hidden_states", "L0_attn_W_qkvz", "L0_attn_W_ba", "L0_attn_conv_w", "L0_attn_dt_bias",
        "L0_attn_A_log", "L0_attn_norm_weight", "L0_attn_W_out", "L0_ffn_w_router", "L0_ffn_we1", "L0_ffn_we3",
        "L0_ffn_we2", "L0_ffn_ws1", "L0_ffn_ws3", "L0_ffn_ws2", "L0_c", "L0_wmod"]


def constants():
    c = np.zeros((128, C_N), np.float32)
    c[:, C_ID:C_ID + 128] = np.eye(128)
    p, q = np.arange(128)[:, None] % HB, np.arange(HB)[None, :]
    for lvl in range(LEVELS):
        b = BB * 2 ** lvl
        c[:, C_MASK + HB * lvl:C_MASK + HB * (lvl + 1)] = -1.0 * ((p // (2 * b) == q // (2 * b)) & (p // b > q // b))
    c[:, C_ONE] = 1.0
    r16, r32, q32 = p % BB, p % (2 * BB), q[:, 0:2 * BB]
    c[:, C_ID16:C_ID16 + BB] = r16 == q[:, 0:BB]
    c[:, C_BASE:C_BASE + 2 * BB] = -1.0 * ((r32 // BB == q32 // BB) & (r32 < q32))
    c[:, C_PLACE:C_PLACE + HB] = p // BB == q // BB
    return c


def kernel(**inputs):
    import concourse.bacc as _bacc
    from concourse.bass_utils import run_bass_kernel_spmd as _run

    nc = _bacc.Bacc("TRN2", target_bir_lowering=False, num_devices=1)
    arrays, args = {}, []
    for name in _INS:
        a = np.ascontiguousarray(inputs[name])
        arrays[f"in_{name}"] = a
        args.append(nc.dram_tensor(f"in_{name}", a.shape, F32, kind="ExternalInput").ap())
    arrays["in_constants"] = constants()
    args.append(nc.dram_tensor("in_constants", (128, C_N), F32, kind="ExternalInput").ap())
    args.append(nc.dram_tensor("decays", (NH, NC, C), F32, kind="Internal").ap())
    args.append(nc.dram_tensor("last_decays", (NH, NC), F32, kind="Internal").ap())
    args.append(nc.dram_tensor("out_0", (1, T, D), F32, kind="ExternalOutput").ap())
    adaln_block(nc, *args)
    r = _run(nc, [arrays], core_ids=[0])
    return r.results[0]["out_0"]
```
